# Optimizing a Trainium2 kernel written in Bass

```python
import numpy as np
import jax
import jax.numpy as jnp

def _softmax(x, axis=-1):
    return jax.nn.softmax(x, axis=axis)
def _gelu(x):
    return jax.nn.gelu(x, approximate=True)
def _silu(x):
    return jax.nn.silu(x)
def _sigmoid(x):
    return jax.nn.sigmoid(x)
def _layernorm(x, axis=-1, eps=1e-5):
    m = jnp.mean(x, axis=axis, keepdims=True)
    v = jnp.var(x, axis=axis, keepdims=True)
    return (x - m) / jnp.sqrt(v + eps)
def _scatter_add(tgt, idx, src, axis=0):
    return tgt.at[idx].add(src)
def _segment_sum(src, seg, n):
    return jax.ops.segment_sum(src, seg, n)

kernel_name = 'mk_conv_preact_d1_conv_nhwc256_de0d3d'

def setup_inputs(seed: int = 0):
    np.random.seed(seed)
    _w = jnp.asarray
    def _rec_inputs():
        import jax
        import jax.numpy as jnp
        _gk = jax.random.key(seed)
        x = -0.0002928 + 1 * jax.random.normal(jax.random.fold_in(_gk, 1), (4, 64, 64, 256), jnp.float32)
        return x
    x = _rec_inputs()
    def _L0_conv_setup():
        import jax, jax.numpy as jnp
        import numpy as np
        DG = 8
        K = 3

        def conv1x1(x, w):
            return jnp.einsum('bhwc,cf->bhwf', x, w)

        def conv3x3_same(x, w, b):
            out = jax.lax.conv_general_dilated(x, w, (1, 1), 'SAME', dimension_numbers=('NHWC', 'HWIO', 'NHWC'))
            return out + b

        def dcn_v2(x, offset, mask, weight, bias):
            B, H, W, C = x.shape
            cpg = C // DG
            ky, kx = jnp.meshgrid(jnp.arange(K) - K // 2, jnp.arange(K) - K // 2, indexing='ij')
            ky = ky.reshape(-1).astype(x.dtype)
            kx = kx.reshape(-1).astype(x.dtype)
            iy = jnp.arange(H, dtype=x.dtype)[None, :, None, None, None]
            ix = jnp.arange(W, dtype=x.dtype)[None, None, :, None, None]
            yp = iy + ky + offset[..., 0]
            xp = ix + kx + offset[..., 1]
            xt = jnp.transpose(x.reshape(B, H, W, DG, cpg), (0, 3, 1, 2, 4)).reshape(B, DG, H * W, cpg)

            def gather(yi, xi):
                valid = ((yi >= 0) & (yi < H) & (xi >= 0) & (xi < W)).astype(x.dtype)
                yc = jnp.clip(yi, 0, H - 1)
                xc = jnp.clip(xi, 0, W - 1)
                flat = (yc * W + xc).astype(jnp.int32)
                idx = jnp.transpose(flat, (0, 3, 1, 2, 4)).reshape(B, DG, -1)
                v = jnp.take_along_axis(xt, idx[..., None], axis=2)
                v = v.reshape(B, DG, H, W, K * K, cpg)
                v = jnp.transpose(v, (0, 2, 3, 1, 4, 5))
                return v * valid[..., None]
            y0 = jnp.floor(yp)
            x0 = jnp.floor(xp)
            wy = (yp - y0)[..., None]
            wx = (xp - x0)[..., None]
            val = gather(y0, x0) * (1 - wy) * (1 - wx) + gather(y0, x0 + 1) * (1 - wy) * wx + gather(y0 + 1, x0) * wy * (1 - wx) + gather(y0 + 1, x0 + 1) * wy * wx
            val = val * mask[..., None]
            val = jnp.transpose(val, (0, 1, 2, 4, 3, 5)).reshape(B, H, W, K * K, C)
            out = jnp.einsum('bhwkc,kcf->bhwf', val, weight.reshape(K * K, C, -1))
            return out + bias
        key = jax.random.key(seed)
        ks = jax.random.split(key, 8)
        B, H, W, Cf, Cc, F = (4, 64, 64, 256, 256, 256)
        fine = jax.random.normal(ks[0], (B, H, W, Cf), jnp.float32)
        coarse = jax.random.normal(ks[1], (B, H // 2, W // 2, Cc), jnp.float32)
        attend_w = jax.random.normal(ks[2], (Cf, Cf), jnp.float32) * 0.05
        select_w = jax.random.normal(ks[3], (Cf, F), jnp.float32) * 0.05
        offset_w = jax.random.normal(ks[4], (F + Cc, 2 * F), jnp.float32) * 0.05
        om_w = jax.random.normal(ks[5], (3, 3, 2 * F, DG * 3 * K * K), jnp.float32) * 0.01
        om_b = jnp.zeros((DG * 3 * K * K,), jnp.float32)
        dcn_w = jax.random.normal(ks[6], (3, 3, Cc, F), jnp.float32) * 0.05
        dcn_b = jnp.zeros((F,), jnp.float32)
        return {'fine': fine, 'coarse': coarse, 'attend_w': attend_w, 'select_w': select_w, 'offset_w': offset_w, 'om_w': om_w, 'om_b': om_b, 'dcn_w': dcn_w, 'dcn_b': dcn_b}
    _L0_conv_all = _L0_conv_setup()
    _L0_conv_in = {k: v for k, v in _L0_conv_all.items() if k in ('coarse', 'attend_w', 'select_w', 'offset_w', 'om_w', 'om_b', 'dcn_w', 'dcn_b', )}
    del _L0_conv_all

    return {
        "x": x,
        "L0_conv_coarse": _L0_conv_in["coarse"],
        "L0_conv_attend_w": _L0_conv_in["attend_w"],
        "L0_conv_select_w": _L0_conv_in["select_w"],
        "L0_conv_offset_w": _L0_conv_in["offset_w"],
        "L0_conv_om_w": _L0_conv_in["om_w"],
        "L0_conv_om_b": _L0_conv_in["om_b"],
        "L0_conv_dcn_w": _L0_conv_in["dcn_w"],
        "L0_conv_dcn_b": _L0_conv_in["dcn_b"],
    }

def reference(x, L0_conv_coarse, L0_conv_attend_w, L0_conv_select_w, L0_conv_offset_w, L0_conv_om_w, L0_conv_om_b, L0_conv_dcn_w, L0_conv_dcn_b):
    import jax
    import jax.numpy as jnp
    def _L0_conv_ref(fine, coarse, attend_w, select_w, offset_w, om_w, om_b, dcn_w, dcn_b):
        import jax, jax.numpy as jnp
        import numpy as np
        DG = 8
        K = 3

        def conv1x1(x, w):
            return jnp.einsum('bhwc,cf->bhwf', x, w)

        def conv3x3_same(x, w, b):
            out = jax.lax.conv_general_dilated(x, w, (1, 1), 'SAME', dimension_numbers=('NHWC', 'HWIO', 'NHWC'))
            return out + b

        def dcn_v2(x, offset, mask, weight, bias):
            B, H, W, C = x.shape
            cpg = C // DG
            ky, kx = jnp.meshgrid(jnp.arange(K) - K // 2, jnp.arange(K) - K // 2, indexing='ij')
            ky = ky.reshape(-1).astype(x.dtype)
            kx = kx.reshape(-1).astype(x.dtype)
            iy = jnp.arange(H, dtype=x.dtype)[None, :, None, None, None]
            ix = jnp.arange(W, dtype=x.dtype)[None, None, :, None, None]
            yp = iy + ky + offset[..., 0]
            xp = ix + kx + offset[..., 1]
            xt = jnp.transpose(x.reshape(B, H, W, DG, cpg), (0, 3, 1, 2, 4)).reshape(B, DG, H * W, cpg)

            def gather(yi, xi):
                valid = ((yi >= 0) & (yi < H) & (xi >= 0) & (xi < W)).astype(x.dtype)
                yc = jnp.clip(yi, 0, H - 1)
                xc = jnp.clip(xi, 0, W - 1)
                flat = (yc * W + xc).astype(jnp.int32)
                idx = jnp.transpose(flat, (0, 3, 1, 2, 4)).reshape(B, DG, -1)
                v = jnp.take_along_axis(xt, idx[..., None], axis=2)
                v = v.reshape(B, DG, H, W, K * K, cpg)
                v = jnp.transpose(v, (0, 2, 3, 1, 4, 5))
                return v * valid[..., None]
            y0 = jnp.floor(yp)
            x0 = jnp.floor(xp)
            wy = (yp - y0)[..., None]
            wx = (xp - x0)[..., None]
            val = gather(y0, x0) * (1 - wy) * (1 - wx) + gather(y0, x0 + 1) * (1 - wy) * wx + gather(y0 + 1, x0) * wy * (1 - wx) + gather(y0 + 1, x0 + 1) * wy * wx
            val = val * mask[..., None]
            val = jnp.transpose(val, (0, 1, 2, 4, 3, 5)).reshape(B, H, W, K * K, C)
            out = jnp.einsum('bhwkc,kcf->bhwf', val, weight.reshape(K * K, C, -1))
            return out + bias
        B, H, W, Cf = fine.shape
        Cc = coarse.shape[-1]
        coarse_up = jax.image.resize(coarse, (B, H, W, Cc), 'bilinear')
        attn = jax.nn.sigmoid(conv1x1(jnp.mean(fine, axis=(1, 2), keepdims=True), attend_w))
        fine_cal = conv1x1(fine * (attn + 1.0), select_w)
        align = conv1x1(jnp.concatenate([fine_cal, coarse_up * 2.0], axis=-1), offset_w)
        om = conv3x3_same(align, om_w, om_b)
        n_off = DG * 2 * K * K
        off = om[..., :n_off].reshape(B, H, W, DG, K * K, 2)
        mask = jax.nn.sigmoid(om[..., n_off:]).reshape(B, H, W, DG, K * K)
        aligned = dcn_v2(coarse_up, off, mask, dcn_w, dcn_b)
        return jax.nn.relu(aligned) + fine_cal

    def _gn(v, G=32, eps=1e-5):
        B_, H_, W_, C_ = v.shape
        g = v.reshape(B_, H_, W_, G, C_ // G)
        m = jnp.mean(g, axis=(1, 2, 4), keepdims=True)
        s = jnp.var(g, axis=(1, 2, 4), keepdims=True)
        return ((g - m) / jnp.sqrt(s + eps)).reshape(v.shape)

    def _ln_c(v, eps=1e-6):
        m = jnp.mean(v, axis=-1, keepdims=True)
        s = jnp.var(v, axis=-1, keepdims=True)
        return (v - m) / jnp.sqrt(s + eps)

    def _ln_t(v, eps=1e-5):
        m = jnp.mean(v, axis=-1, keepdims=True)
        s = jnp.var(v, axis=-1, keepdims=True)
        return (v - m) / jnp.sqrt(s + eps)

    def _to_tokens(v):
        B_, H_, W_, C_ = v.shape
        return v.reshape(B_, H_ * W_, C_)
    def _from_tokens(t, like):
        return t.reshape(like.shape)

    x = x + _L0_conv_ref(_gn(x), L0_conv_coarse, L0_conv_attend_w, L0_conv_select_w, L0_conv_offset_w, L0_conv_om_w, L0_conv_om_b, L0_conv_dcn_w, L0_conv_dcn_b)
    return x


_drawn_inputs = setup_inputs


def setup_inputs(seed=0):
    import zlib

    import numpy as np

    out = dict(_drawn_inputs(seed))
    spreads = {'L0_conv_om_b': (0.0, 0.1), 'L0_conv_dcn_b': (0.0, 0.1)}
    factors = {'L0_conv_attend_w': 36.693}
    for name, (base, spread) in spreads.items():
        noise = np.random.default_rng([zlib.crc32(name.encode()), seed]).standard_normal(out[name].shape)
        drawn = base * np.exp(spread * noise) if base else spread * noise
        out[name] = jnp.asarray(drawn.astype(out[name].dtype))
    for name, factor in factors.items():
        out[name] = (out[name] * factor).astype(out[name].dtype)
    return out
```

```python
import concourse.bass as bass
from concourse import mybir
from contextlib import ExitStack

B, H, W, C = 4, 64, 64, 256
HC = H // 2
NG, NK = 8, 9
GK = NG * NK
NOM = 3 * GK
OMC = NOM // 2
CH = C // 128
HP = H + 2
CP = HC + 2
WIN = 10
WQ = WIN * WIN
LIMIT = 6.0
PADLO = 4
NWIN = 4
PADC = 43
SB = 8
ST = H * B // 4
BLK = 8
GN_EPS = 1e-5

f32 = mybir.dt.float32
i32 = mybir.dt.int32
ACT = mybir.ActivationFunctionType
ALU = mybir.AluOpType
AX = mybir.AxisListType


NCOORD = ST * NK + ST * WIN + 2 * NK + 2 * WIN + NWIN * WIN
NT = 9
UNITS = 4
GH = NG // 2


def merge_weights(nc, om_w, offset_w, ident_d, wm):
    NT = 4
    with ExitStack() as ctx:
        sb = lambda name, shape: ctx.enter_context(nc.sbuf_tensor(name, shape, f32))
        sem = lambda name: ctx.enter_context(nc.semaphore(name))
        ident = sb("ident0", [128, 128])
        ow = sb("ow", [128, NT, 512])
        owT = sb("owT", [128, NT, NT, 128])
        omw = sb("omw", [128, NK, NT, NOM])
        tps = [ctx.enter_context(nc.psum_tensor(f"tps{i}", [128, 512], f32)) for i in range(2)]
        mps = [ctx.enter_context(nc.psum_tensor(f"mps{i}", [128, NOM], f32)) for i in range(2)]
        w_loaded, omw_loaded = sem("w_loaded"), sem("omw_loaded")
        turned, turned_out = sem("turned"), sem("turned_out")
        merged, merged_out = sem("merged"), sem("merged_out")
        block = ctx.enter_context(nc.Block())

        @block.sync
        def _(sp):
            sp.dma_start(ident[:], ident_d).then_inc(w_loaded, 16)
            sp.dma_start(ow[:], offset_w.rearrange("(i p) m -> p i m", p=128)).then_inc(w_loaded, 16)
            sp.dma_start(omw[:], om_w.rearrange("u v (m p) o -> p (u v) m o", p=128)).then_inc(omw_loaded, 16)

        @block.tensor
        def _(pe):
            pe.wait_ge(w_loaded, 32)
            for m in range(NT):
                if m >= 2:
                    pe.wait_ge(turned_out, m - 1)
                for i in range(NT):
                    last = nc.tensor.transpose(tps[m % 2][:, 128 * i:128 * i + 128],
                                               ow[:, i, 128 * m:128 * m + 128], ident[:])
                last.then_inc(turned, 1)
            pe.wait_ge(turned_out, NT)
            pe.wait_ge(omw_loaded, 16)
            for n in range(NK * NT):
                tap, i = n // NT, n % NT
                if n >= 2:
                    pe.wait_ge(merged_out, 2 * (n - 1))
                for m in range(NT):
                    last = nc.tensor.matmul(mps[n % 2][:], owT[:, m, i, :], omw[:, tap, m, :],
                                            start=(m == 0), stop=(m == NT - 1))
                last.then_inc(merged, 1)

        @block.vector
        def _(dve):
            for m in range(NT):
                dve.wait_ge(turned, m + 1)
                nc.vector.tensor_copy(owT[:, m, :, :], tps[m % 2][:].rearrange("p (i c) -> p i c", i=NT)
                                      ).then_inc(turned_out, 1)
            for n in range(NK * NT):
                tap, i = n // NT, n % NT
                dve.wait_ge(merged, n + 1)
                nc.vector.tensor_scalar(
                    wm[:, i, tap, 0:2 * GK].rearrange("p (t q) -> p t q", t=2),
                    mps[n % 2][:, 0:2 * GK].rearrange("p (q t) -> p t q", t=2),
                    1.0 if i < 2 else 2.0, None, ALU.mult).then_inc(merged_out, 1)
                nc.vector.tensor_scalar(wm[:, i, tap, 2 * GK:NOM], mps[n % 2][:, 2 * GK:NOM],
                                        1.0 if i < 2 else 2.0, None, ALU.mult).then_inc(merged_out, 1)


def pad_coarse(nc, coarse, cpad):
    hi = PADLO + HC
    nlo, nhi = PADLO, PADC - hi
    with nc.semaphore("rows_padded") as rows_padded, nc.semaphore("padded") as padded, nc.Block() as block:
        @block.sync
        def _(sp):
            for b in range(B):
                sp.dma_start(cpad[b, PADLO:hi, PADLO:hi, :], coarse[b]).then_inc(rows_padded, 16)
                sp.dma_start(cpad[b, 0:PADLO, PADLO:hi, :], coarse[b, 0:1].broadcast_to([nlo, HC, C])).then_inc(rows_padded, 16)
                sp.dma_start(cpad[b, hi:PADC, PADLO:hi, :], coarse[b, HC - 1:HC].broadcast_to([nhi, HC, C])).then_inc(rows_padded, 16)
            sp.wait_ge(rows_padded, 16 * 3 * B)
            for b in range(B):
                for col in range(PADLO):
                    sp.dma_start(cpad[b, :, col, :], cpad[b, :, PADLO, :]).then_inc(padded, 16)
                for col in range(hi, PADC):
                    sp.dma_start(cpad[b, :, col, :], cpad[b, :, hi - 1, :]).then_inc(padded, 16)
            sp.wait_ge(padded, 16 * B * (PADLO + nhi))


def offsets_and_calibration(nc, x, coarse, attend_w, select_w, om_b, ident_d, gmean_d, wm, om_d, r_d, flag):
    NX, NC = 8, 2
    with ExitStack() as ctx:
        sb = lambda name, shape, dt=f32: ctx.enter_context(nc.sbuf_tensor(name, shape, dt))
        sem = lambda name: ctx.enter_context(nc.semaphore(name))
        ident = sb("ident1", [128, 128])
        gmean = sb("gmean", [128, 128])
        att = sb("att", [128, CH, C])
        sel = sb("sel", [128, CH, C])
        omb = sb("omb", [OMC, 2])
        chunk = [sb(f"chunk{i}", [128, 4, C]) for i in range(2)]
        xT = sb("xT", [128, CH, H * W])
        cT = sb("cT", [128, CH, CP, CP])
        ux = sb("ux", [128, CH, CP, W])
        fine = sb("fine", [128, CH, HP, HP])
        up = sb("up", [128, CH, HP, HP])
        xn = [sb(f"xn{i}", [128, CH, 512]) for i in range(2)]
        r = [sb(f"r{i}", [128, CH, 512]) for i in range(2)]
        omT = [sb(f"omT{i}", [OMC, 2, 2, 256]) for i in range(2)]
        oms = [sb(f"oms{i}", [128, 4, NOM]) for i in range(2)]
        st = sb("st", [128, CH, NX, 6])
        mv = sb("mv", [128, CH, 2])
        dev, dev2, var, rstd, mfine, gate, scale, shift = (
            sb(n, [128, CH]) for n in ("dev", "dev2", "var", "rstd", "mfine", "gate", "scale", "shift"))
        sd = sb("sd", [128, CH])
        ext = sb("ext", [128, 2 * B * SB])
        far = sb("far", [128, 2])
        row = sb("row", [2, 128])
        top = sb("top", [2, 1])
        topr = sb("topr", [1, 2])
        worst = sb("worst", [1, 1])
        ps = [ctx.enter_context(nc.psum_tensor(f"ps{i}", [128, 512], f32)) for i in range(8)]
        conv, turn, cal = ps[0:4], ps[4:6], ps[6:8]
        small = conv[3]
        names = ("consts", "edges", "conv_done", "conv_out", "turn_done", "turn_out", "xn_done", "cal_done",
                 "cal_padded", "r_ready", "stats", "dchain", "gm_done", "gv_done", "sd_done", "att_done",
                 "gate_done", "affine", "chunk_stats", "cT_edged", "up_done", "flag_T", "flag_T2", "flagged", "near_x", "near_up", "ext_done")
        s = {n: sem(n) for n in names}
        loaded = [sem("loaded0"), sem("loaded1")]
        r_stored = [sem("r_stored0"), sem("r_stored1")]
        om_stored = [sem("om_stored0"), sem("om_stored1")]
        block = ctx.enter_context(nc.Block())
        NTURN = 2 * (NX + NC) + 2 * SB
        x_v = x.rearrange("b h w c -> (b h w) c").rearrange("(n t p) c -> n p t c", p=128, t=4)
        c_v = coarse.rearrange("b h w c -> (b h w) c").rearrange("(n t p) c -> n p t c", p=128, t=4)

        @block.sync
        def _(sp):
            sp.dma_start(ident[:], ident_d).then_inc(s["consts"], 16)
            sp.dma_start(gmean[:], gmean_d).then_inc(s["consts"], 16)
            sp.dma_start(att[:], attend_w.rearrange("(h p) f -> p h f", p=128)).then_inc(s["consts"], 16)
            sp.dma_start(sel[:], select_w.rearrange("(h p) f -> p h f", p=128)).then_inc(s["consts"], 16)
            yx = om_b[0:2 * GK].rearrange("(q t) -> q t", t=2)
            with nc.allow_non_contiguous_dma(reason="216 bias values, once"):
                sp.dma_start(omb[0:GK, 0:1], yx[:, 0:1]).then_inc(s["consts"], 16)
                sp.dma_start(omb[GK:OMC, 0:1], yx[0:OMC - GK, 1:2]).then_inc(s["consts"], 16)
                sp.dma_start(omb[0:GK - (OMC - GK), 1:2], yx[OMC - GK:GK, 1:2]).then_inc(s["consts"], 16)
                sp.dma_start(omb[GK - (OMC - GK):OMC, 1:2],
                             om_b[2 * GK:NOM].rearrange("(q t) -> q t", t=1)).then_inc(s["consts"], 16)

            def load(b, n):
                src = x_v[bass.ds(b * NX + n, 1)] if n < NX else c_v[bass.ds(b * NC + n - NX, 1)]
                sp.dma_start(chunk[n % 2][:], src.rearrange("o p t c -> (o p) t c")).then_inc(loaded[n % 2], 16)

            def load_after(b, n):
                sp.wait_ge(s["turn_done"], b * NTURN + 2 * (n - 1))
                load(*((b, n) if n < NX + NC else (b + 1, n - NX - NC)))

            load(0, 0)
            load(0, 1)
            with sp.Fori(0, B - 1) as b:
                for n in range(2, NX + NC + 2):
                    load_after(b, n)
            for n in range(2, NX + NC):
                load_after(B - 1, n)

        @block.tensor
        def _(pe):
            pe.wait_ge(s["consts"], 16 * 8)
            with pe.Fori(0, B) as b:
                for n in range(NX + NC):
                    pe.wait_ge(loaded[n % 2], b * (16 * (NX + NC) // 2) + 16 * (n // 2 + 1))
                    for h in range(CH):
                        u = 2 * n + h
                        if u >= 2:
                            pe.wait_ge(s["turn_out"], b * NTURN + u - 1)
                        for t in range(4):
                            last = nc.tensor.transpose(turn[h][:, 128 * t:128 * t + 128],
                                                       chunk[n % 2][:, t, 128 * h:128 * h + 128], ident[:])
                        last.then_inc(s["turn_done"], 1)
                pe.wait_ge(s["stats"], b + 1)
                nc.tensor.matmul(small[:, 0:2], gmean[:], mv[:, :, 0], start=True, stop=True).then_inc(s["gm_done"], 1)
                pe.wait_ge(s["dchain"], b * 9 + 3)
                nc.tensor.matmul(small[:, 2:4], gmean[:], var[:], start=True, stop=True).then_inc(s["gv_done"], 1)
                pe.wait_ge(s["dchain"], b * 9 + 6)
                for fo in range(CH):
                    for h in range(CH):
                        last = nc.tensor.matmul(small[:, 4 + fo:5 + fo], att[:, h, 128 * fo:128 * fo + 128],
                                                mfine[:, h:h + 1], start=(h == 0), stop=(h == CH - 1))
                last.then_inc(s["att_done"], 1)
                for n in range(NX):
                    pe.wait_ge(s["xn_done"], b * 2 * NX + 2 * (n + 1))
                    for fo in range(CH):
                        if n:
                            pe.wait_ge(s["cal_padded"], b * 2 * NX + 2 * (n - 1) + fo + 1)
                        for h in range(CH):
                            last = nc.tensor.matmul(cal[fo][:], sel[:, h, 128 * fo:128 * fo + 128], xn[n % 2][:, h, :],
                                                    start=(h == 0), stop=(h == CH - 1))
                        last.then_inc(s["cal_done"], 1)

                def turn_offsets(n):
                    pe.wait_ge(s["conv_out"], b * 2 * SB + 2 * (n + 1))
                    for hy in range(2):
                        u = 2 * (NX + NC) + 2 * n + hy
                        pe.wait_ge(s["turn_out"], b * NTURN + u - 1)
                        for hx in range(2):
                            for o in range(2):
                                last = nc.tensor.transpose(
                                    turn[hy][:, NOM * hx + OMC * o:NOM * hx + OMC * (o + 1)],
                                    omT[n % 2][:, o, hy, 128 * hx:128 * hx + 128], ident[0:OMC, 0:OMC])
                        last.then_inc(s["turn_done"], 1)

                pe.wait_ge(s["up_done"], 4 * (b + 1))
                pe.wait_ge(s["cal_padded"], 2 * NX * (b + 1))
                for n in range(SB):
                    for o in range(2):
                        use = 2 * n + o
                        if use >= 4:
                            pe.wait_ge(s["conv_out"], b * 2 * SB + use - 3)
                        k = 0
                        for i, src in enumerate((fine, up)):
                            for h in range(CH):
                                for tap in range(NK):
                                    dy, dx = tap // 3, tap % 3
                                    last = nc.tensor.matmul(
                                        conv[use % 4][0:OMC, :], wm[:, 2 * i + h, tap, OMC * o:OMC * (o + 1)],
                                        src[:, h, 8 * n + dy:8 * n + dy + 8, dx:dx + W],
                                        start=(k == 0), stop=(k == 4 * NK - 1))
                                    k += 1
                        last.then_inc(s["conv_done"], 1)
                    if n >= 1:
                        turn_offsets(n - 1)
                turn_offsets(SB - 1)
                pe.wait_ge(s["turn_out"], (b + 1) * NTURN)
            pe.wait_ge(s["flagged"], 3)
            nc.tensor.transpose(turn[0][0:2, 0:128], far[:], ident[:]).then_inc(s["flag_T"], 1)
            pe.wait_ge(s["flagged"], 5)
            nc.tensor.transpose(turn[1][0:1, 0:2], top[:], ident[0:2, 0:2]).then_inc(s["flag_T2"], 1)

        @block.scalar
        def _(act):
            with act.Fori(0, B) as b:
                act.wait_ge(s["dchain"], b * 9 + 4)
                nc.scalar.activation(sd[:], var[:], ACT.Sqrt).then_inc(s["sd_done"], 1)
                act.wait_ge(s["att_done"], b + 1)
                nc.scalar.activation(gate[:], small[:, 4:6], ACT.Sigmoid).then_inc(s["gate_done"], 1)
                act.wait_ge(s["affine"], 2 * (b + 1))

                def normalise(n):
                    if n >= 2:
                        act.wait_ge(s["cal_done"], b * 2 * NX + 2 * (n - 1))
                    for h in range(CH):
                        nc.scalar.activation(xn[n % 2][:, h, :], xT[:, h, 512 * n:512 * n + 512], ACT.Identity,
                                             bias=shift[:, h:h + 1], scale=scale[:, h:h + 1]).then_inc(s["xn_done"], 1)
                act.wait_ge(s["edges"], 2)
                normalise(0)
                for n in range(NX):
                    if n + 1 < NX:
                        normalise(n + 1)
                    for fo in range(CH):
                        act.wait_ge(s["cal_done"], b * 2 * NX + 2 * n + fo + 1)
                        nc.scalar.activation(fine[:, fo, 8 * n + 1:8 * n + 9, 1:W + 1],
                                             cal[fo][:].rearrange("p (y x) -> p y x", y=8), ACT.Identity
                                             ).then_inc(s["cal_padded"], 1)
                for n in range(SB):
                    for o in range(2):
                        act.wait_ge(s["conv_done"], b * 2 * SB + 2 * n + o + 1)
                        if n >= 2:
                            act.wait_ge(s["turn_done"], b * NTURN + 2 * (NX + NC) + 2 * (n - 1))
                        for hy in range(2):
                            last = nc.scalar.activation(
                                omT[n % 2][:, o, hy, :].rearrange("p (j r c) -> p r j c", r=4, c=4),
                                conv[(2 * n + o) % 4][0:OMC, 256 * hy:256 * hy + 256].rearrange(
                                    "p (r j c) -> p r j c", r=4, c=4), ACT.Identity, bias=omb[:, o:o + 1])
                        last.then_inc(s["conv_out"], 1)

        @block.gpsimd
        def _(pool):
            nc.gpsimd.memset(fine[:], 0.0).then_inc(s["edges"], 1)
            nc.gpsimd.memset(up[:], 0.0).then_inc(s["edges"], 1)
            pool.wait_ge(s["edges"], 2)
            with pool.Fori(0, B) as b:
                for n in range(NX):
                    for h in range(CH):
                        pool.wait_ge(s["r_ready"], b * 2 * NX + 2 * n + h + 1)
                    pool.dma_start(r_d[bass.ds(b * NX + n, 1)].rearrange("o p h c -> (o p) h c"), r[n % 2][:]
                                   ).then_inc(r_stored[n % 2], 16)
                for n in range(SB):
                    pool.wait_ge(s["turn_out"], b * NTURN + 2 * (NX + NC) + 2 * (n + 1))
                    pool.dma_start(om_d[bass.ds((b * SB + n) * 2, 2)].rearrange("y p x o -> p y (x o)"),
                                   oms[n % 2][:].rearrange("p (y x) o -> p y (x o)", y=2)).then_inc(om_stored[n % 2], 16)
            for i in range(2):
                pool.wait_ge(r_stored[i], 16 * B * NX // 2)
                pool.wait_ge(om_stored[i], 16 * B * SB // 2)

        @block.vector
        def _(dve):
            with dve.Fori(0, B) as b:
                for n in range(NX + NC):
                    for h in range(CH):
                        dve.wait_ge(s["turn_done"], b * NTURN + 2 * n + h + 1)
                        if n < NX:
                            nc.vector.tensor_copy(xT[:, h, 512 * n:512 * n + 512], turn[h][:]).then_inc(s["turn_out"], 1)
                            dve.wait_ge(s["turn_out"], b * NTURN + 2 * n + h + 1)
                            nc.vector.bn_stats(st[:, h, n, :], xT[:, h, 512 * n:512 * n + 512]).then_inc(s["chunk_stats"], 1)
                        else:
                            y = (n - NX) * 16
                            if n == NX:
                                dve.wait_ge(s["chunk_stats"], 2 * NX * (b + 1))
                            nc.vector.tensor_copy(cT[:, h, 1 + y:17 + y, 1:HC + 1],
                                                  turn[h][:].rearrange("p (y x) -> p y x", y=16)).then_inc(s["turn_out"], 1)
                for h in range(CH):
                    last = nc.vector.bn_aggr(mv[:, h, :], st[:, h, :, :].rearrange("p n k -> p (n k)"))
                last.then_inc(s["stats"], 1)
                dve.wait_ge(s["stats"], b + 1)
                dve.wait_ge(s["gm_done"], b + 1)
                nc.vector.tensor_tensor(dev[:], mv[:, :, 0], small[:, 0:2], ALU.subtract).then_inc(s["dchain"], 1)
                dve.wait_ge(s["dchain"], b * 9 + 1)
                nc.vector.tensor_tensor(dev2[:], dev[:], dev[:], ALU.mult).then_inc(s["dchain"], 1)
                dve.wait_ge(s["dchain"], b * 9 + 2)
                nc.vector.tensor_tensor(var[:], dev2[:], mv[:, :, 1], ALU.add).then_inc(s["dchain"], 1)
                dve.wait_ge(s["gv_done"], b + 1)
                nc.vector.tensor_scalar(var[:], small[:, 2:4], GN_EPS, None, ALU.add).then_inc(s["dchain"], 1)
                dve.wait_ge(s["sd_done"], b + 1)
                nc.vector.reciprocal(rstd[:], sd[:]).then_inc(s["dchain"], 1)
                dve.wait_ge(s["dchain"], b * 9 + 5)
                nc.vector.tensor_tensor(mfine[:], dev[:], rstd[:], ALU.mult).then_inc(s["dchain"], 1)
                dve.wait_ge(s["gate_done"], b + 1)
                nc.vector.scalar_tensor_tensor(out=scale[:], in0=gate[:], scalar=1.0, in1=rstd[:],
                                               op0=ALU.add, op1=ALU.mult).then_inc(s["affine"], 1)
                nc.vector.tensor_scalar(dev2[:], small[:, 0:2], -1.0, None, ALU.mult).then_inc(s["dchain"], 1)
                dve.wait_ge(s["dchain"], b * 9 + 7)
                dve.wait_ge(s["affine"], 2 * b + 1)
                nc.vector.tensor_tensor(shift[:], dev2[:], scale[:], ALU.mult).then_inc(s["affine"], 1)
                for n in range(NX):
                    if n >= 2:
                        dve.wait_ge(r_stored[n % 2], b * 64 + 16 * (n // 2))
                    for fo in range(CH):
                        dve.wait_ge(s["cal_padded"], b * 2 * NX + 2 * n + fo + 1)
                        nc.vector.tensor_tensor(r[n % 2][:, fo, :].rearrange("p (y x) -> p y x", y=8),
                                                fine[:, fo, 8 * n + 1:8 * n + 9, 1:W + 1],
                                                xT[:, fo, 512 * n:512 * n + 512].rearrange("p (y x) -> p y x", y=8),
                                                ALU.add).then_inc(s["r_ready"], 1)
                    if n == 0:
                        nc.vector.tensor_copy(cT[:, :, 1:HC + 1, 0:1], cT[:, :, 1:HC + 1, 1:2]).then_inc(s["dchain"], 1)
                        nc.vector.tensor_copy(cT[:, :, 1:HC + 1, CP - 1:CP], cT[:, :, 1:HC + 1, CP - 2:CP - 1]
                                              ).then_inc(s["dchain"], 1)
                        dve.wait_ge(s["dchain"], b * 9 + 9)
                        nc.vector.tensor_copy(cT[:, :, 0:1, :], cT[:, :, 1:2, :]).then_inc(s["cT_edged"], 1)
                        nc.vector.tensor_copy(cT[:, :, CP - 1:CP, :], cT[:, :, CP - 2:CP - 1, :]).then_inc(s["cT_edged"], 1)
                        dve.wait_ge(s["cT_edged"], 2 * (b + 1))
                        for h in range(CH):
                            nc.vector.tensor_scalar(ux[:, h].rearrange("p y (x t) -> p y t x", t=2)[:, :, 0, :],
                                                    cT[:, h, :, 1:HC + 1], 0.75, None, ALU.mult).then_inc(s["near_x"], 1)
                            nc.vector.tensor_scalar(ux[:, h].rearrange("p y (x t) -> p y t x", t=2)[:, :, 1, :],
                                                    cT[:, h, :, 1:HC + 1], 0.75, None, ALU.mult).then_inc(s["near_x"], 1)
                        dve.wait_ge(s["near_x"], b * 8 + 4)
                        for h in range(CH):
                            for t in range(2):
                                v = ux[:, h].rearrange("p y (x t) -> p y t x", t=2)[:, :, t, :]
                                nc.vector.scalar_tensor_tensor(out=v, in0=cT[:, h, :, 2 * t:2 * t + HC], scalar=0.25,
                                                               in1=v, op0=ALU.mult, op1=ALU.add).then_inc(s["near_x"], 1)
                        dve.wait_ge(s["near_x"], b * 8 + 8)
                        dve.wait_ge(s["edges"], 2)
                        upv = up[:, :, 1:H + 1, 1:W + 1].rearrange("p h (y t) x -> p h t y x", t=2)
                        for h in range(CH):
                            for t in range(2):
                                nc.vector.tensor_scalar(upv[:, h, t], ux[:, h, 1:HC + 1, :], 0.75, None, ALU.mult
                                                        ).then_inc(s["near_up"], 1)
                        dve.wait_ge(s["near_up"], 4 * (b + 1))
                        for h in range(CH):
                            for t in range(2):
                                nc.vector.scalar_tensor_tensor(out=upv[:, h, t], in0=ux[:, h, 2 * t:2 * t + HC, :], scalar=0.25,
                                                               in1=upv[:, h, t], op0=ALU.mult, op1=ALU.add
                                                               ).then_inc(s["up_done"], 1)
                for n in range(SB):
                    if n >= 2:
                        dve.wait_ge(om_stored[n % 2], b * 64 + 16 * (n // 2))
                    for hy in range(2):
                        u = 2 * (NX + NC) + 2 * n + hy
                        dve.wait_ge(s["turn_done"], b * NTURN + u + 1)
                        nc.vector.tensor_copy(oms[n % 2][:, 2 * hy:2 * hy + 2, :],
                                              turn[hy][:, 0:2 * NOM].rearrange("p (x o) -> p x o", x=2)
                                              ).then_inc(s["turn_out"], 1)
                    dve.wait_ge(s["turn_out"], b * NTURN + 2 * (NX + NC) + 2 * (n + 1))
                    nc.vector.tensor_reduce(ext[:, bass.ds(b * SB + n, 1)], oms[n % 2][:, :, 0:2 * GK], axis=AX.XY, op=ALU.max
                                            ).then_inc(s["ext_done"], 1)
                    nc.vector.tensor_reduce(ext[:, bass.ds(b * SB + n + B * SB, 1)], oms[n % 2][:, :, 0:2 * GK], axis=AX.XY,
                                            op=ALU.min).then_inc(s["ext_done"], 1)
                dve.wait_ge(s["xn_done"], 2 * NX * (b + 1))
                for i in range(2):
                    dve.wait_ge(r_stored[i], 64 * (b + 1))
                    dve.wait_ge(om_stored[i], 64 * (b + 1))
            dve.wait_ge(s["ext_done"], 2 * B * SB)
            nc.vector.tensor_reduce(far[:, 0:1], ext[:, 0:B * SB], axis=AX.X, op=ALU.max).then_inc(s["flagged"], 1)
            nc.vector.tensor_reduce(far[:, 1:2], ext[:, B * SB:], axis=AX.X, op=ALU.min).then_inc(s["flagged"], 1)
            dve.wait_ge(s["flagged"], 2)
            nc.vector.tensor_scalar(far[:, 1:2], far[:, 1:2], -1.0, None, ALU.mult).then_inc(s["flagged"], 1)
            dve.wait_ge(s["flag_T"], 1)
            nc.vector.tensor_copy(row[:], turn[0][0:2, 0:128]).then_inc(s["flagged"], 1)
            dve.wait_ge(s["flagged"], 4)
            nc.vector.tensor_reduce(top[:], row[:], axis=AX.X, op=ALU.max).then_inc(s["flagged"], 1)
            dve.wait_ge(s["flag_T2"], 1)
            nc.vector.tensor_copy(topr[:], turn[1][0:1, 0:2]).then_inc(s["flagged"], 1)
            dve.wait_ge(s["flagged"], 6)
            nc.vector.tensor_reduce(worst[:], topr[:], axis=AX.X, op=ALU.max).then_inc(s["flagged"], 1)
            dve.wait_ge(s["flagged"], 7)
            nc.vector.tensor_scalar(flag[:], worst[:], LIMIT, None, ALU.is_gt).then_inc(s["flagged"], 1)


def sample_and_project(nc, cpad, om_d, r_d, dcn_w, dcn_b, ident_d, coords_d, flag, out):
    ctx = ExitStack()
    with ctx:
        sb = lambda name, shape, dt=f32: ctx.enter_context(nc.sbuf_tensor(name, shape, dt))
        sem = lambda name: ctx.enter_context(nc.semaphore(name))
        ident = sb("ident2", [128, 128])
        coords = sb("coords", [128, NCOORD])
        base_y = coords[:, 0:ST * NK].rearrange("p (s k) -> p s k", k=NK)
        o = ST * NK
        ctr_y = coords[:, o:o + ST * WIN].rearrange("p (s a) -> p s a", a=WIN)
        o += ST * WIN
        base_x = coords[:, o:o + 2 * NK].rearrange("p (x k) -> p x k", k=NK)
        o += 2 * NK
        ctr_x = coords[:, o:o + 2 * WIN].rearrange("p (x a) -> p x a", a=WIN)
        o += 2 * WIN
        ctr_all = coords[:, o:o + NWIN * WIN].rearrange("p (w a) -> p w a", a=WIN)
        wd = sb("wd", [128, CH, NK, C])
        bias = sb("bias", [128, CH])
        k34, k14 = sb("k34", [128, 1]), sb("k14", [128, 1])
        om = [sb(f"om{i}", [128, 2, NOM]) for i in range(2)]
        pos = [sb(f"pos{i}", [128, 2, 2, GK]) for i in range(2)]
        lo, hi = sb("lo", [128, 2, 2, GK]), sb("hi", [128, 2, 2, GK])
        mask = [sb(f"mask{i}", [128, 2, GK]) for i in range(2)]
        coef = [sb(f"coef{i}", [128, 2, GK]) for i in range(2)]
        tap = [sb(f"tap{i}", [128, 2, GK, WIN]) for i in range(2)]
        wt = [sb(f"wt{i}", [128, GH * NK, WQ]) for i in range(2)]
        wtT = [sb(f"wtT{i}", [WQ, GH * NK, 128]) for i in range(2)]
        win = [sb(f"win{i}", [WQ, BLK, C]) for i in range(2)]
        val = [sb(f"val{i}", [128, CH, NK, 256]) for i in range(2)]
        res = [sb(f"res{i}", [128, CH, 256]) for i in range(2)]
        rt = [sb(f"rt{i}", [128, CH, 256]) for i in range(2)]
        ot = [sb(f"ot{i}", [128, 512]) for i in range(2)]
        bank = lambda name: ctx.enter_context(nc.psum_tensor(name, [128, 512], f32))
        tb = [bank(f"tb{i}") for i in range(3)]
        vb = [bank(f"vb{i}") for i in range(2)]
        eb = [bank(f"eb{i}") for i in range(2)]
        ob = bank("ob")

        def tables():
            consts, const_set = sem("consts2"), sem("const_set")
            with nc.Block() as block:
                @block.sync
                def _(sp):
                    sp.dma_start(ident[:], ident_d).then_inc(consts, 16)
                    sp.dma_start(coords[:], coords_d).then_inc(consts, 16)
                    for h in range(CH):
                        sp.dma_start(wd[:, h], dcn_w.rearrange("u v (h p) f -> h p (u v) f", p=128)[h]
                                     ).then_inc(consts, 16)
                    with nc.allow_non_contiguous_dma(reason="256 bias values, once"):
                        sp.dma_start(bias[:], dcn_b.rearrange("(h p) -> p h", p=128)).then_inc(consts, 16)
                    sp.wait_ge(consts, 16 * (3 + CH))

                @block.vector
                def _(dve):
                    nc.vector.memset(k34[:], 0.75).then_inc(const_set, 1)
                    nc.vector.memset(k14[:], 0.25).then_inc(const_set, 1)

        tables()

        def wait(e, sm, v):
            if not isinstance(v, int) or v > 0:
                e.wait_ge(sm, v)

        def load_windows(sp, buf, first, step, signal):
            for a in range(WIN):
                src = bass.AP(tensor=cpad.tensor, offset=first + a * PADC * C,
                              ap=[[C, WIN], [step * C, BLK], [1, C]])
                sp.dma_start(win[buf][WIN * a:WIN * a + WIN], src).then_inc(signal, 16)

        def positions(dve, s, p, chain, start):
            def step(n, f):
                if n:
                    dve.wait_ge(chain, start + n)
                f().then_inc(chain, 1)
            omv = om[p][:, :, 0:2 * GK].rearrange("p x (t g k) -> p t x g k", t=2, k=NK)
            posv = pos[p][:].rearrange("p t x (g k) -> p t x g k", k=NK)
            g = nc.vector
            by = base_y[:, bass.ds(s, 1)].rearrange("p s k -> p (s k)").unsqueeze(1).unsqueeze(1).broadcast_to([128, 2, NG, NK])
            bx = base_x.unsqueeze(2).broadcast_to([128, 2, NG, NK])
            step(0, lambda: g.tensor_tensor(posv[:, 0], omv[:, 0], by, ALU.add))
            step(0, lambda: g.tensor_tensor(posv[:, 1], omv[:, 1], bx, ALU.add))
            step(2, lambda: g.tensor_scalar(lo[:], pos[p][:], 1.0, 1.0, ALU.add, ALU.min))
            step(2, lambda: g.tensor_scalar(hi[:], pos[p][:], -float(H), -1.0, ALU.add, ALU.max))
            step(4, lambda: g.tensor_tensor(lo[:], lo[:], hi[:], ALU.mult))
            step(4, lambda: g.tensor_scalar(pos[p][:], pos[p][:], 0.0, float(H - 1), ALU.max, ALU.min))
            step(5, lambda: g.tensor_scalar(lo[:], lo[:], -1.0, 0.0, ALU.mult, ALU.max))
            step(7, lambda: g.tensor_tensor(lo[:, 0], lo[:, 0], lo[:, 1], ALU.mult))
        NPOS = 8

        def distances(engine, p, hx, q, t, centers):
            return engine.tensor_tensor(
                tap[q][:, t], pos[p][:, t, hx].unsqueeze(2).broadcast_to([128, GK, WIN]),
                centers.unsqueeze(1).broadcast_to([128, GK, WIN]), ALU.subtract)

        def tap_weights(act, q, chain, start):
            nc.scalar.activation(tap[q][:], tap[q][:], ACT.Abs).then_inc(chain, 1)
            act.wait_ge(chain, start + 1)
            nc.scalar.activation(tap[q][:], tap[q][:], ACT.Identity, bias=k34[:], scale=-0.5).then_inc(chain, 1)

        def cap_weights(dve, p, hx, q, chain, start):
            nc.vector.scalar_tensor_tensor(out=tap[q][:], in0=tap[q][:], scalar=0.5, in1=tap[q][:],
                                           op0=ALU.mult, op1=ALU.max).then_inc(chain, 1)
            dve.wait_ge(chain, start + 1)
            nc.vector.tensor_scalar(tap[q][:], tap[q][:], 0.25, 0.0, ALU.add, ALU.max).then_inc(chain, 1)
            dve.wait_ge(chain, start + 2)
            nc.vector.scalar_tensor_tensor(out=tap[q][:, 0], in0=tap[q][:, 0], scalar=0.75,
                                           in1=coef[p][:, hx].unsqueeze(2).broadcast_to([128, GK, WIN]),
                                           op0=ALU.min, op1=ALU.mult).then_inc(chain, 1)
            nc.vector.tensor_scalar(tap[q][:, 1], tap[q][:, 1], 0.75, None, ALU.min).then_inc(chain, 1)

        def window_weights(q, half, g, w):
            gk = (half * GH + g) * NK
            shape = [128, NK, WIN, WIN]
            return nc.vector.tensor_tensor(
                wt[w][:, g * NK:(g + 1) * NK].rearrange("p k (a b) -> p k a b", a=WIN),
                tap[q][:, 0, gk:gk + NK].unsqueeze(3).broadcast_to(shape),
                tap[q][:, 1, gk:gk + NK].unsqueeze(2).broadcast_to(shape), ALU.mult)

        def transpose_batch(w, i, b):
            for j in range(4):
                last = nc.tensor.transpose(tb[b][0:WQ, 128 * j:128 * j + 128], wt[w][:, 4 * i + j, :], ident[:])
            return last

        def copy_batch(e, w, i, b):
            dst, src = wtT[w][:, 4 * i:4 * i + 4, :], tb[b][0:WQ, :].rearrange("p (i c) -> p i c", i=4)
            return nc.scalar.copy(dst, src) if e == "act" else nc.vector.tensor_copy(dst, src)

        def sample_block(w, q, half, j, v):
            for g in range(GH):
                ch = (half * GH + g) * 32
                last = nc.tensor.matmul(vb[v][32 * g:32 * g + 32, 144 * (j % 3):144 * (j % 3) + 144],
                                        win[q][:, j, ch:ch + 32],
                                        wtT[w][:, g * NK:(g + 1) * NK, 16 * j:16 * j + 16],
                                        start=True, stop=True)
            return last

        def samples(p, hx, half, j0, v):
            n = min(3, BLK - j0)
            src = vb[v][:, 0:144 * n].rearrange("p (j k c) -> p k j c", j=n, k=NK)
            at = 128 * hx + 16 * j0
            dst = val[p][:, half, :, at:at + 16 * n].rearrange("p k (j c) -> p k j c", j=n)
            return dst, src

        def project(p, fo, n):
            half, k = n // NK, n % NK
            return nc.tensor.matmul(eb[fo][:, 0:256], wd[:, half, k, 128 * fo:128 * fo + 128], val[p][:, half, k, :],
                                    start=(n == 0), stop=(n == CH * NK - 1))

        def finish(p, fo):
            return nc.scalar.activation(
                res[p][:, fo, :].rearrange("p (r j c) -> p j r c", r=4, c=4),
                eb[fo][:, 0:256].rearrange("p (j r c) -> p j r c", r=4, c=4), ACT.Relu, bias=bias[:, fo:fo + 1])

        def turn_result(p):
            for c2 in range(2):
                for fo in range(CH):
                    last = nc.tensor.transpose(ob[:, 256 * c2 + 128 * fo:256 * c2 + 128 * fo + 128],
                                               res[p][:, fo, 128 * c2:128 * c2 + 128], ident[:])
            return last

        def out_rows(s):
            return out.rearrange("b h w c -> (b h w) c").rearrange("(s t p) c -> s p t c", t=2, p=128
                                                                    )[bass.ds(s, 1)].rearrange("o p t c -> (o p) t c")

        def r_strip(s):
            return r_d[bass.ds(s, 1)].rearrange("o p h c -> (o p) h c")

        def fast():
            names = ("om_ready0 om_ready1 r_ready0 r_ready1 out_stored0 out_stored1 win_ready0 win_ready1 masked "
                     "pchain coef_ready dist_ready achain capped products batched "
                     "tb_out0 tb_out1 tb_out2 sampled vb_out0 vb_out1 projected finished summed turned ob_out").split()
            sems = {n: sem("f_" + n) for n in names}

            def w(e, name, v):
                wait(e, sems[name], v)

            def loop(e, strips):
                strips(0)
                strips(1)
                with e.Fori(2, ST // 2 - 1) as it:
                    strips(it)
                strips(ST // 2 - 1)

            def known(v, least, end):
                return not isinstance(v, int) or least <= v < end

            def copy_samples(e, me, s, p, u, v, half_s):
                if me != ("act", "dve")[(3 * (u - 1) + v) % 2]:
                    return
                n1 = 4 * s + u - 1
                if not known(n1, 0, UNITS * ST):
                    return
                w(e, "sampled", 3 * n1 + v + 1)
                sp_, pp, uu = (s, p, u - 1) if u else (s - 1, 1 - p, 3)
                w(e, "projected", 2 * (sp_ - 1))
                dst, src = samples(pp, uu // 2, uu % 2, 3 * v, (3 * (u - 1) + v) % 2)
                i = nc.scalar.copy(dst, src) if me == "act" else nc.vector.tensor_copy(dst, src)
                i.then_inc(sems[f"vb_out{(3 * (u - 1) + v) % 2}"], 1)

            def sp_fast(sp):
                def strips(it):
                    at = ((it // 8) * (PADC - HC) + 4 * it) * PADC * C
                    if not isinstance(it, int):
                        at = sp.snap(at)
                    for p in range(2):
                        s = 2 * it + p
                        for hx in range(2):
                            w(sp, "sampled", 6 * (2 * s + hx - 1))
                            load_windows(sp, hx, at + 2 * p * PADC * C + 16 * hx * C, 2, sems[f"win_ready{hx}"])
                        w(sp, "summed", s - 1)
                        sp.dma_start(rt[p][:], r_d[bass.ds(it, 1), :, :, 256 * p:256 * p + 256].rearrange(
                            "o p h c -> (o p) h c")).then_inc(sems[f"r_ready{p}"], 16)
                loop(sp, strips)
                for p in range(2):
                    sp.wait_ge(sems[f"out_stored{p}"], 16 * ST // 2)

            def pool_fast(pool):
                def load_om(s, p):
                    pool.dma_start(om[p][:], om_d[bass.ds(s, 1)].rearrange("o p x c -> (o p) x c")
                                   ).then_inc(sems[f"om_ready{p}"], 16)

                def strips(it):
                    for p in range(2):
                        s = 2 * it + p
                        if known(s, 0, ST - 1):
                            w(pool, "masked", s)
                            w(pool, "coef_ready", s)
                            load_om(s + 1, 1 - p)
                        w(pool, "coef_ready", s + 1)
                        for hx in range(2):
                            w(pool, "products", 8 * (2 * s + hx - 1))
                            cy = ctr_y[:, bass.ds(s, 1)].rearrange("p s a -> p (s a)")
                            distances(nc.gpsimd, p, hx, hx, 1, ctr_x[:, hx]).then_inc(sems["dist_ready"], 1)
                            distances(nc.gpsimd, p, hx, hx, 0, cy).then_inc(sems["dist_ready"], 1)
                load_om(0, 0)
                loop(pool, strips)

            def act_fast(act):
                def taps(qg, q):
                    if known(qg, 0, 2 * ST):
                        w(act, "dist_ready", 2 * (qg + 1))
                        tap_weights(act, q, sems["achain"], 2 * qg)

                def sigmoid(s, p, n16):
                    if known(s, 0, ST):
                        w(act, f"om_ready{p}", n16)
                        w(act, "coef_ready", s - 1)
                        nc.scalar.activation(mask[p][:], om[p][:, :, 2 * GK:NOM], ACT.Sigmoid
                                             ).then_inc(sems["masked"], 1)

                def slot(s, p, u, half_s):
                    n = 4 * s + u
                    if u == 0:
                        sigmoid(s + 1, 1 - p, 16 * (half_s + 1 + p))
                    if u == 3 and known(s - 1, 0, ST):
                        w(act, "projected", 2 * (s - 1) + 1)
                        w(act, "turned", s - 2)
                        finish(1 - p, 0).then_inc(sems["finished"], 1)
                    if u == 1 and known(s - 2, 0, ST):
                        w(act, "projected", 2 * (s - 2) + 2)
                        finish(p, 1).then_inc(sems["finished"], 1)
                    for i in range(NT):
                        if known(s, 0, ST):
                            w(act, "batched", 9 * n + i + 1)
                            w(act, "sampled", 3 * (n - 1))
                            copy_batch("act", u % 2, i, i % 3).then_inc(sems[f"tb_out{i % 3}"], 1)
                        if i in (2, 5, 7):
                            copy_samples(act, "act", s, p, u, (2, 5, 7).index(i), half_s)
                        if i == 3 and u % 2 == 0:
                            taps(2 * s + 1 + u // 2, (1 + u // 2) % 2)
                    if u == 2 and known(s - 2, 0, ST):
                        w(act, "turned", s - 1)
                        w(act, f"out_stored{p}", 16 * (half_s - 1))
                        nc.scalar.copy(ot[p][:], ob[:]).then_inc(sems["ob_out"], 1)
                        w(act, "ob_out", s - 1)
                        act.dma_start(out_rows(s - 2), ot[p][:].rearrange("p (t c) -> p t c", t=2)
                                      ).then_inc(sems[f"out_stored{p}"], 16)

                def strips(it):
                    for p in range(2):
                        for u in range(UNITS):
                            slot(2 * it + p, p, u, it)
                sigmoid(0, 0, 16)
                taps(0, 0)
                loop(act, strips)
                strips(ST // 2)

            def dve_fast(dve):
                def cap(s, p, hx):
                    if known(s, 0, ST):
                        w(dve, "achain", 2 * (2 * s + hx + 1))
                        w(dve, "coef_ready", s + 1)
                        cap_weights(dve, p, hx, hx, sems["capped"], 4 * (2 * s + hx))
                        w(dve, "capped", 4 * (2 * s + hx + 1))

                def product(s, p, u, g):
                    if known(s, 0, ST):
                        n = 4 * s + u
                        w(dve, "batched", 9 * (n - 1))
                        window_weights(u // 2, u % 2, g, u % 2).then_inc(sems["products"], 1)

                def place(s, p, n16):
                    if known(s, 0, ST):
                        w(dve, f"om_ready{p}", n16)
                        w(dve, "dist_ready", 4 * (s - 1))
                        positions(dve, s, p, sems["pchain"], NPOS * s)
                        w(dve, "pchain", NPOS * (s + 1))
                        w(dve, "masked", s + 1)
                        nc.vector.tensor_tensor(coef[p][:], lo[:, 0], mask[p][:], ALU.mult).then_inc(sems["coef_ready"], 1)

                def slot(s, p, u, half_s):
                    n = 4 * s + u
                    after = (s, p, u + 1) if u < 3 else (s + 1, 1 - p, 0)
                    if u % 2 == 1:
                        cap(after[0], after[1], after[2] // 2)
                    for i in range(NT):
                        if i in (0, 2, 4, 6):
                            product(*after, i // 2)
                        if i in (2, 5, 7):
                            copy_samples(dve, "dve", s, p, u, (2, 5, 7).index(i), None)
                        if i == 8 and u == 0:
                            place(s + 1, 1 - p, 16 * (half_s + 1 + p))
                        if i == 4 and u == 1 and known(s - 2, 0, ST):
                            w(dve, "finished", 2 * (s - 1))
                            w(dve, f"r_ready{p}", 8 * (s - p))
                            nc.vector.tensor_tensor(res[p][:], res[p][:], rt[p][:], ALU.add).then_inc(sems["summed"], 1)

                def strips(it):
                    for p in range(2):
                        for u in range(UNITS):
                            slot(2 * it + p, p, u, it)
                place(0, 0, 16)
                cap(0, 0, 0)
                for g in range(GH):
                    product(0, 0, 0, g)
                loop(dve, strips)
                strips(ST // 2)

            def pe_fast(pe):
                def slot(s, p, u, half_s):
                    n = 4 * s + u
                    s1, p1, e = (s - 1, 1 - p, u - 1) if u else (s - 2, p, 3)
                    unit = (s, p, u - 1) if u else (s - 1, 1 - p, 3)
                    m6 = 6 * s + (3 * (u - 1)) // 2
                    for i in range(NT):
                        if known(s1, 0, ST):
                            fo, k = e // 2, (e % 2) * NT + i
                            if i == 0 and e % 2 == 0:
                                if fo == 0:
                                    w(pe, "vb_out0", 6 * (s1 + 1))
                                    w(pe, "vb_out1", 6 * (s1 + 1))
                                w(pe, "finished", 2 * (s1 - 1) + fo + 1)
                            last = project(p1, fo, k)
                            if e % 2 and i == NT - 1:
                                last.then_inc(sems["projected"], 1)
                        if known(s, 0, ST):
                            w(pe, "products", 4 * n + (4 * i + 3) // NK + 1)
                            w(pe, f"tb_out{i % 3}", 3 * n + i // 3)
                            transpose_batch(u % 2, i, i % 3).then_inc(sems["batched"], 1)
                        if i < BLK and known(4 * s + u - 1, 0, UNITS * ST):
                            v = (3 * (u - 1) + i // 3)
                            if i % 3 == 0:
                                w(pe, f"vb_out{v % 2}", 6 * s + v // 2)
                            if i == 0:
                                for b in range(3):
                                    w(pe, f"tb_out{b}", 3 * n)
                                w(pe, f"win_ready{unit[2] // 2}", 16 * WIN * (unit[0] + 1))
                            last = sample_block(unit[2] % 2, unit[2] // 2, unit[2] % 2, i, v % 2)
                            if i in (2, 5, 7):
                                last.then_inc(sems["sampled"], 1)
                        if i == 6 and u == 2 and known(s - 2, 0, ST):
                            w(pe, "summed", s - 1)
                            w(pe, "ob_out", s - 2)
                            turn_result(p).then_inc(sems["turned"], 1)

                def strips(it):
                    for p in range(2):
                        for u in range(UNITS):
                            slot(2 * it + p, p, u, it)
                loop(pe, strips)
                strips(ST // 2)

            return sp_fast, pool_fast, act_fast, dve_fast, pe_fast

        def general():
            names = ("om_ready r_ready out_stored win_ready masked pchain coef_ready dist_ready achain capped products "
                     "batched copied sampled zeroed added projected finished summed turned ob_out").split()
            sems = {n: sem("g_" + n) for n in names}
            WINDOWS = NWIN * NWIN
            PER_STRIP = 2 * 2 * 3 * WINDOWS

            def w(e, name, v):
                wait(e, sems[name], v)

            def sp_general(sp):
                pass

            def pool_general(pool):
                pass

            def act_general(act):
                with act.Fori(0, ST) as s:
                    act.dma_start(om[0][:], om_d[bass.ds(s, 1)].rearrange("o p x c -> (o p) x c")
                                  ).then_inc(sems["om_ready"], 16)
                    r_at = (s // 2) * (128 * CH * 512) + (s % 2) * 256
                    act.dma_start(rt[0][:], bass.AP(tensor=r_d.tensor, offset=r_at, ap=[[CH * 512, 128], [512, CH], [1, 256]])
                                  ).then_inc(sems["r_ready"], 16)
                    w(act, "om_ready", 16 * (s + 1))
                    nc.scalar.activation(mask[0][:], om[0][:, :, 2 * GK:NOM], ACT.Sigmoid).then_inc(sems["masked"], 1)
                    with act.Fori(0, NWIN) as wy:
                        with act.Fori(0, NWIN) as wx:
                            at = act.snap((((s // 16) * PADC + PADLO - 1 + WIN * wy) * PADC + PADLO - 1 + WIN * wx) * C)
                            for hx in range(2):
                                t = ((s * NWIN + wy) * NWIN + wx) * 2 + hx
                                load_windows(act, 0, at, 0, sems["win_ready"])
                                w(act, "dist_ready", 2 * (t + 1))
                                tap_weights(act, 0, sems["achain"], 2 * t)
                                w(act, "sampled", 6 * (t + 1))
                    for fo in range(CH):
                        w(act, "projected", 2 * s + fo + 1)
                        finish(0, fo).then_inc(sems["finished"], 1)
                    w(act, "turned", s + 1)
                    nc.scalar.copy(ot[0][:], ob[:]).then_inc(sems["ob_out"], 1)
                    w(act, "ob_out", s + 1)
                    act.dma_start(out_rows(s), ot[0][:].rearrange("p (t c) -> p t c", t=2)
                                  ).then_inc(sems["out_stored"], 16)
                    w(act, "out_stored", 16 * (s + 1))
                    w(act, "coef_ready", s + 1)

            def dve_general(dve):
                with dve.Fori(0, ST) as s:
                    w(dve, "om_ready", 16 * (s + 1))
                    positions(dve, s, 0, sems["pchain"], NPOS * s)
                    w(dve, "pchain", NPOS * (s + 1))
                    w(dve, "masked", s + 1)
                    nc.vector.tensor_tensor(coef[0][:], lo[:, 0], mask[0][:], ALU.mult).then_inc(sems["coef_ready"], 1)
                    w(dve, "coef_ready", s + 1)
                    nc.vector.memset(val[0][:], 0.0).then_inc(sems["zeroed"], 1)
                    with dve.Fori(0, NWIN) as wy:
                        with dve.Fori(0, NWIN) as wx:
                            for hx in range(2):
                                t = ((s * NWIN + wy) * NWIN + wx) * 2 + hx
                                for d, win_no in enumerate((wy, wx)):
                                    centers = ctr_all[:, bass.ds(win_no, 1)].rearrange("p w a -> p (w a)")
                                    distances(nc.vector, 0, hx, 0, d, centers).then_inc(sems["dist_ready"], 1)
                                w(dve, "achain", 2 * (t + 1))
                                cap_weights(dve, 0, hx, 0, sems["capped"], 4 * t)
                                w(dve, "capped", 4 * (t + 1))
                                for half in range(2):
                                    n = 2 * t + half
                                    for g in range(GH):
                                        window_weights(0, half, g, 0).then_inc(sems["products"], 1)
                                    for i in range(NT):
                                        w(dve, "batched", 9 * n + i + 1)
                                        copy_batch("dve", 0, i, i % 3).then_inc(sems["copied"], 1)
                                    for v in range(3):
                                        w(dve, "sampled", 3 * n + v + 1)
                                        w(dve, "zeroed", s + 1)
                                        dst, src = samples(0, hx, half, 3 * v, v % 2)
                                        nc.vector.tensor_tensor(dst, src, dst, ALU.add).then_inc(sems["added"], 1)
                                    w(dve, "products", 4 * (n + 1))
                                    w(dve, "added", 3 * (n + 1))
                    w(dve, "finished", 2 * (s + 1))
                    w(dve, "r_ready", 16 * (s + 1))
                    nc.vector.tensor_tensor(res[0][:], res[0][:], rt[0][:], ALU.add).then_inc(sems["summed"], 1)

            def pe_general(pe):
                with pe.Fori(0, ST) as s:
                    with pe.Fori(0, WINDOWS) as i:
                        for hx in range(2):
                            t = s * (2 * WINDOWS) + 2 * i + hx
                            for half in range(2):
                                n = 2 * t + half
                                for i4 in range(NT):
                                    w(pe, "products", 4 * n + (4 * i4 + 3) // NK + 1)
                                    if i4 >= 3:
                                        w(pe, "copied", 9 * n + i4 - 2)
                                    transpose_batch(0, i4, i4 % 3).then_inc(sems["batched"], 1)
                                w(pe, "copied", 9 * (n + 1))
                                w(pe, "win_ready", 16 * WIN * (t + 1))
                                for v in range(3):
                                    if v == 2:
                                        w(pe, "added", 3 * n + 1)
                                    for j in range(3 * v, min(3 * v + 3, BLK)):
                                        last = sample_block(0, 0, half, j, v % 2)
                                    last.then_inc(sems["sampled"], 1)
                                w(pe, "added", 3 * (n + 1))
                    w(pe, "added", PER_STRIP * (s + 1))
                    for fo in range(CH):
                        for k in range(CH * NK):
                            last = project(0, fo, k)
                        last.then_inc(sems["projected"], 1)
                    w(pe, "summed", s + 1)
                    turn_result(0).then_inc(sems["turned"], 1)
                    w(pe, "ob_out", s + 1)

            return sp_general, pool_general, act_general, dve_general, pe_general

        fast_sp, fast_pool, fast_act, fast_dve, fast_pe = fast()
        gen_sp, gen_pool, gen_act, gen_dve, gen_pe = general()

        def choose(e, fast_path, general_path):
            beyond = e.value_load(flag[0:1, 0:1], min_val=0, max_val=1)
            with e.If(beyond == 0):
                fast_path(e)
            with e.Else():
                general_path(e)

        with nc.Block() as block:
            @block.sync
            def _(sp):
                choose(sp, fast_sp, gen_sp)

            @block.gpsimd
            def _(pool):
                choose(pool, fast_pool, gen_pool)

            @block.scalar
            def _(act):
                choose(act, fast_act, gen_act)

            @block.vector
            def _(dve):
                choose(dve, fast_dve, gen_dve)

            @block.tensor
            def _(pe):
                choose(pe, fast_pe, gen_pe)


def conv_preact(nc, x, coarse, attend_w, select_w, offset_w, om_w, om_b, dcn_w, dcn_b, ident, gmean, coords, out):
    cpad = nc.dram_tensor("cpad", [B, PADC, PADC, C], f32, kind="Internal").ap()
    om_d = nc.dram_tensor("om_d", [ST, 128, 2, NOM], f32, kind="Internal").ap()
    r_d = nc.dram_tensor("r_d", [B * SB, 128, CH, 512], f32, kind="Internal").ap()
    with nc.sbuf_tensor("flag", [1, 1], i32) as flag:
        with nc.sbuf_tensor("wm", [128, 4, NK, NOM], f32) as wm:
            pad_coarse(nc, coarse, cpad)
            merge_weights(nc, om_w, offset_w, ident, wm)
            offsets_and_calibration(nc, x, coarse, attend_w, select_w, om_b, ident, gmean, wm, om_d, r_d, flag)
        sample_and_project(nc, cpad, om_d, r_d, dcn_w, dcn_b, ident, coords, flag, out)


_INS = ["x", "L0_conv_coarse", "L0_conv_attend_w", "L0_conv_select_w", "L0_conv_offset_w", "L0_conv_om_w",
        "L0_conv_om_b", "L0_conv_dcn_w", "L0_conv_dcn_b"]


def _constants():
    import numpy as np
    p = np.arange(128)
    j, r, c = p // 16, p // 4 % 4, p % 4
    block_row = np.arange(ST) % (H // 4)
    k, a, hx = np.arange(NK), np.arange(WIN), np.arange(2)
    base_y = 4 * block_row[None, :, None] + r[:, None, None] + k // 3 - 1
    base_x = 32 * hx[None, :, None] + (4 * j + c)[:, None, None] + k % 3 - 1
    centre = lambda n: 2 * n + 0.5
    ctr_y = np.broadcast_to(centre(2 * block_row[:, None] - PADLO + a), (128, ST, WIN))
    ctr_x = centre(2 * (BLK * hx[None, :, None] + j[:, None, None]) - PADLO + a)
    ctr_all = np.broadcast_to(centre(-1 + WIN * np.arange(NWIN)[:, None] + a), (128, NWIN, WIN))
    coords = np.concatenate([t.reshape(128, -1) for t in (base_y, ctr_y, base_x, ctr_x, ctr_all)], 1)
    return {"ident": np.eye(128, dtype=np.float32),
            "gmean": np.kron(np.eye(16), np.full((8, 8), 0.125)).astype(np.float32),
            "coords": coords.astype(np.float32)}


def kernel(**inputs):
    import numpy as np
    import concourse.bacc as bacc
    from concourse.bass_utils import run_bass_kernel_spmd

    nc = bacc.Bacc("TRN2", target_bir_lowering=False, num_devices=1)
    arrays, args = {}, []
    given = {name: np.ascontiguousarray(inputs[name]) for name in _INS} | _constants()
    for name, a in given.items():
        arrays[f"in_{name}"] = a
        args.append(nc.dram_tensor(f"in_{name}", a.shape, mybir.dt.from_np(a.dtype), kind="ExternalInput").ap())
    out = nc.dram_tensor("out_0", (B, H, W, C), f32, kind="ExternalOutput").ap()
    conv_preact(nc, *args, out)
    got = run_bass_kernel_spmd(nc, [arrays], core_ids=[0])
    return got.results[0]["out_0"]
```

```python
import concourse.bass as bass
from concourse import mybir
from contextlib import ExitStack

B, H, W, C = 4, 64, 64, 256
HC = H // 2
NG, NK = 8, 9
GK = NG * NK
NOM = 3 * GK
OMC = NOM // 2
CH = C // 128
HP = H + 2
CP = HC + 2
WIN = 10
WQ = WIN * WIN
LIMIT = 6.0
PADLO = 4
NWIN = 4
PADC = 43
SB = 8
NS = B * SB
ST = H * B // 4
BLK = 8
GN_EPS = 1e-5

f32 = mybir.dt.float32
f32r = mybir.dt.float32r
i32 = mybir.dt.int32
ACT = mybir.ActivationFunctionType
ALU = mybir.AluOpType
AX = mybir.AxisListType


NCOORD = ST * NK + ST * WIN + 2 * NK + 2 * WIN + NWIN * WIN
NT = 9
UNITS = 4
GH = NG // 2


def pad_rows(e, coarse, cpad, padded):
    hi = PADLO + HC
    for b in range(B):
        e.dma_start(cpad[b, PADLO:hi, PADLO:hi, :], coarse[b]).then_inc(padded, 16)
        e.dma_start(cpad[b, 0:PADLO, PADLO:hi, :], coarse[b, 0:1].broadcast_to([PADLO, HC, C])).then_inc(padded, 16)
        e.dma_start(cpad[b, hi:PADC, PADLO:hi, :], coarse[b, HC - 1:HC].broadcast_to([PADC - hi, HC, C])
                    ).then_inc(padded, 16)


def pad_columns(e, cpad, rows_padded, padded):
    hi = PADLO + HC
    e.wait_ge(rows_padded, 16 * 3 * B)
    for b in range(B):
        for col in [*range(PADLO), *range(hi, PADC)]:
            src = PADLO if col < PADLO else hi - 1
            e.dma_start(cpad[b, :, col, :], cpad[b, :, src, :]).then_inc(padded, 16)


def statistics_and_weights(nc, x, attend_w, om_w, offset_w, ident_d, gmean_d, wm, scale, shift):
    NT = 4
    NBUF = 4
    with ExitStack() as ctx:
        sb = lambda name, shape, dt=f32: ctx.enter_context(nc.sbuf_tensor(name, shape, dt))
        sem = lambda name: ctx.enter_context(nc.semaphore(name))
        ident = sb("ident0", [128, 128])
        gmean = sb("gmean", [128, 128])
        att = sb("att", [128, CH, C])
        ow = sb("ow", [128, NT, 512])
        owT = sb("owT", [128, NT, NT, 128])
        omw = sb("omw", [128, NK, NT, NOM])
        chunk = [sb(f"chunk{i}", [128, 4, C]) for i in range(NBUF)]
        st = sb("st", [128, CH, B, SB, 6])
        mv = sb("mv", [128, CH, B, 2])
        dev, dev2, var, sd, rstd, mfine, gate, mg = (
            sb(n, [128, CH, B]) for n in ("dev", "dev2", "var", "sd", "rstd", "mfine", "gate", "mg"))
        bank = lambda name: ctx.enter_context(nc.psum_tensor(name, [128, 512], f32))
        wps = [bank(f"wps{i}") for i in range(2)]
        xps = [bank(f"xps{i}") for i in range(4)]
        small = bank("small")
        consts, w_loaded, omw_loaded = sem("consts"), sem("w_loaded"), sem("omw_loaded")
        x_loaded = [sem(f"x_loaded{i}") for i in range(NBUF)]
        turned, turned_out, merged, merged_out, wm_hi = (
            sem(n) for n in ("turned", "turned_out", "merged", "merged_out", "wm_hi"))
        x_turned, counted = sem("x_turned"), sem("counted")
        chain, gm_done, gv_done, sd_done, att_done, gate_done = (
            sem(n) for n in ("chain", "gm_done", "gv_done", "sd_done", "att_done", "gate_done"))
        block = ctx.enter_context(nc.Block())
        x_v = x.rearrange("b h w c -> (b h w) c").rearrange("(n t p) c -> n p t c", p=128, t=4)
        flat = lambda t: t[:].rearrange("p h b -> p (h b)")

        @block.sync
        def _(sp):
            sp.dma_start(ident[:], ident_d).then_inc(w_loaded, 16)
            sp.dma_start(ow[:], offset_w.rearrange("(i p) m -> p i m", p=128)).then_inc(w_loaded, 16)
            for n in range(NBUF):
                sp.dma_start(chunk[n][:], x_v[n]).then_inc(x_loaded[n], 16)
            sp.dma_start(omw[:], om_w.rearrange("u v (m p) o -> p (u v) m o", p=128)).then_inc(omw_loaded, 16)
            sp.dma_start(gmean[:], gmean_d).then_inc(consts, 16)
            sp.dma_start(att[:], attend_w.rearrange("(h p) f -> p h f", p=128)).then_inc(consts, 16)
            with sp.Fori(1, NS // NBUF) as m:
                for i in range(NBUF):
                    sp.wait_ge(x_turned, 2 * (NBUF * m + i - NBUF + 1))
                    sp.dma_start(chunk[i][:], x_v[bass.ds(NBUF * m + i, 1)].rearrange("o p t c -> (o p) t c")
                                 ).then_inc(x_loaded[i], 16)

        def turn_weights(pe):
            pe.wait_ge(w_loaded, 32)
            for m in range(NT):
                if m >= 2:
                    pe.wait_ge(turned_out, m - 1)
                for i in range(NT):
                    last = nc.tensor.transpose(wps[m % 2][:, 128 * i:128 * i + 128],
                                               ow[:, i, 128 * m:128 * m + 128], ident[:])
                last.then_inc(turned, 1)

        def merge(pe, n):
            pe.wait_ge(merged_out, n - 1) if n >= 2 else pe.wait_ge(turned_out, NT)
            for m in range(NT):
                last = nc.tensor.matmul(wps[n % 2][:, 0:NOM], owT[:, m, n % NT, :], omw[:, n // NT, m, :],
                                        start=(m == 0), stop=(m == NT - 1))
            last.then_inc(merged, 1)

        @block.tensor
        def _(pe):
            def turn_x(g):
                pe.wait_ge(x_loaded[g % NBUF], 16 * (g // NBUF + 1))
                for h in range(CH):
                    if g >= 2:
                        pe.wait_ge(counted, 2 * (g - 2) + h + 1)
                    for t in range(4):
                        last = nc.tensor.transpose(xps[2 * (g % 2) + h][:, 128 * t:128 * t + 128],
                                                   chunk[g % NBUF][:, t, 128 * h:128 * h + 128], ident[:])
                    last.then_inc(x_turned, 1)
            turn_weights(pe)
            for g in range(NBUF):
                turn_x(g)
            pe.wait_ge(omw_loaded, 16)
            PER = -(-NK * NT // (NS // NBUF - 1))
            for m in range(1, NS // NBUF):
                for n in range(PER * (m - 1), min(PER * m, NK * NT)):
                    merge(pe, n)
                for i in range(NBUF):
                    turn_x(NBUF * m + i)
            pe.wait_ge(consts, 32)
            pe.wait_ge(chain, 1)
            nc.tensor.matmul(small[:, 0:8], gmean[:], mv[:, :, :, 0].rearrange("p h b -> p (h b)"),
                             start=True, stop=True).then_inc(gm_done, 1)
            pe.wait_ge(chain, 5)
            nc.tensor.matmul(small[:, 8:16], gmean[:], flat(var), start=True, stop=True).then_inc(gv_done, 1)
            pe.wait_ge(chain, 8)
            for fo in range(CH):
                for h in range(CH):
                    last = nc.tensor.matmul(small[:, 16 + 4 * fo:20 + 4 * fo], att[:, h, 128 * fo:128 * fo + 128],
                                            mfine[:, h, :], start=(h == 0), stop=(h == CH - 1))
            last.then_inc(att_done, 1)

        @block.scalar
        def _(act):
            act.wait_ge(chain, 6)
            nc.scalar.activation(sd[:], var[:], ACT.Sqrt).then_inc(sd_done, 1)
            act.wait_ge(att_done, 1)
            nc.scalar.activation(flat(gate), small[:, 16:24], ACT.Sigmoid).then_inc(gate_done, 1)

        @block.vector
        def _(dve):
            def count(g):
                for h in range(CH):
                    dve.wait_ge(x_turned, 2 * g + h + 1)
                    nc.vector.bn_stats(st[:, h, g // SB, g % SB, :], xps[2 * (g % 2) + h][:]).then_inc(counted, 1)

            def split(n):
                tap, i = n // NT, n % NT
                factor = 1.0 if i < 2 else 0.5
                dve.wait_ge(merged, n + 1)
                views = [(lambda t: t[:, i, tap, 0:2 * GK].rearrange("p (t q) -> p t q", t=2),
                          wps[n % 2][:, 0:2 * GK].rearrange("p (q t) -> p t q", t=2)),
                         (lambda t: t[:, i, tap, 2 * GK:NOM], wps[n % 2][:, 2 * GK:NOM])]
                for dst, src in views:
                    last = nc.vector.tensor_scalar(dst(wm[0]), src, factor, None, ALU.mult)
                last.then_inc(wm_hi, 1)
                dve.wait_ge(wm_hi, n + 1)
                for dst, src in views:
                    last = nc.vector.scalar_tensor_tensor(out=dst(wm[1]), in0=src, scalar=factor, in1=dst(wm[0]).bitcast(f32),
                                                          op0=ALU.mult, op1=ALU.subtract)
                last.then_inc(merged_out, 1)

            for m in range(NT):
                dve.wait_ge(turned, m + 1)
                nc.vector.tensor_copy(owT[:, m, :, :], wps[m % 2][:].rearrange("p (i c) -> p i c", i=NT)
                                      ).then_inc(turned_out, 1)
            for g in range(NBUF):
                count(g)
            PER = -(-NK * NT // (NS // NBUF - 1))
            for m in range(1, NS // NBUF):
                for n in range(PER * (m - 1), min(PER * m, NK * NT)):
                    split(n)
                for i in range(NBUF):
                    count(NBUF * m + i)

            def link(ins, n):
                ins.then_inc(chain, 1)
                dve.wait_ge(chain, n)
            dve.wait_ge(counted, 2 * NS)
            for h in range(CH):
                for b in range(B):
                    last = nc.vector.bn_aggr(mv[:, h, b, :], st[:, h, b, :, :].rearrange("p n k -> p (n k)"))
            link(last, 1)
            dve.wait_ge(gm_done, 1)
            link(nc.vector.tensor_copy(flat(mg), small[:, 0:8]), 2)
            link(nc.vector.tensor_tensor(dev[:], mv[:, :, :, 0], mg[:], ALU.subtract), 3)
            link(nc.vector.tensor_tensor(dev2[:], dev[:], dev[:], ALU.mult), 4)
            link(nc.vector.tensor_tensor(var[:], dev2[:], mv[:, :, :, 1], ALU.add), 5)
            dve.wait_ge(gv_done, 1)
            link(nc.vector.tensor_scalar(flat(var), small[:, 8:16], GN_EPS, None, ALU.add), 6)
            dve.wait_ge(sd_done, 1)
            link(nc.vector.reciprocal(rstd[:], sd[:]), 7)
            link(nc.vector.tensor_tensor(mfine[:], dev[:], rstd[:], ALU.mult), 8)
            dve.wait_ge(gate_done, 1)
            link(nc.vector.scalar_tensor_tensor(out=flat(scale), in0=flat(gate), scalar=1.0, in1=flat(rstd),
                                                op0=ALU.add, op1=ALU.mult), 9)
            link(nc.vector.scalar_tensor_tensor(out=flat(shift), in0=flat(mg), scalar=-1.0, in1=flat(scale),
                                                op0=ALU.mult, op1=ALU.mult), 10)


def offsets_and_calibration(nc, x, coarse, select_w, om_b, ident_d, cpad, wm, scale, shift, om_d, r_d, flag):
    NSLAB, NRING = 4, 16
    with ExitStack() as ctx:
        sb = lambda name, shape, dt=f32: ctx.enter_context(nc.sbuf_tensor(name, shape, dt))
        sem = lambda name: ctx.enter_context(nc.semaphore(name))
        ident = sb("ident1", [128, 128])
        sel = sb("sel", [128, CH, C])
        omb = sb("omb", [OMC, 2])
        omb4 = sb("omb4", [OMC, 2])
        chunk = [sb(f"xchunk{i}", [128, 4, C]) for i in range(2)]
        xs = [sb(f"xs{i}", [128, CH, 512]) for i in range(2)]
        xn = [sb(f"xn{i}", [128, CH, 512]) for i in range(2)]
        r = [sb(f"r{i}", [128, CH, 512]) for i in range(2)]
        fine = [[sb(f"fine{i}_{q}", [128, CH, 10, HP], f32r) for q in range(2)] for i in range(NSLAB)]
        cs = [sb(f"cs{i}", [128, C]) for i in range(2)]
        cT = sb("cT", [128, CH, 4, CP])
        ux = sb("ux", [128, CH, 4, W])
        up = [[sb(f"up{i}_{q}", [128, CH, 4, HP], f32r) for q in range(2)] for i in range(2)]
        z = sb("z", [OMC, 3, 2, NRING, W])
        part = sb("part", [OMC, 2, 2, 4, W])
        omT = [sb(f"omT{i}", [OMC, 2, 2, 256]) for i in range(2)]
        oms = [sb(f"oms{i}", [128, 4, NOM]) for i in range(2)]
        ext = sb("ext", [128, 2 * NS])
        far = sb("far", [128, 2])
        row = sb("row", [2, 128])
        top = sb("top", [2, 1])
        topr = sb("topr", [1, 2])
        worst = sb("worst", [1, 1])
        bank = lambda name: ctx.enter_context(nc.psum_tensor(name, [128, 512], f32))
        conv, zb, cal, tb = ([bank(f"{n}{i}") for i in range(2)] for n in ("conv", "zb", "cal", "turned"))
        names = ("consts cleared quartered rows_padded padded x_turned xs_done xn_done cal_done hi_done lo_done "
                 "halo_done c_turned cT_done cT_edged ux_near ux_done up_hi_done up_done z_done z_out part_term "
                 "edged conv_done omT_done o_turned oms_done ext_done flag_T flag_T2 flagged").split()
        s = {n: sem(n) for n in names}
        x_ready, c_ready, r_stored, om_stored = ([sem(f"{n}{i}") for i in range(2)]
                                                 for n in ("x_ready", "c_ready", "r_stored", "om_stored"))
        x_v = x.rearrange("b h w c -> (b h w) c").rearrange("(n t p) c -> n p t c", p=128, t=4)
        c_v = coarse.rearrange("b h w c -> (b h w) c").rearrange("(n p) c -> n p c", p=128)

        def w(e, sm, v):
            if not isinstance(v, int) or v > 0:
                e.wait_ge(s[sm] if isinstance(sm, str) else sm, v)

        def known(g):
            return not isinstance(g, int) or 0 <= g < NS

        def upto(g):
            return min(g, NS) if isinstance(g, int) else g

        def loop(e, batch, between=lambda: None):
            batch(0)
            between()
            with e.Fori(1, B - 1) as b:
                batch(b)
            batch(B - 1)

        block = ctx.enter_context(nc.Block())

        @block.sync
        def _(sp):
            def load(g, i):
                sp.dma_start(chunk[i][:], x_v[bass.ds(g, 1)].rearrange("o p t c -> (o p) t c")).then_inc(x_ready[i], 16)
                sp.dma_start(cs[i][:], c_v[bass.ds(g, 1)].rearrange("o p c -> (o p) c")).then_inc(c_ready[i], 16)
            load(0, 0)
            load(1, 1)
            sp.dma_start(ident[:], ident_d).then_inc(s["consts"], 16)
            sp.dma_start(sel[:], select_w.rearrange("(h p) f -> p h f", p=128)).then_inc(s["consts"], 16)
            yx = om_b[0:2 * GK].rearrange("(q t) -> q t", t=2)
            nx = OMC - GK
            with nc.allow_non_contiguous_dma(reason="216 bias values, once"):
                sp.dma_start(omb[0:GK, 0:1], yx[:, 0:1]).then_inc(s["consts"], 16)
                sp.dma_start(omb[GK:OMC, 0:1], yx[0:nx, 1:2]).then_inc(s["consts"], 16)
                sp.dma_start(omb[0:GK - nx, 1:2], yx[nx:GK, 1:2]).then_inc(s["consts"], 16)
                sp.dma_start(omb[GK - nx:OMC, 1:2], om_b[2 * GK:NOM].rearrange("(q t) -> q t", t=1)
                             ).then_inc(s["consts"], 16)

            def batch(b):
                for n in range(SB):
                    g = b * SB + n
                    if known(g + 2):
                        w(sp, "x_turned", 2 * (g + 1))
                        w(sp, "c_turned", g + 1)
                        load(g + 2, n % 2)
            loop(sp, batch)

        @block.tensor
        def _(pe):
            def turn_x(g, i):
                if known(g):
                    pe.wait_ge(x_ready[i % 2], 8 * (g - i % 2) + 16)
                    for h in range(CH):
                        w(pe, "lo_done", 2 * (g - 1) + h + 1)
                        for t in range(4):
                            last = nc.tensor.transpose(cal[h][:, 128 * t:128 * t + 128],
                                                       chunk[i % 2][:, t, 128 * h:128 * h + 128], ident[:])
                        last.then_inc(s["x_turned"], 1)

            def turn_coarse(g, i):
                if known(g):
                    pe.wait_ge(c_ready[i % 2], 8 * (g - i % 2) + 16)
                    w(pe, "cT_done", g)
                    w(pe, "oms_done", 2 * (g - 4) + 1)
                    for h in range(CH):
                        last = nc.tensor.transpose(tb[0][:, 128 * h:128 * h + 128],
                                                   cs[i % 2][:, 128 * h:128 * h + 128], ident[:])
                    last.then_inc(s["c_turned"], 1)

            def calibrate(g, i):
                if known(g):
                    w(pe, "xn_done", g + 1)
                    for fo in range(CH):
                        for h in range(CH):
                            last = nc.tensor.matmul(cal[fo][:], sel[:, h, 128 * fo:128 * fo + 128], xn[i % 2][:, h, :],
                                                    start=(h == 0), stop=(h == CH - 1))
                        last.then_inc(s["cal_done"], 1)

            PARTS = ((0, 0), (0, 1), (1, 0))

            def coarse_products(g, i):
                if known(g):
                    w(pe, "up_done", g + 1)
                    for q in range(6):
                        o, dy = q // 3, q % 3
                        w(pe, "z_out", 6 * g + q - 1)
                        k = 0
                        for wp, ip in PARTS:
                            for h in range(CH):
                                for dx in range(3):
                                    last = nc.tensor.matmul(
                                        zb[q % 2][0:OMC, 0:256], wm[wp][:, CH + h, 3 * dy + dx, OMC * o:OMC * (o + 1)],
                                        up[i % 2][ip][:, h, :, dx:dx + W], start=(k == 0), stop=(k == 17))
                                    k += 1
                        last.then_inc(s["z_done"], 1)

            def turn_offsets(g, i):
                if known(g):
                    w(pe, "omT_done", 2 * (g + 1))
                    w(pe, "cT_done", upto(g + 4))
                    w(pe, "oms_done", 2 * g)
                    for hy in range(2):
                        for hx in range(2):
                            for o in range(2):
                                last = nc.tensor.transpose(tb[hy][:, NOM * hx + OMC * o:NOM * hx + OMC * (o + 1)],
                                                           omT[i % 2][:, o, hy, 128 * hx:128 * hx + 128],
                                                           ident[0:OMC, 0:OMC])
                        last.then_inc(s["o_turned"], 1)

            def convolve(g, i):
                if known(g):
                    w(pe, "halo_done", 4 * upto(g + 2))
                    for o in range(2):
                        w(pe, "omT_done", 2 * (g - 1) + o + 1)
                        k = 0
                        for wp, ip in PARTS:
                            for h in range(CH):
                                for tap in range(NK):
                                    dy, dx = tap // 3, tap % 3
                                    last = nc.tensor.matmul(
                                        conv[o][0:OMC, :], wm[wp][:, h, tap, OMC * o:OMC * (o + 1)],
                                        fine[i % NSLAB][ip][:, h, dy:dy + 8, dx:dx + W],
                                        start=(k == 0), stop=(k == 6 * NK - 1))
                                    k += 1
                        last.then_inc(s["conv_done"], 1)

            pe.wait_ge(s["consts"], 16 * 6)
            pe.wait_ge(s["cleared"], 12)
            for g in range(2):
                turn_x(g, g)
                turn_coarse(g, g)
                calibrate(g, g)
            turn_x(2, 2)
            coarse_products(0, 0)

            def batch(b):
                for n in range(SB):
                    g = b * SB + n
                    turn_coarse(g + 2, n + 2)
                    calibrate(g + 2, n + 2)
                    coarse_products(g + 1, n + 1)
                    turn_x(g + 3, n + 3)
                    turn_offsets(g - 1, n - 1)
                    convolve(g, n)
            loop(pe, batch)
            turn_offsets(NS - 1, SB - 1)
            pe.wait_ge(s["flagged"], 3)
            nc.tensor.transpose(tb[0][0:2, 0:128], far[:], ident[:]).then_inc(s["flag_T"], 1)
            pe.wait_ge(s["flagged"], 5)
            nc.tensor.transpose(tb[1][0:1, 0:2], top[:], ident[0:2, 0:2]).then_inc(s["flag_T2"], 1)

        @block.scalar
        def _(act):
            pad_rows(act, coarse, cpad, s["rows_padded"])
            act.wait_ge(s["consts"], 16 * 6)
            nc.scalar.mul(omb4[:], omb[:], 0.25).then_inc(s["quartered"], 1)

            def keep_x(g, i):
                if known(g):
                    for h in range(CH):
                        w(act, "x_turned", 2 * g + h + 1)
                        w(act, "lo_done", 2 * (g - 2) + h + 1)
                        nc.scalar.copy(xs[i % 2][:, h, :], cal[h][:]).then_inc(s["xs_done"], 1)

            def keep_fine(g, i):
                if known(g):
                    for fo in range(CH):
                        w(act, "cal_done", 2 * g + fo + 1)
                        nc.scalar.copy(fine[i % NSLAB][0][:, fo, 1:9, 1:W + 1],
                                       cal[fo][:].rearrange("p (y x) -> p y x", y=8)).then_inc(s["hi_done"], 1)

            def keep_z(g, i):
                if known(g):
                    w(act, "omT_done", 2 * (g - 2))
                    for q in range(6):
                        o, dy = q // 3, q % 3
                        w(act, "z_done", 6 * g + q + 1)
                        dst = z[:, dy, o, 4 * (i % 4):4 * (i % 4) + 4, :].rearrange("p y x -> p (y x)")
                        if dy == 1:
                            ins = nc.scalar.activation(dst, zb[q % 2][0:OMC, 0:256], ACT.Identity, bias=omb4[:, o:o + 1])
                        else:
                            ins = nc.scalar.copy(dst, zb[q % 2][0:OMC, 0:256])
                        ins.then_inc(s["z_out"], 1)

            act.wait_ge(s["cleared"], 12)
            act.wait_ge(s["quartered"], 1)
            for g in range(2):
                keep_x(g, g)
                keep_fine(g, g)
            keep_x(2, 2)
            keep_z(0, 0)

            def batch(b):
                for n in range(SB):
                    g = b * SB + n
                    keep_fine(g + 2, n + 2)
                    keep_z(g + 1, n + 1)
                    keep_x(g + 3, n + 3)
            loop(act, batch, lambda: pad_columns(act, cpad, s["rows_padded"], s["padded"]))
            act.wait_ge(s["padded"], 16 * B * (PADC - HC))

        @block.gpsimd
        def _(pool):
            for t in [t for pair in fine + up for t in pair]:
                nc.gpsimd.memset(t[:].bitcast(f32), 0.0).then_inc(s["cleared"], 1)

            def store_r(g, i):
                if known(g):
                    w(pool, "lo_done", 2 * (g + 1))
                    pool.dma_start(r_d[bass.ds(g, 1)].rearrange("o p h c -> (o p) h c"), r[i % 2][:]
                                   ).then_inc(r_stored[i % 2], 16)

            def store_offsets(g, i):
                if known(g):
                    w(pool, "oms_done", 2 * (g + 1))
                    pool.dma_start(om_d[bass.ds(2 * g, 2)].rearrange("y p x o -> p y (x o)"),
                                   oms[i % 2][:].rearrange("p (y x) o -> p y (x o)", y=2)).then_inc(om_stored[i % 2], 16)

            store_r(0, 0)
            store_r(1, 1)

            def batch(b):
                for n in range(SB):
                    g = b * SB + n
                    store_r(g + 2, n + 2)
                    store_offsets(g - 1, n - 1)
            loop(pool, batch)
            store_offsets(NS - 1, SB - 1)
            for i in range(2):
                pool.wait_ge(r_stored[i], 16 * NS // 2)
                pool.wait_ge(om_stored[i], 16 * NS // 2)

        @block.vector
        def _(dve):
            TERMS = 5

            def normalise(g, i, b):
                if known(g):
                    w(dve, "xs_done", 2 * (g + 1))
                    for h in range(CH):
                        last = nc.vector.tensor_scalar(xn[i % 2][:, h, :], xs[i % 2][:, h, :], scale[:, h, bass.ds(b, 1)],
                                                       shift[:, h, bass.ds(b, 1)], ALU.mult, ALU.add)
                    last.then_inc(s["xn_done"], 1)

            def upsample_columns(g, i):
                if known(g):
                    w(dve, "c_turned", g + 1)
                    w(dve, "ux_done", g)
                    nc.vector.tensor_copy(cT[:, :, :, 1:HC + 1],
                                          tb[0][:, 0:256].rearrange("p (h y x) -> p h y x", h=CH, y=4)
                                          ).then_inc(s["cT_done"], 1)
                    w(dve, "cT_done", g + 1)
                    rows = cT[:].rearrange("p h y x -> p (h y) x")
                    nc.vector.tensor_copy(rows[:, :, 0:1], rows[:, :, 1:2])
                    nc.vector.tensor_copy(rows[:, :, CP - 1:CP], rows[:, :, CP - 2:CP - 1]).then_inc(s["cT_edged"], 1)
                    uxv = ux[:].rearrange("p h y (x t) -> p (h y) t x", t=2)
                    w(dve, "up_done", g)
                    for t in range(2):
                        last = nc.vector.tensor_scalar(uxv[:, :, t, :], rows[:, :, 1:HC + 1], 0.75, None, ALU.mult)
                    last.then_inc(s["ux_near"], 1)
                    w(dve, "ux_near", g + 1)
                    w(dve, "cT_edged", g + 1)
                    for t in range(2):
                        last = nc.vector.scalar_tensor_tensor(out=uxv[:, :, t, :], in0=rows[:, :, 2 * t:2 * t + HC], scalar=0.25,
                                                              in1=uxv[:, :, t, :], op0=ALU.mult, op1=ALU.add)
                    last.then_inc(s["ux_done"], 1)
                    w(dve, "ux_done", g + 1)
                    w(dve, "z_done", 6 * (g - 1))
                    inner = lambda t: t[:].rearrange("p h y x -> p (h y) x")[:, :, 1:W + 1]
                    hi, lo = up[i % 2]
                    src = ux[:].rearrange("p h y x -> p (h y) x")
                    nc.vector.tensor_copy(inner(hi), src).then_inc(s["up_hi_done"], 1)
                    w(dve, "up_hi_done", g + 1)
                    nc.vector.tensor_tensor(inner(lo), src, inner(hi).bitcast(f32), ALU.subtract).then_inc(s["up_done"], 1)

            def rest_of_fine(g, i):
                if known(g):
                    w(dve, r_stored[i % 2], 8 * (g - i % 2))
                    hi, lo = fine[i % NSLAB]
                    for fo in range(CH):
                        w(dve, "hi_done", 2 * g + fo + 1)
                        nc.vector.tensor_tensor(lo[:, fo, 1:9, 1:W + 1], cal[fo][:].rearrange("p (y x) -> p y x", y=8),
                                                hi[:, fo, 1:9, 1:W + 1].bitcast(f32), ALU.subtract)
                        nc.vector.tensor_tensor(r[i % 2][:, fo, :], cal[fo][:], xs[i % 2][:, fo, :], ALU.add
                                                ).then_inc(s["lo_done"], 1)

            def halo(g, i):
                if known(g):
                    n = i % SB
                    w(dve, "lo_done", 2 * (g + 1))
                    for q in range(2):
                        own, after, before = (fine[(i + d) % NSLAB][q] for d in (0, 1, -1))
                        if n == 0:
                            nc.vector.memset(own[:, :, 0, :].bitcast(f32), 0.0).then_inc(s["halo_done"], 1)
                        else:
                            nc.vector.tensor_copy(before[:, :, 9, :], own[:, :, 1, :]).then_inc(s["halo_done"], 1)
                        if n == SB - 1:
                            nc.vector.memset(own[:, :, 9, :].bitcast(f32), 0.0).then_inc(s["halo_done"], 1)
                        else:
                            nc.vector.tensor_copy(after[:, :, 0, :], own[:, :, 8, :]).then_inc(s["halo_done"], 1)

            def rows_before(n):
                p = 4 * n % NRING
                return ((0, p, 1), (1, p, 3)) if n == 0 else ((0, NRING - 1, 1), (1, 0, 3)) if p == 0 else ((0, p - 1, 4),)

            def rows_after(n):
                p = 4 * n % NRING
                return ((0, p + 1, 3), (3, p + 3, 1)) if n == SB - 1 else \
                    ((0, p + 1, 3), (3, 0, 1)) if p == NRING - 4 else ((0, p + 1, 4),)

            def upsample_rows(g, n):
                here, before, after = ((0, 4 * n % NRING, 4),), rows_before(n), rows_after(n)
                zr = lambda dy, at, k: z[:, dy, :, at:at + k, :].rearrange("p o y x -> p o (y x)")
                pr = lambda t, at, k: part[:, t, :, at:at + k, :].rearrange("p o y x -> p o (y x)")
                w(dve, "z_out", 6 * upto(g + 2))
                w(dve, "omT_done", 2 * g)
                terms = (((1, 3.0, here), (1, 3.0, here)),
                         ((2, 3.0, here), (0, 3.0, here)),
                         ((0, 3.0, before), (0, 1.0, before)),
                         ((1, 1.0, before), (1, 1.0, after)),
                         ((2, 1.0, after), (2, 3.0, after)))
                for k, pair in enumerate(terms):
                    w(dve, "part_term", TERMS * g + k)
                    for t, (dy, factor, rows) in enumerate(pair):
                        for at, place, m in rows:
                            add_to = pr(t, at, m) if k > 0 else zr((0, 2)[t], place, m)
                            last = nc.vector.scalar_tensor_tensor(out=pr(t, at, m), in0=zr(dy, place, m), scalar=factor,
                                                                  in1=add_to, op0=ALU.mult, op1=ALU.add)
                    last.then_inc(s["part_term"], 1)
                w(dve, "part_term", TERMS * (g + 1))
                if n in (0, SB - 1):
                    t, dy, at, place = (0, 0, 0, 0) if n == 0 else (1, 2, 3, NRING - 1)
                    nc.vector.scalar_tensor_tensor(out=pr(t, at, 1), in0=zr(dy, place, 1), scalar=-4.0, in1=pr(t, at, 1),
                                                   op0=ALU.mult, op1=ALU.add).then_inc(s["edged"], 1)

            def offsets_out(g, i):
                if known(g):
                    w(dve, om_stored[i % 2], 8 * (g - i % 2))
                    for hy in range(2):
                        w(dve, "o_turned", 2 * g + hy + 1)
                        nc.vector.tensor_copy(oms[i % 2][:, 2 * hy:2 * hy + 2, :],
                                              tb[hy][:, 0:2 * NOM].rearrange("p (x o) -> p x o", x=2)
                                              ).then_inc(s["oms_done"], 1)
                    w(dve, "oms_done", 2 * (g + 1))
                    for k, op in enumerate((ALU.max, ALU.min)):
                        nc.vector.tensor_reduce(ext[:, bass.ds(g + k * NS, 1)], oms[i % 2][:, :, 0:2 * GK], axis=AX.XY, op=op
                                                ).then_inc(s["ext_done"], 1)

            def add_parts(b, n):
                g = b * SB + n
                if n in (0, SB - 1):
                    w(dve, "edged", 2 * b + (1 if n == 0 else 2))
                w(dve, "o_turned", 2 * (g - 1))
                for o in range(2):
                    w(dve, "conv_done", 2 * g + o + 1)
                    for hy in range(2):
                        for t in range(2):
                            last = nc.vector.tensor_tensor(
                                omT[n % 2][:, o, hy, :].rearrange("p (j a t c) -> p t a j c", a=2, t=2, c=4)[:, t],
                                conv[o][0:OMC, 256 * hy:256 * hy + 256].rearrange("p (a t j c) -> p t a j c", a=2, t=2, c=4)[:, t],
                                part[:, t, o, 2 * hy:2 * hy + 2, :].rearrange("p a (j c) -> p a j c", c=4), ALU.add)
                    last.then_inc(s["omT_done"], 1)

            dve.wait_ge(s["cleared"], 12)
            for g in range(2):
                normalise(g, g, 0)
                upsample_columns(g, g)
                rest_of_fine(g, g)
                halo(g, g)
            normalise(2, 2, 0)

            def batch(b):
                for n in range(SB):
                    g = b * SB + n
                    upsample_columns(g + 2, n + 2)
                    rest_of_fine(g + 2, n + 2)
                    halo(g + 2, n + 2)
                    upsample_rows(g, n)
                    normalise(g + 3, n + 3, b + (n + 3) // SB)
                    offsets_out(g - 1, n - 1)
                    add_parts(b, n)
            loop(dve, batch)
            offsets_out(NS - 1, SB - 1)

            dve.wait_ge(s["ext_done"], 2 * NS)
            nc.vector.tensor_reduce(far[:, 0:1], ext[:, 0:NS], axis=AX.X, op=ALU.max).then_inc(s["flagged"], 1)
            nc.vector.tensor_reduce(far[:, 1:2], ext[:, NS:], axis=AX.X, op=ALU.min).then_inc(s["flagged"], 1)
            dve.wait_ge(s["flagged"], 2)
            nc.vector.tensor_scalar(far[:, 1:2], far[:, 1:2], -1.0, None, ALU.mult).then_inc(s["flagged"], 1)
            dve.wait_ge(s["flag_T"], 1)
            nc.vector.tensor_copy(row[:], tb[0][0:2, 0:128]).then_inc(s["flagged"], 1)
            dve.wait_ge(s["flagged"], 4)
            nc.vector.tensor_reduce(top[:], row[:], axis=AX.X, op=ALU.max).then_inc(s["flagged"], 1)
            dve.wait_ge(s["flag_T2"], 1)
            nc.vector.tensor_copy(topr[:], tb[1][0:1, 0:2]).then_inc(s["flagged"], 1)
            dve.wait_ge(s["flagged"], 6)
            nc.vector.tensor_reduce(worst[:], topr[:], axis=AX.X, op=ALU.max).then_inc(s["flagged"], 1)
            dve.wait_ge(s["flagged"], 7)
            nc.vector.tensor_scalar(flag[:], worst[:], LIMIT, None, ALU.is_gt).then_inc(s["flagged"], 1)


def sample_and_project(nc, cpad, om_d, r_d, dcn_w, dcn_b, ident_d, coords_d, flag, out):
    ctx = ExitStack()
    with ctx:
        sb = lambda name, shape, dt=f32: ctx.enter_context(nc.sbuf_tensor(name, shape, dt))
        sem = lambda name: ctx.enter_context(nc.semaphore(name))
        ident = sb("ident2", [128, 128])
        coords = sb("coords", [128, NCOORD])
        base_y = coords[:, 0:ST * NK].rearrange("p (s k) -> p s k", k=NK)
        o = ST * NK
        ctr_y = coords[:, o:o + ST * WIN].rearrange("p (s a) -> p s a", a=WIN)
        o += ST * WIN
        base_x = coords[:, o:o + 2 * NK].rearrange("p (x k) -> p x k", k=NK)
        o += 2 * NK
        ctr_x = coords[:, o:o + 2 * WIN].rearrange("p (x a) -> p x a", a=WIN)
        o += 2 * WIN
        ctr_all = coords[:, o:o + NWIN * WIN].rearrange("p (w a) -> p w a", a=WIN)
        wd = [sb(f"wd{q}", [128, CH, NK, C], f32r) for q in range(2)]
        bias = sb("bias", [128, CH])
        k34, k14 = sb("k34", [128, 1]), sb("k14", [128, 1])
        om = [sb(f"om{i}", [128, 2, NOM]) for i in range(2)]
        pos = [sb(f"pos{i}", [128, 2, 2, GK]) for i in range(2)]
        lo, hi = sb("lo", [128, 2, 2, GK]), sb("hi", [128, 2, 2, GK])
        mask = [sb(f"mask{i}", [128, 2, GK]) for i in range(2)]
        coef = [sb(f"coef{i}", [128, 2, GK]) for i in range(2)]
        tap = [sb(f"tap{i}", [128, 2, GK, WIN]) for i in range(2)]
        NWT, NSUM = GH * NK * WQ, CH * NK * 256
        wt_all = sb("wt_all", [128, NWT + NSUM])
        wt = [wt_all[:, i * NWT:(i + 1) * NWT].rearrange("p (k q) -> p k q", q=WQ) for i in range(2)]
        sums = wt_all[:, NWT:].rearrange("p (h k c) -> p h k c", h=CH, k=NK)
        wtT = [sb(f"wtT{i}", [WQ, GH * NK, 128]) for i in range(2)]
        win = [sb(f"win{i}", [WQ, BLK, C]) for i in range(2)]
        val = [sb(f"val{q}", [128, CH, NK, 256], f32r) for q in range(2)]
        res = [sb(f"res{i}", [128, CH, 256]) for i in range(2)]
        rt = [sb(f"rt{i}", [128, CH, 256]) for i in range(2)]
        ot = [sb(f"ot{i}", [128, 512]) for i in range(2)]
        bank = lambda name: ctx.enter_context(nc.psum_tensor(name, [128, 512], f32))
        tb = [bank(f"tb{i}") for i in range(3)]
        vb = [bank(f"vb{i}") for i in range(3)]
        eb = [bank(f"eb{i}") for i in range(2)]
        ob = [b[:, 256:512] for b in eb]

        def tables():
            consts, const_set, wd_hi, wd_lo = sem("consts2"), sem("const_set"), sem("wd_hi"), sem("wd_lo")
            raw = [wt_all[:, h * NK * C:(h + 1) * NK * C].rearrange("p (k c) -> p k c", k=NK) for h in range(CH)]
            loaded = [sem(f"wd_loaded{h}") for h in range(CH)]
            with nc.Block() as block:
                @block.sync
                def _(sp):
                    for h in range(CH):
                        sp.dma_start(raw[h], dcn_w.rearrange("u v (h p) f -> h p (u v) f", p=128)[h]
                                     ).then_inc(loaded[h], 16)
                    sp.dma_start(ident[:], ident_d).then_inc(consts, 16)
                    sp.dma_start(coords[:], coords_d).then_inc(consts, 16)
                    with nc.allow_non_contiguous_dma(reason="256 bias values, once"):
                        sp.dma_start(bias[:], dcn_b.rearrange("(h p) -> p h", p=128)).then_inc(consts, 16)
                    sp.wait_ge(consts, 16 * 3)

                @block.vector
                def _(dve):
                    nc.vector.memset(k34[:], 0.75).then_inc(const_set, 1)
                    nc.vector.memset(k14[:], 0.25).then_inc(const_set, 1)
                    for h in range(CH):
                        dve.wait_ge(wd_hi, h + 1)
                        nc.vector.tensor_tensor(wd[1][:, h], raw[h], wd[0][:, h].bitcast(f32), ALU.subtract
                                                ).then_inc(wd_lo, 1)

                @block.scalar
                def _(act):
                    for h in range(CH):
                        act.wait_ge(loaded[h], 16)
                        nc.scalar.copy(wd[0][:, h], raw[h]).then_inc(wd_hi, 1)

        tables()

        def wait(e, sm, v):
            if not isinstance(v, int) or v > 0:
                e.wait_ge(sm, v)

        def load_windows(sp, buf, first, step, signal):
            for a in range(WIN):
                src = bass.AP(tensor=cpad.tensor, offset=first + a * PADC * C,
                              ap=[[C, WIN], [step * C, BLK], [1, C]])
                sp.dma_start(win[buf][WIN * a:WIN * a + WIN], src).then_inc(signal, 16)

        def positions(dve, s, p, chain, start):
            def step(n, f):
                if n:
                    dve.wait_ge(chain, start + n)
                f().then_inc(chain, 1)
            omv = om[p][:, :, 0:2 * GK].rearrange("p x (t g k) -> p t x g k", t=2, k=NK)
            posv = pos[p][:].rearrange("p t x (g k) -> p t x g k", k=NK)
            g = nc.vector
            by = base_y[:, bass.ds(s, 1)].rearrange("p s k -> p (s k)").unsqueeze(1).unsqueeze(1).broadcast_to([128, 2, NG, NK])
            bx = base_x.unsqueeze(2).broadcast_to([128, 2, NG, NK])
            step(0, lambda: g.tensor_tensor(posv[:, 0], omv[:, 0], by, ALU.add))
            step(0, lambda: g.tensor_tensor(posv[:, 1], omv[:, 1], bx, ALU.add))
            step(2, lambda: g.tensor_scalar(lo[:], pos[p][:], 1.0, 1.0, ALU.add, ALU.min))
            step(2, lambda: g.tensor_scalar(hi[:], pos[p][:], -float(H), -1.0, ALU.add, ALU.max))
            step(4, lambda: g.tensor_tensor(lo[:], lo[:], hi[:], ALU.mult))
            step(4, lambda: g.tensor_scalar(pos[p][:], pos[p][:], 0.0, float(H - 1), ALU.max, ALU.min))
            step(5, lambda: g.tensor_scalar(lo[:], lo[:], -1.0, 0.0, ALU.mult, ALU.max))
            step(7, lambda: g.tensor_tensor(lo[:, 0], lo[:, 0], lo[:, 1], ALU.mult))
        NPOS = 8

        def distances(engine, p, hx, q, t, centers):
            return engine.tensor_tensor(
                tap[q][:, t], pos[p][:, t, hx].unsqueeze(2).broadcast_to([128, GK, WIN]),
                centers.unsqueeze(1).broadcast_to([128, GK, WIN]), ALU.subtract)

        def tap_weights(act, q, chain, start):
            nc.scalar.activation(tap[q][:], tap[q][:], ACT.Abs).then_inc(chain, 1)
            act.wait_ge(chain, start + 1)
            nc.scalar.activation(tap[q][:], tap[q][:], ACT.Identity, bias=k34[:], scale=-0.5).then_inc(chain, 1)

        def cap_weights(dve, p, hx, q, chain, start):
            nc.vector.scalar_tensor_tensor(out=tap[q][:], in0=tap[q][:], scalar=0.5, in1=tap[q][:],
                                           op0=ALU.mult, op1=ALU.max).then_inc(chain, 1)
            dve.wait_ge(chain, start + 1)
            nc.vector.tensor_scalar(tap[q][:], tap[q][:], 0.25, 0.0, ALU.add, ALU.max).then_inc(chain, 1)
            dve.wait_ge(chain, start + 2)
            nc.vector.scalar_tensor_tensor(out=tap[q][:, 0], in0=tap[q][:, 0], scalar=0.75,
                                           in1=coef[p][:, hx].unsqueeze(2).broadcast_to([128, GK, WIN]),
                                           op0=ALU.min, op1=ALU.mult).then_inc(chain, 1)
            nc.vector.tensor_scalar(tap[q][:, 1], tap[q][:, 1], 0.75, None, ALU.min).then_inc(chain, 1)

        def window_weights(q, half, g, w):
            gk = (half * GH + g) * NK
            shape = [128, NK, WIN, WIN]
            return nc.vector.tensor_tensor(
                wt[w][:, g * NK:(g + 1) * NK].rearrange("p k (a b) -> p k a b", a=WIN),
                tap[q][:, 0, gk:gk + NK].unsqueeze(3).broadcast_to(shape),
                tap[q][:, 1, gk:gk + NK].unsqueeze(2).broadcast_to(shape), ALU.mult)

        def transpose_batch(w, i, b):
            for j in range(4):
                last = nc.tensor.transpose(tb[b][0:WQ, 128 * j:128 * j + 128], wt[w][:, 4 * i + j, :], ident[:])
            return last

        def copy_batch(e, w, i, b):
            dst, src = wtT[w][:, 4 * i:4 * i + 4, :], tb[b][0:WQ, :].rearrange("p (i c) -> p i c", i=4)
            return nc.scalar.copy(dst, src) if e == "act" else nc.vector.tensor_copy(dst, src)

        def sample_block(w, q, half, j, v):
            for g in range(GH):
                ch = (half * GH + g) * 32
                last = nc.tensor.matmul(vb[v][32 * g:32 * g + 32, 144 * (j % 3):144 * (j % 3) + 144],
                                        win[q][:, j, ch:ch + 32],
                                        wtT[w][:, g * NK:(g + 1) * NK, 16 * j:16 * j + 16],
                                        start=True, stop=True)
            return last

        def samples(of, hx, half, j0, v):
            n = min(3, BLK - j0)
            src = vb[v][:, 0:144 * n].rearrange("p (j k c) -> p k j c", j=n, k=NK)
            at = 128 * hx + 16 * j0
            dst = of[:, half, :, at:at + 16 * n].rearrange("p k (j c) -> p k j c", j=n)
            return dst, src

        def project(half, k):
            for fo in range(CH):
                for wp, vp in ((0, 0), (0, 1), (1, 0)):
                    last = nc.tensor.matmul(eb[fo][:, 0:256], wd[wp][:, half, k, 128 * fo:128 * fo + 128],
                                            val[vp][:, half, k, :], start=(half == 0 and k == 0 and wp + vp == 0),
                                            stop=(half == CH - 1 and k == NK - 1 and wp == 1))
            return last

        def finish(p, fo):
            return nc.scalar.activation(
                res[p][:, fo, :].rearrange("p (r j c) -> p j r c", r=4, c=4),
                eb[fo][:, 0:256].rearrange("p (j r c) -> p j r c", r=4, c=4), ACT.Relu, bias=bias[:, fo:fo + 1])

        def turn_result(p):
            for c2 in range(2):
                for fo in range(CH):
                    last = nc.tensor.transpose(ob[c2][:, 128 * fo:128 * fo + 128],
                                               res[p][:, fo, 128 * c2:128 * c2 + 128], ident[:])
            return last

        def copy_result(p):
            for c2 in range(2):
                last = nc.scalar.copy(ot[p][:, 256 * c2:256 * c2 + 256], ob[c2])
            return last

        def out_rows(s):
            return out.rearrange("b h w c -> (b h w) c").rearrange("(s t p) c -> s p t c", t=2, p=128
                                                                    )[bass.ds(s, 1)].rearrange("o p t c -> (o p) t c")

        def r_strip(s):
            return r_d[bass.ds(s, 1)].rearrange("o p h c -> (o p) h c")

        def fast():
            names = ("om_ready0 om_ready1 r_ready0 r_ready1 out_stored0 out_stored1 win_ready0 win_ready1 masked "
                     "pchain coef_ready dist_ready achain capped products batched "
                     "tb_out0 tb_out1 tb_out2 sampled val_hi vb_out0 vb_out1 vb_out2 projected finished summed turned ob_out").split()
            sems = {n: sem("f_" + n) for n in names}

            def w(e, name, v):
                wait(e, sems[name], v)

            def loop(e, strips):
                strips(0)
                strips(1)
                with e.Fori(2, ST // 2 - 1) as it:
                    strips(it)
                strips(ST // 2 - 1)

            def known(v, least, end):
                return not isinstance(v, int) or least <= v < end

            def copy_samples(e, me, s, u, v):
                n1 = 4 * s + u - 1
                if not known(n1, 0, UNITS * ST):
                    return
                strip, unit = (s, u - 1) if u else (s - 1, 3)
                half = unit % 2
                dst, src = samples(val[0], unit // 2, half, 3 * v, v)
                if me == "act":
                    w(e, "sampled", 3 * n1 + v + 1)
                    w(e, "projected", 2 * (strip - 1) + half + 1)
                    nc.scalar.copy(dst, src).then_inc(sems["val_hi"], 1)
                else:
                    w(e, "val_hi", 3 * n1 + v + 1)
                    rest, _ = samples(val[1], unit // 2, half, 3 * v, v)
                    nc.vector.tensor_tensor(rest, src, dst.bitcast(f32), ALU.subtract).then_inc(sems[f"vb_out{v}"], 1)

            def sp_fast(sp):
                def strips(it):
                    at = ((it // 8) * (PADC - HC) + 4 * it) * PADC * C
                    if not isinstance(it, int):
                        at = sp.snap(at)
                    for p in range(2):
                        s = 2 * it + p
                        for hx in range(2):
                            w(sp, "sampled", 6 * (2 * s + hx - 1))
                            load_windows(sp, hx, at + 2 * p * PADC * C + 16 * hx * C, 2, sems[f"win_ready{hx}"])
                        w(sp, "summed", s - 1)
                        sp.dma_start(rt[p][:], r_d[bass.ds(it, 1), :, :, 256 * p:256 * p + 256].rearrange(
                            "o p h c -> (o p) h c")).then_inc(sems[f"r_ready{p}"], 16)
                loop(sp, strips)
                for p in range(2):
                    sp.wait_ge(sems[f"out_stored{p}"], 16 * ST // 2)

            def pool_fast(pool):
                def load_om(s, p):
                    pool.dma_start(om[p][:], om_d[bass.ds(s, 1)].rearrange("o p x c -> (o p) x c")
                                   ).then_inc(sems[f"om_ready{p}"], 16)

                def strips(it):
                    for p in range(2):
                        s = 2 * it + p
                        if known(s, 0, ST - 1):
                            w(pool, "masked", s)
                            w(pool, "coef_ready", s)
                            load_om(s + 1, 1 - p)
                        w(pool, "coef_ready", s + 1)
                        for hx in range(2):
                            w(pool, "products", 8 * (2 * s + hx - 1))
                            cy = ctr_y[:, bass.ds(s, 1)].rearrange("p s a -> p (s a)")
                            distances(nc.gpsimd, p, hx, hx, 1, ctr_x[:, hx]).then_inc(sems["dist_ready"], 1)
                            distances(nc.gpsimd, p, hx, hx, 0, cy).then_inc(sems["dist_ready"], 1)
                load_om(0, 0)
                loop(pool, strips)

            def act_fast(act):
                def taps(qg, q):
                    if known(qg, 0, 2 * ST):
                        w(act, "dist_ready", 2 * (qg + 1))
                        tap_weights(act, q, sems["achain"], 2 * qg)

                def sigmoid(s, p, n16):
                    if known(s, 0, ST):
                        w(act, f"om_ready{p}", n16)
                        w(act, "coef_ready", s - 1)
                        nc.scalar.activation(mask[p][:], om[p][:, :, 2 * GK:NOM], ACT.Sigmoid
                                             ).then_inc(sems["masked"], 1)

                def slot(s, p, u, half_s):
                    n = 4 * s + u
                    if u == 0:
                        sigmoid(s + 1, 1 - p, 16 * (half_s + 1 + p))
                    if u == 2 and known(s - 1, 0, ST):
                        w(act, "projected", 2 * s)
                        w(act, "turned", s - 2)
                        for fo in range(CH):
                            finish(1 - p, fo).then_inc(sems["finished"], 1)
                    for i in range(NT):
                        if known(s, 0, ST):
                            w(act, "batched", 9 * n + i + 1)
                            w(act, "sampled", 3 * (n - 1))
                            copy_batch("act", u % 2, i, i % 3).then_inc(sems[f"tb_out{i % 3}"], 1)
                        if i in (2, 5, 7):
                            copy_samples(act, "act", s, u, (2, 5, 7).index(i))
                        if (u, i) in ((0, 3), (1, 6)):
                            taps(2 * s + 1 + u, 1 - u)
                    if u == 3 and known(s - 2, 0, ST):
                        w(act, "turned", s - 1)
                        w(act, f"out_stored{p}", 16 * (half_s - 1))
                        copy_result(p).then_inc(sems["ob_out"], 1)
                        w(act, "ob_out", s - 1)
                        act.dma_start(out_rows(s - 2), ot[p][:].rearrange("p (t c) -> p t c", t=2)
                                      ).then_inc(sems[f"out_stored{p}"], 16)

                def strips(it):
                    for p in range(2):
                        for u in range(UNITS):
                            slot(2 * it + p, p, u, it)
                sigmoid(0, 0, 16)
                taps(0, 0)
                loop(act, strips)
                strips(ST // 2)

            def dve_fast(dve):
                def cap(s, p, hx):
                    if known(s, 0, ST):
                        w(dve, "achain", 2 * (2 * s + hx + 1))
                        w(dve, "coef_ready", s + 1)
                        cap_weights(dve, p, hx, hx, sems["capped"], 4 * (2 * s + hx))
                        w(dve, "capped", 4 * (2 * s + hx + 1))

                def product(s, p, u, g):
                    if known(s, 0, ST):
                        n = 4 * s + u
                        w(dve, "batched", 9 * (n - 1))
                        window_weights(u // 2, u % 2, g, u % 2).then_inc(sems["products"], 1)

                def place(s, p, n16):
                    if known(s, 0, ST):
                        w(dve, f"om_ready{p}", n16)
                        w(dve, "dist_ready", 4 * (s - 1))
                        positions(dve, s, p, sems["pchain"], NPOS * s)
                        w(dve, "pchain", NPOS * (s + 1))
                        w(dve, "masked", s + 1)
                        nc.vector.tensor_tensor(coef[p][:], lo[:, 0], mask[p][:], ALU.mult).then_inc(sems["coef_ready"], 1)

                def slot(s, p, u, half_s):
                    n = 4 * s + u
                    after = (s, p, u + 1) if u < 3 else (s + 1, 1 - p, 0)
                    for i in range(NT):
                        if i in (0, 2, 4, 6):
                            product(*after, i // 2)
                        if i in (2, 5, 7):
                            copy_samples(dve, "dve", s, u, (2, 5, 7).index(i))
                        if i == 1 and u == 0:
                            place(s + 1, 1 - p, 16 * (half_s + 1 + p))
                        if i == 8 and u == 0:
                            cap(s, p, 1)
                        if i == 8 and u == 1:
                            cap(s + 1, 1 - p, 0)
                        if i == 4 and u == 1 and known(s - 2, 0, ST):
                            w(dve, "finished", 2 * (s - 1))
                            w(dve, f"r_ready{p}", 8 * (s - p))
                            nc.vector.tensor_tensor(res[p][:], res[p][:], rt[p][:], ALU.add).then_inc(sems["summed"], 1)

                def strips(it):
                    for p in range(2):
                        for u in range(UNITS):
                            slot(2 * it + p, p, u, it)
                place(0, 0, 16)
                cap(0, 0, 0)
                for g in range(GH):
                    product(0, 0, 0, g)
                loop(dve, strips)
                strips(ST // 2)

            def pe_fast(pe):
                LATE = 3

                def slot(s, p, u, half_s):
                    n = 4 * s + u
                    unit = (s, p, u - 1) if u else (s - 1, 1 - p, 3)
                    for i in range(NT):
                        if known(s, 0, ST):
                            w(pe, "products", 4 * n + (4 * i + 3) // NK + 1)
                            w(pe, f"tb_out{i % 3}", 3 * n + i // 3)
                            transpose_batch(u % 2, i, i % 3).then_inc(sems["batched"], 1)
                        if u < CH and i >= LATE and known(s - 1, 0, ST):
                            if i == LATE:
                                for v in range(3):
                                    w(pe, f"vb_out{v}", 4 * (s - 1) + 3 + u)
                                w(pe, "finished", 2 * (s - 1))
                                w(pe, "ob_out", s - 2)
                            for k in range(NK * (i - LATE) // (NT - LATE), NK * (i - LATE + 1) // (NT - LATE)):
                                last = project(u, k)
                            if i == NT - 1:
                                last.then_inc(sems["projected"], 1)
                        if i < BLK and known(4 * s + u - 1, 0, UNITS * ST):
                            v = i // 3
                            if i % 3 == 0:
                                w(pe, f"vb_out{v}", n - 1)
                            if i == 0:
                                for b in range(3):
                                    w(pe, f"tb_out{b}", 3 * n)
                                w(pe, f"win_ready{unit[2] // 2}", 16 * WIN * (unit[0] + 1))
                            last = sample_block(unit[2] % 2, unit[2] // 2, unit[2] % 2, i, v)
                            if i in (2, 5, 7):
                                last.then_inc(sems["sampled"], 1)
                        if i == 6 and u == 2 and known(s - 2, 0, ST):
                            w(pe, "summed", s - 1)
                            w(pe, "finished", 2 * (min(s, ST) if isinstance(s, int) else s))
                            w(pe, "ob_out", s - 2)
                            turn_result(p).then_inc(sems["turned"], 1)

                def strips(it):
                    for p in range(2):
                        for u in range(UNITS):
                            slot(2 * it + p, p, u, it)
                loop(pe, strips)
                strips(ST // 2)

            return sp_fast, pool_fast, act_fast, dve_fast, pe_fast

        def general():
            names = ("om_ready r_ready out_stored win_ready masked pchain coef_ready dist_ready achain capped products "
                     "batched copied sampled zeroed added val_hi split projected finished summed turned ob_out").split()
            sems = {n: sem("g_" + n) for n in names}
            WINDOWS = NWIN * NWIN

            def w(e, name, v):
                wait(e, sems[name], v)

            def sp_general(sp):
                pass

            def pool_general(pool):
                pass

            def act_general(act):
                with act.Fori(0, ST) as s:
                    act.dma_start(om[0][:], om_d[bass.ds(s, 1)].rearrange("o p x c -> (o p) x c")
                                  ).then_inc(sems["om_ready"], 16)
                    r_at = (s // 2) * (128 * CH * 512) + (s % 2) * 256
                    act.dma_start(rt[0][:], bass.AP(tensor=r_d.tensor, offset=r_at, ap=[[CH * 512, 128], [512, CH], [1, 256]])
                                  ).then_inc(sems["r_ready"], 16)
                    w(act, "om_ready", 16 * (s + 1))
                    nc.scalar.activation(mask[0][:], om[0][:, :, 2 * GK:NOM], ACT.Sigmoid).then_inc(sems["masked"], 1)
                    with act.Fori(0, NWIN) as wy:
                        with act.Fori(0, NWIN) as wx:
                            at = act.snap((((s // 16) * PADC + PADLO - 1 + WIN * wy) * PADC + PADLO - 1 + WIN * wx) * C)
                            for hx in range(2):
                                t = ((s * NWIN + wy) * NWIN + wx) * 2 + hx
                                load_windows(act, 0, at, 0, sems["win_ready"])
                                w(act, "dist_ready", 2 * (t + 1))
                                tap_weights(act, 0, sems["achain"], 2 * t)
                                w(act, "sampled", 6 * (t + 1))
                    for fo in range(CH):
                        w(act, "projected", s + 1)
                        finish(0, fo).then_inc(sems["finished"], 1)
                    w(act, "turned", s + 1)
                    copy_result(0).then_inc(sems["ob_out"], 1)
                    w(act, "ob_out", s + 1)
                    act.dma_start(out_rows(s), ot[0][:].rearrange("p (t c) -> p t c", t=2)
                                  ).then_inc(sems["out_stored"], 16)
                    w(act, "out_stored", 16 * (s + 1))
                    w(act, "coef_ready", s + 1)

            def dve_general(dve):
                with dve.Fori(0, ST) as s:
                    w(dve, "om_ready", 16 * (s + 1))
                    positions(dve, s, 0, sems["pchain"], NPOS * s)
                    w(dve, "pchain", NPOS * (s + 1))
                    w(dve, "masked", s + 1)
                    nc.vector.tensor_tensor(coef[0][:], lo[:, 0], mask[0][:], ALU.mult).then_inc(sems["coef_ready"], 1)
                    w(dve, "coef_ready", s + 1)
                    nc.vector.memset(sums, 0.0).then_inc(sems["zeroed"], 1)
                    with dve.Fori(0, NWIN) as wy:
                        with dve.Fori(0, NWIN) as wx:
                            for hx in range(2):
                                t = ((s * NWIN + wy) * NWIN + wx) * 2 + hx
                                for d, win_no in enumerate((wy, wx)):
                                    centers = ctr_all[:, bass.ds(win_no, 1)].rearrange("p w a -> p (w a)")
                                    distances(nc.vector, 0, hx, 0, d, centers).then_inc(sems["dist_ready"], 1)
                                w(dve, "achain", 2 * (t + 1))
                                cap_weights(dve, 0, hx, 0, sems["capped"], 4 * t)
                                w(dve, "capped", 4 * (t + 1))
                                for half in range(2):
                                    n = 2 * t + half
                                    for g in range(GH):
                                        window_weights(0, half, g, 0).then_inc(sems["products"], 1)
                                    for i in range(NT):
                                        w(dve, "batched", 9 * n + i + 1)
                                        copy_batch("dve", 0, i, i % 3).then_inc(sems["copied"], 1)
                                    for v in range(3):
                                        w(dve, "sampled", 3 * n + v + 1)
                                        w(dve, "zeroed", s + 1)
                                        dst, src = samples(sums, hx, half, 3 * v, v)
                                        nc.vector.tensor_tensor(dst, src, dst, ALU.add).then_inc(sems["added"], 1)
                                    w(dve, "products", 4 * (n + 1))
                                    w(dve, "added", 3 * (n + 1))
                    nc.vector.tensor_copy(val[0][:], sums).then_inc(sems["val_hi"], 1)
                    w(dve, "val_hi", s + 1)
                    nc.vector.tensor_tensor(val[1][:], sums, val[0][:].bitcast(f32), ALU.subtract
                                            ).then_inc(sems["split"], 1)
                    w(dve, "split", s + 1)
                    w(dve, "finished", 2 * (s + 1))
                    w(dve, "r_ready", 16 * (s + 1))
                    nc.vector.tensor_tensor(res[0][:], res[0][:], rt[0][:], ALU.add).then_inc(sems["summed"], 1)

            def pe_general(pe):
                with pe.Fori(0, ST) as s:
                    with pe.Fori(0, WINDOWS) as i:
                        for hx in range(2):
                            t = s * (2 * WINDOWS) + 2 * i + hx
                            for half in range(2):
                                n = 2 * t + half
                                for i4 in range(NT):
                                    w(pe, "products", 4 * n + (4 * i4 + 3) // NK + 1)
                                    if i4 >= 3:
                                        w(pe, "copied", 9 * n + i4 - 2)
                                    transpose_batch(0, i4, i4 % 3).then_inc(sems["batched"], 1)
                                w(pe, "copied", 9 * (n + 1))
                                w(pe, "win_ready", 16 * WIN * (t + 1))
                                for v in range(3):
                                    for j in range(3 * v, min(3 * v + 3, BLK)):
                                        last = sample_block(0, 0, half, j, v)
                                    last.then_inc(sems["sampled"], 1)
                                w(pe, "added", 3 * (n + 1))
                    w(pe, "split", s + 1)
                    for half in range(CH):
                        for k in range(NK):
                            last = project(half, k)
                    last.then_inc(sems["projected"], 1)
                    w(pe, "summed", s + 1)
                    turn_result(0).then_inc(sems["turned"], 1)
                    w(pe, "ob_out", s + 1)

            return sp_general, pool_general, act_general, dve_general, pe_general

        fast_sp, fast_pool, fast_act, fast_dve, fast_pe = fast()
        gen_sp, gen_pool, gen_act, gen_dve, gen_pe = general()

        def choose(e, fast_path, general_path):
            beyond = e.value_load(flag[0:1, 0:1], min_val=0, max_val=1)
            with e.If(beyond == 0):
                fast_path(e)
            with e.Else():
                general_path(e)

        with nc.Block() as block:
            @block.sync
            def _(sp):
                choose(sp, fast_sp, gen_sp)

            @block.gpsimd
            def _(pool):
                choose(pool, fast_pool, gen_pool)

            @block.scalar
            def _(act):
                choose(act, fast_act, gen_act)

            @block.vector
            def _(dve):
                choose(dve, fast_dve, gen_dve)

            @block.tensor
            def _(pe):
                choose(pe, fast_pe, gen_pe)


def conv_preact(nc, x, coarse, attend_w, select_w, offset_w, om_w, om_b, dcn_w, dcn_b, ident, gmean, coords, out):
    cpad = nc.dram_tensor("cpad", [B, PADC, PADC, C], f32, kind="Internal").ap()
    om_d = nc.dram_tensor("om_d", [ST, 128, 2, NOM], f32, kind="Internal").ap()
    r_d = nc.dram_tensor("r_d", [B * SB, 128, CH, 512], f32, kind="Internal").ap()
    with nc.sbuf_tensor("flag", [1, 1], i32) as flag:
        with ExitStack() as ctx:
            wm = [ctx.enter_context(nc.sbuf_tensor(f"wm{q}", [128, 4, NK, NOM], f32r)) for q in range(2)]
            scale, shift = (ctx.enter_context(nc.sbuf_tensor(n, [128, CH, B], f32)) for n in ("scale", "shift"))
            statistics_and_weights(nc, x, attend_w, om_w, offset_w, ident, gmean, wm, scale, shift)
            offsets_and_calibration(nc, x, coarse, select_w, om_b, ident, cpad, wm, scale, shift, om_d, r_d, flag)
        sample_and_project(nc, cpad, om_d, r_d, dcn_w, dcn_b, ident, coords, flag, out)


_INS = ["x", "L0_conv_coarse", "L0_conv_attend_w", "L0_conv_select_w", "L0_conv_offset_w", "L0_conv_om_w",
        "L0_conv_om_b", "L0_conv_dcn_w", "L0_conv_dcn_b"]


def _constants():
    import numpy as np
    p = np.arange(128)
    j, r, c = p // 16, p // 4 % 4, p % 4
    block_row = np.arange(ST) % (H // 4)
    k, a, hx = np.arange(NK), np.arange(WIN), np.arange(2)
    base_y = 4 * block_row[None, :, None] + r[:, None, None] + k // 3 - 1
    base_x = 32 * hx[None, :, None] + (4 * j + c)[:, None, None] + k % 3 - 1
    centre = lambda n: 2 * n + 0.5
    ctr_y = np.broadcast_to(centre(2 * block_row[:, None] - PADLO + a), (128, ST, WIN))
    ctr_x = centre(2 * (BLK * hx[None, :, None] + j[:, None, None]) - PADLO + a)
    ctr_all = np.broadcast_to(centre(-1 + WIN * np.arange(NWIN)[:, None] + a), (128, NWIN, WIN))
    coords = np.concatenate([t.reshape(128, -1) for t in (base_y, ctr_y, base_x, ctr_x, ctr_all)], 1)
    return {"ident": np.eye(128, dtype=np.float32),
            "gmean": np.kron(np.eye(16), np.full((8, 8), 0.125)).astype(np.float32),
            "coords": coords.astype(np.float32)}


def kernel(**inputs):
    import numpy as np
    import concourse.bacc as bacc
    from concourse.bass_utils import run_bass_kernel_spmd

    nc = bacc.Bacc("TRN2", target_bir_lowering=False, num_devices=1)
    arrays, args = {}, []
    given = {name: np.ascontiguousarray(inputs[name]) for name in _INS} | _constants()
    for name, a in given.items():
        arrays[f"in_{name}"] = a
        args.append(nc.dram_tensor(f"in_{name}", a.shape, mybir.dt.from_np(a.dtype), kind="ExternalInput").ap())
    out = nc.dram_tensor("out_0", (B, H, W, C), f32, kind="ExternalOutput").ap()
    conv_preact(nc, *args, out)
    got = run_bass_kernel_spmd(nc, [arrays], core_ids=[0])
    return got.results[0]["out_0"]
```

```python
import concourse.bass as bass
from concourse import mybir
from contextlib import ExitStack

B, H, W, C = 4, 64, 64, 256
HC = H // 2
NG, NK = 8, 9
GK = NG * NK
NOM = 3 * GK
OMC = NOM // 2
CH = C // 128
HP = H + 2
CP = HC + 2
WIN = 10
WQ = WIN * WIN
LIMIT = 6.0
PADLO = 4
NWIN = 4
PADC = 43
SB = 8
NS = B * SB
ST = H * B // 4
BLK = 8
GN_EPS = 1e-5

f32 = mybir.dt.float32
f32r = mybir.dt.float32r
i32 = mybir.dt.int32
ACT = mybir.ActivationFunctionType
ALU = mybir.AluOpType
AX = mybir.AxisListType


NCOORD = ST * NK + ST * WIN + 2 * NK + 2 * WIN + NWIN * WIN
NT = 9
UNITS = 4
GH = NG // 2


def pad_rows(e, coarse, cpad, padded):
    hi = PADLO + HC
    for b in range(B):
        e.dma_start(cpad[b, PADLO:hi, PADLO:hi, :], coarse[b]).then_inc(padded, 16)
    for edge, rows in ((coarse[:, 0:1], cpad[:, 0:PADLO]), (coarse[:, HC - 1:HC], cpad[:, hi:PADC])):
        e.dma_start(rows[:, :, PADLO:hi, :].rearrange("b y x c -> b y (x c)"),
                    edge.rearrange("b y x c -> b y (x c)").broadcast_to([B, rows.shape[1], HC * C])).then_inc(padded, 16)


def pad_columns(e, cpad, rows_padded, padded):
    hi = PADLO + HC
    e.wait_ge(rows_padded, 16 * (B + 2))
    rows = cpad.rearrange("b y x c -> (b y) x c")
    for src, first, end in ((PADLO, 0, PADLO), (hi - 1, hi, PADC)):
        e.dma_start(rows[:, first:end, :], rows[:, src:src + 1, :].broadcast_to([B * PADC, end - first, C])
                    ).then_inc(padded, 16)


def statistics_and_weights(nc, x, attend_w, om_w, offset_w, ident_d, gmean_d, wf, wc, scale, shift):
    NT = 4
    NBUF = 4
    with ExitStack() as ctx:
        sb = lambda name, shape, dt=f32: ctx.enter_context(nc.sbuf_tensor(name, shape, dt))
        sem = lambda name: ctx.enter_context(nc.semaphore(name))
        ident = sb("ident0", [128, 128])
        gmean = sb("gmean", [128, 128])
        att = sb("att", [128, CH, C])
        ow = sb("ow", [128, NT, 512])
        owT = sb("owT", [128, NT, NT, 128])
        omw = sb("omw", [128, NK, NT, NOM])
        mid = sb("mid", [128, 2, 3, NT, NOM])
        chunk = [sb(f"chunk{i}", [128, 4, C]) for i in range(NBUF)]
        st = sb("st", [128, CH, B, SB, 6])
        mv = sb("mv", [128, CH, B, 2])
        dev, dev2, var, sd, rstd, mfine, gate, mg = (
            sb(n, [128, CH, B]) for n in ("dev", "dev2", "var", "sd", "rstd", "mfine", "gate", "mg"))
        bank = lambda name: ctx.enter_context(nc.psum_tensor(name, [128, 512], f32))
        wps = [bank(f"wps{i}") for i in range(2)]
        xps = [bank(f"xps{i}") for i in range(4)]
        small = bank("small")
        consts, w_loaded, omw_loaded = sem("consts"), sem("w_loaded"), sem("omw_loaded")
        x_loaded = [sem(f"x_loaded{i}") for i in range(NBUF)]
        turned, turned_out, merged, merged_out, w_hi = (
            sem(n) for n in ("turned", "turned_out", "merged", "merged_out", "w_hi"))
        row_sums = sem("row_sums")
        x_turned, counted = sem("x_turned"), sem("counted")
        chain, gm_done, gv_done, sd_done, att_done, gate_done = (
            sem(n) for n in ("chain", "gm_done", "gv_done", "sd_done", "att_done", "gate_done"))
        block = ctx.enter_context(nc.Block())
        x_v = x.rearrange("b h w c -> (b h w) c").rearrange("(n t p) c -> n p t c", p=128, t=4)
        flat = lambda t: t[:].rearrange("p h b -> p (h b)")
        products = [(CH + h, omw[:, 3 * dy + dx], 0.5, [w_[:, h, dy, dx] for w_ in wc])
                    for h in range(CH) for dy in range(3) for dx in range(3)]
        products += [(h, omw[:, 6 * (j // 3) + dx], 1.0, [w_[:, h, j, dx] for w_ in wf])
                     for j in (0, 3) for h in range(CH) for dx in range(3)]
        FIRST_MID = len(products)
        products += [(h, mid[:, j - 1, dx], 0.5, [w_[:, h, j, dx] for w_ in wf])
                     for j in (1, 2) for h in range(CH) for dx in range(3)]
        PER = -(-len(products) // (NS // NBUF - 1))

        @block.sync
        def _(sp):
            sp.dma_start(ident[:], ident_d).then_inc(w_loaded, 16)
            sp.dma_start(ow[:], offset_w.rearrange("(i p) m -> p i m", p=128)).then_inc(w_loaded, 16)
            for n in range(NBUF):
                sp.dma_start(chunk[n][:], x_v[n]).then_inc(x_loaded[n], 16)
            sp.dma_start(omw[:], om_w.rearrange("u v (m p) o -> p (u v) m o", p=128)).then_inc(omw_loaded, 16)
            sp.dma_start(gmean[:], gmean_d).then_inc(consts, 16)
            sp.dma_start(att[:], attend_w.rearrange("(h p) f -> p h f", p=128)).then_inc(consts, 16)
            with sp.Fori(1, NS // NBUF) as m:
                for i in range(NBUF):
                    sp.wait_ge(x_turned, 2 * (NBUF * m + i - NBUF + 1))
                    sp.dma_start(chunk[i][:], x_v[bass.ds(NBUF * m + i, 1)].rearrange("o p t c -> (o p) t c")
                                 ).then_inc(x_loaded[i], 16)

        def turn_weights(pe):
            pe.wait_ge(w_loaded, 32)
            for m in range(NT):
                if m >= 2:
                    pe.wait_ge(turned_out, m - 1)
                for i in range(NT):
                    last = nc.tensor.transpose(wps[m % 2][:, 128 * i:128 * i + 128],
                                               ow[:, i, 128 * m:128 * m + 128], ident[:])
                last.then_inc(turned, 1)

        def merge(pe, n):
            pe.wait_ge(merged_out, n - 1) if n >= 2 else pe.wait_ge(turned_out, NT)
            if n == FIRST_MID:
                pe.wait_ge(row_sums, 3)
            rows, taps, _, _ = products[n]
            for m in range(NT):
                last = nc.tensor.matmul(wps[n % 2][:, 0:NOM], owT[:, m, rows, :], taps[:, m, :],
                                        start=(m == 0), stop=(m == NT - 1))
            last.then_inc(merged, 1)

        @block.tensor
        def _(pe):
            def turn_x(g):
                pe.wait_ge(x_loaded[g % NBUF], 16 * (g // NBUF + 1))
                for h in range(CH):
                    if g >= 2:
                        pe.wait_ge(counted, 2 * (g - 2) + h + 1)
                    for t in range(4):
                        last = nc.tensor.transpose(xps[2 * (g % 2) + h][:, 128 * t:128 * t + 128],
                                                   chunk[g % NBUF][:, t, 128 * h:128 * h + 128], ident[:])
                    last.then_inc(x_turned, 1)
            turn_weights(pe)
            for g in range(NBUF):
                turn_x(g)
            pe.wait_ge(omw_loaded, 16)
            for m in range(1, NS // NBUF):
                for n in range(PER * (m - 1), min(PER * m, len(products))):
                    merge(pe, n)
                for i in range(NBUF):
                    turn_x(NBUF * m + i)
            pe.wait_ge(consts, 32)
            pe.wait_ge(chain, 1)
            nc.tensor.matmul(small[:, 0:8], gmean[:], mv[:, :, :, 0].rearrange("p h b -> p (h b)"),
                             start=True, stop=True).then_inc(gm_done, 1)
            pe.wait_ge(chain, 5)
            nc.tensor.matmul(small[:, 8:16], gmean[:], flat(var), start=True, stop=True).then_inc(gv_done, 1)
            pe.wait_ge(chain, 8)
            for fo in range(CH):
                for h in range(CH):
                    last = nc.tensor.matmul(small[:, 16 + 4 * fo:20 + 4 * fo], att[:, h, 128 * fo:128 * fo + 128],
                                            mfine[:, h, :], start=(h == 0), stop=(h == CH - 1))
            last.then_inc(att_done, 1)

        @block.scalar
        def _(act):
            act.wait_ge(chain, 6)
            nc.scalar.activation(sd[:], var[:], ACT.Sqrt).then_inc(sd_done, 1)
            act.wait_ge(att_done, 1)
            nc.scalar.activation(flat(gate), small[:, 16:24], ACT.Sigmoid).then_inc(gate_done, 1)

        @block.gpsimd
        def _(pool):
            row = lambda dy: omw[:, 3 * dy:3 * dy + 3]
            pool.wait_ge(omw_loaded, 16)
            nc.gpsimd.tensor_tensor(mid[:, 1], row(0), row(2), ALU.add).then_inc(row_sums, 1)
            pool.wait_ge(row_sums, 1)
            nc.gpsimd.tensor_tensor(mid[:, 0], mid[:, 1], row(1), ALU.add).then_inc(row_sums, 1)
            pool.wait_ge(row_sums, 2)
            nc.gpsimd.tensor_tensor(mid[:, 1], mid[:, 1], row(1), ALU.subtract).then_inc(row_sums, 1)

        @block.vector
        def _(dve):
            def count(g):
                for h in range(CH):
                    dve.wait_ge(x_turned, 2 * g + h + 1)
                    nc.vector.bn_stats(st[:, h, g // SB, g % SB, :], xps[2 * (g % 2) + h][:]).then_inc(counted, 1)

            def split(n):
                _, _, factor, parts = products[n]
                dve.wait_ge(merged, n + 1)
                views = [(lambda t: t[:, 0:2 * GK].rearrange("p (t q) -> p t q", t=2),
                          wps[n % 2][:, 0:2 * GK].rearrange("p (q t) -> p t q", t=2)),
                         (lambda t: t[:, 2 * GK:NOM], wps[n % 2][:, 2 * GK:NOM])]
                for dst, src in views:
                    last = nc.vector.tensor_scalar(dst(parts[0]), src, factor, None, ALU.mult)
                last.then_inc(w_hi, 1)
                dve.wait_ge(w_hi, n + 1)
                for dst, src in views:
                    last = nc.vector.scalar_tensor_tensor(out=dst(parts[1]), in0=src, scalar=factor, in1=dst(parts[0]).bitcast(f32),
                                                          op0=ALU.mult, op1=ALU.subtract)
                last.then_inc(merged_out, 1)

            for m in range(NT):
                dve.wait_ge(turned, m + 1)
                nc.vector.tensor_copy(owT[:, m, :, :], wps[m % 2][:].rearrange("p (i c) -> p i c", i=NT)
                                      ).then_inc(turned_out, 1)
            for g in range(NBUF):
                count(g)
            for m in range(1, NS // NBUF):
                for n in range(PER * (m - 1), min(PER * m, len(products))):
                    split(n)
                for i in range(NBUF):
                    count(NBUF * m + i)

            def link(ins, n):
                ins.then_inc(chain, 1)
                dve.wait_ge(chain, n)
            dve.wait_ge(counted, 2 * NS)
            for h in range(CH):
                for b in range(B):
                    last = nc.vector.bn_aggr(mv[:, h, b, :], st[:, h, b, :, :].rearrange("p n k -> p (n k)"))
            link(last, 1)
            dve.wait_ge(gm_done, 1)
            link(nc.vector.tensor_copy(flat(mg), small[:, 0:8]), 2)
            link(nc.vector.tensor_tensor(dev[:], mv[:, :, :, 0], mg[:], ALU.subtract), 3)
            link(nc.vector.tensor_tensor(dev2[:], dev[:], dev[:], ALU.mult), 4)
            link(nc.vector.tensor_tensor(var[:], dev2[:], mv[:, :, :, 1], ALU.add), 5)
            dve.wait_ge(gv_done, 1)
            link(nc.vector.tensor_scalar(flat(var), small[:, 8:16], GN_EPS, None, ALU.add), 6)
            dve.wait_ge(sd_done, 1)
            link(nc.vector.reciprocal(rstd[:], sd[:]), 7)
            link(nc.vector.tensor_tensor(mfine[:], dev[:], rstd[:], ALU.mult), 8)
            dve.wait_ge(gate_done, 1)
            link(nc.vector.scalar_tensor_tensor(out=flat(scale), in0=flat(gate), scalar=1.0, in1=flat(rstd),
                                                op0=ALU.add, op1=ALU.mult), 9)
            link(nc.vector.scalar_tensor_tensor(out=flat(shift), in0=flat(mg), scalar=-1.0, in1=flat(scale),
                                                op0=ALU.mult, op1=ALU.mult), 10)


def offsets_and_calibration(nc, x, coarse, select_w, om_b, ident_d, cpad, wf, wc, scale, shift, om_d, r_d, flag):
    NRING, TERMS = 16, 5
    with ExitStack() as ctx:
        sb = lambda name, shape, dt=f32: ctx.enter_context(nc.sbuf_tensor(name, shape, dt))
        sem = lambda name: ctx.enter_context(nc.semaphore(name))
        ident = sb("ident1", [128, 128])
        sel = sb("sel", [128, CH, C])
        omb = sb("omb", [OMC, 2])
        omb4 = sb("omb4", [OMC, 2])
        chunk = [sb(f"xchunk{i}", [128, 4, C]) for i in range(2)]
        xs = sb("xs", [128, CH, 512])
        xn = sb("xn", [128, CH, 512])
        r = sb("r", [128, CH, 512])
        slab = [sb(f"slab{i}", [128, CH, 10, HP]) for i in range(2)]
        mix = [sb(f"mix{i}", [128, CH, 4, HP]) for i in range(2)]
        fine = [[sb(f"fine{i}_{q}", [128, 4, CH, 4, HP], f32r) for q in range(2)] for i in range(2)]
        cs = [sb(f"cs{i}", [128, C]) for i in range(2)]
        cT = sb("cT", [128, CH, 4, CP])
        ux = sb("ux", [128, CH, 4, W])
        up = [[sb(f"up{i}_{q}", [128, CH, 4, HP], f32r) for q in range(2)] for i in range(2)]
        z = sb("z", [OMC, 3, 2, NRING, W])
        part = sb("part", [OMC, 2, 2, 4, W])
        omT = [sb(f"omT{i}", [OMC, 2, 2, 256]) for i in range(2)]
        oms = [sb(f"oms{i}", [128, 4, NOM]) for i in range(2)]
        ext = sb("ext", [128, 2 * NS])
        far = sb("far", [128, 2])
        row = sb("row", [2, 128])
        top = sb("top", [2, 1])
        topr = sb("topr", [1, 2])
        worst = sb("worst", [1, 1])
        bank = lambda name: ctx.enter_context(nc.psum_tensor(name, [128, 512], f32))
        conv, zb, cal, tb = ([bank(f"{n}{i}") for i in range(2)] for n in ("conv", "zb", "cal", "turned"))
        names = ("consts cleared quartered rows_padded padded x_turned xs_done xn_done cal_done slab_done r_done "
                 "halo_done mixed fine_hi fine_lo c_turned cT_done cT_edged ux_near ux_done up_hi_done up_done z_done "
                 "z_out part_term edged conv_done conv_added omT_done o_turned oms_done ext_done flag_T flag_T2 "
                 "flagged").split()
        s = {n: sem(n) for n in names}
        x_ready, c_ready, om_stored = ([sem(f"{n}{i}") for i in range(2)] for n in ("x_ready", "c_ready", "om_stored"))
        r_stored = sem("r_stored")
        x_v = x.rearrange("b h w c -> (b h w) c").rearrange("(n t p) c -> n p t c", p=128, t=4)
        c_v = coarse.rearrange("b h w c -> (b h w) c").rearrange("(n p) c -> n p c", p=128)

        def product(j):
            return conv[j // 2][0:OMC, 256 * (j % 2):256 * (j % 2) + 256]

        def w(e, sm, v):
            if not isinstance(v, int) or v > 0:
                e.wait_ge(s[sm] if isinstance(sm, str) else sm, v)

        def known(g):
            return not isinstance(g, int) or 0 <= g < NS

        def upto(g):
            return min(g, NS) if isinstance(g, int) else g

        def loop(e, batch, between=lambda: None):
            batch(0)
            between()
            with e.Fori(1, B - 1) as b:
                batch(b)
            batch(B - 1)

        block = ctx.enter_context(nc.Block())

        @block.sync
        def _(sp):
            def load(g, i):
                sp.dma_start(chunk[i][:], x_v[bass.ds(g, 1)].rearrange("o p t c -> (o p) t c")).then_inc(x_ready[i], 16)
                sp.dma_start(cs[i][:], c_v[bass.ds(g, 1)].rearrange("o p c -> (o p) c")).then_inc(c_ready[i], 16)
            load(0, 0)
            load(1, 1)
            sp.dma_start(ident[:], ident_d).then_inc(s["consts"], 16)
            sp.dma_start(sel[:], select_w.rearrange("(h p) f -> p h f", p=128)).then_inc(s["consts"], 16)
            yx = om_b[0:2 * GK].rearrange("(q t) -> q t", t=2)
            nx = OMC - GK
            with nc.allow_non_contiguous_dma(reason="216 bias values, once"):
                sp.dma_start(omb[0:GK, 0:1], yx[:, 0:1]).then_inc(s["consts"], 16)
                sp.dma_start(omb[GK:OMC, 0:1], yx[0:nx, 1:2]).then_inc(s["consts"], 16)
                sp.dma_start(omb[0:GK - nx, 1:2], yx[nx:GK, 1:2]).then_inc(s["consts"], 16)
                sp.dma_start(omb[GK - nx:OMC, 1:2], om_b[2 * GK:NOM].rearrange("(q t) -> q t", t=1)
                             ).then_inc(s["consts"], 16)

            def batch(b):
                for n in range(SB):
                    g = b * SB + n
                    if known(g + 2):
                        w(sp, "x_turned", 2 * (g + 1))
                        w(sp, "c_turned", g + 1)
                        load(g + 2, n % 2)
            loop(sp, batch)

        @block.tensor
        def _(pe):
            def turn_x(g, i):
                if known(g):
                    pe.wait_ge(x_ready[i % 2], 8 * (g - i % 2) + 16)
                    for h in range(CH):
                        w(pe, "r_done", 2 * (g - 1) + h + 1)
                        for t in range(4):
                            last = nc.tensor.transpose(cal[h][:, 128 * t:128 * t + 128],
                                                       chunk[i % 2][:, t, 128 * h:128 * h + 128], ident[:])
                        last.then_inc(s["x_turned"], 1)

            def turn_coarse(g, i):
                if known(g):
                    pe.wait_ge(c_ready[i % 2], 8 * (g - i % 2) + 16)
                    w(pe, "cT_done", g)
                    w(pe, "oms_done", 2 * (g - 5) + 1)
                    for h in range(CH):
                        last = nc.tensor.transpose(tb[0][:, 128 * h:128 * h + 128],
                                                   cs[i % 2][:, 128 * h:128 * h + 128], ident[:])
                    last.then_inc(s["c_turned"], 1)

            def calibrate(g, i):
                if known(g):
                    w(pe, "xn_done", g + 1)
                    for fo in range(CH):
                        for h in range(CH):
                            last = nc.tensor.matmul(cal[fo][:], sel[:, h, 128 * fo:128 * fo + 128], xn[:, h, :],
                                                    start=(h == 0), stop=(h == CH - 1))
                        last.then_inc(s["cal_done"], 1)

            PARTS = ((0, 0), (0, 1), (1, 0))

            def coarse_products(g, i, o):
                if known(g):
                    w(pe, "up_done", g + 1)
                    for dy in range(3):
                        q = 3 * o + dy
                        w(pe, "z_out", 6 * g + q - 1)
                        k = 0
                        for wp, ip in PARTS:
                            for h in range(CH):
                                for dx in range(3):
                                    last = nc.tensor.matmul(
                                        zb[q % 2][0:OMC, 0:256], wc[wp][:, h, dy, dx, OMC * o:OMC * (o + 1)],
                                        up[i % 2][ip][:, h, :, dx:dx + W], start=(k == 0), stop=(k == 17))
                                    k += 1
                        last.then_inc(s["z_done"], 1)

            def turn_offsets(g, i):
                if known(g):
                    w(pe, "omT_done", 2 * (g + 1))
                    w(pe, "cT_done", upto(g + 5))
                    w(pe, "oms_done", 2 * g)
                    for hy in range(2):
                        for hx in range(2):
                            for o in range(2):
                                last = nc.tensor.transpose(tb[hy][:, NOM * hx + OMC * o:NOM * hx + OMC * (o + 1)],
                                                           omT[i % 2][:, o, hy, 128 * hx:128 * hx + 128],
                                                           ident[0:OMC, 0:OMC])
                        last.then_inc(s["o_turned"], 1)

            def convolve(g, i, o):
                w(pe, "fine_lo", 4 * (g + 1))
                w(pe, "omT_done", 2 * g + o)
                for j in range(4):
                    k = 0
                    for wp, ip in PARTS:
                        for h in range(CH):
                            for dx in range(3):
                                last = nc.tensor.matmul(product(j), wf[wp][:, h, j, dx, OMC * o:OMC * (o + 1)],
                                                        fine[i % 2][ip][:, j, h, :, dx:dx + W],
                                                        start=(k == 0), stop=(k == 17))
                                k += 1
                last.then_inc(s["conv_done"], 1)

            pe.wait_ge(s["consts"], 16 * 6)
            pe.wait_ge(s["cleared"], 6)
            turn_x(0, 0)
            turn_coarse(0, 0)
            calibrate(0, 0)
            turn_x(1, 1)
            turn_coarse(1, 1)
            coarse_products(0, 0, 0)
            calibrate(1, 1)
            coarse_products(0, 0, 1)
            turn_x(2, 2)
            turn_coarse(2, 2)
            for o in range(2):
                coarse_products(1, 1, o)

            def batch(b):
                for n in range(SB):
                    g = b * SB + n
                    turn_coarse(g + 3, n + 3)
                    calibrate(g + 2, n + 2)
                    convolve(g, n, 0)
                    coarse_products(g + 2, n + 2, 0)
                    turn_x(g + 3, n + 3)
                    turn_offsets(g - 1, n - 1)
                    convolve(g, n, 1)
                    coarse_products(g + 2, n + 2, 1)
            loop(pe, batch)
            turn_offsets(NS - 1, SB - 1)
            pe.wait_ge(s["flagged"], 3)
            nc.tensor.transpose(tb[0][0:2, 0:128], far[:], ident[:]).then_inc(s["flag_T"], 1)
            pe.wait_ge(s["flagged"], 5)
            nc.tensor.transpose(tb[1][0:1, 0:2], top[:], ident[0:2, 0:2]).then_inc(s["flag_T2"], 1)

        @block.scalar
        def _(act):
            act.wait_ge(s["consts"], 16 * 6)
            nc.scalar.mul(omb4[:], omb[:], 0.25).then_inc(s["quartered"], 1)

            def keep_x(g, i):
                if known(g):
                    for h in range(CH):
                        w(act, "x_turned", 2 * g + h + 1)
                        w(act, "r_done", 2 * (g - 1) + h + 1)
                        nc.scalar.copy(xs[:, h, :], cal[h][:]).then_inc(s["xs_done"], 1)

            def keep_slab(g, i):
                if known(g):
                    w(act, "mixed", 4 * (g - 1))
                    for fo in range(CH):
                        w(act, "cal_done", 2 * g + fo + 1)
                        nc.scalar.copy(slab[i % 2][:, fo, 1:9, 1:W + 1],
                                       cal[fo][:].rearrange("p (y x) -> p y x", y=8)).then_inc(s["slab_done"], 1)

            def keep_fine(g, i):
                if known(g):
                    w(act, "conv_done", 2 * (g - 1))
                    for j in range(4):
                        w(act, "mixed", 4 * g + j + 1)
                        nc.scalar.copy(fine[i % 2][0][:, j], mix[j % 2][:]).then_inc(s["fine_hi"], 1)

            def keep_z(g, i, o):
                if known(g):
                    w(act, "part_term", TERMS * (g - 2))
                    for dy in range(3):
                        q = 3 * o + dy
                        w(act, "z_done", 6 * g + q + 1)
                        dst = z[:, dy, o, 4 * (i % 4):4 * (i % 4) + 4, :].rearrange("p y x -> p (y x)")
                        if dy == 1:
                            ins = nc.scalar.activation(dst, zb[q % 2][0:OMC, 0:256], ACT.Identity, bias=omb4[:, o:o + 1])
                        else:
                            ins = nc.scalar.copy(dst, zb[q % 2][0:OMC, 0:256])
                        ins.then_inc(s["z_out"], 1)

            act.wait_ge(s["cleared"], 6)
            act.wait_ge(s["quartered"], 1)
            keep_x(0, 0)
            keep_slab(0, 0)
            keep_x(1, 1)
            keep_z(0, 0, 0)
            keep_slab(1, 1)
            keep_z(0, 0, 1)
            keep_x(2, 2)
            pad_rows(act, coarse, cpad, s["rows_padded"])
            keep_fine(0, 0)
            for o in range(2):
                keep_z(1, 1, o)

            def batch(b):
                for n in range(SB):
                    g = b * SB + n
                    keep_slab(g + 2, n + 2)
                    keep_z(g + 2, n + 2, 0)
                    keep_x(g + 3, n + 3)
                    keep_fine(g + 1, n + 1)
                    keep_z(g + 2, n + 2, 1)
            loop(act, batch, lambda: pad_columns(act, cpad, s["rows_padded"], s["padded"]))
            act.wait_ge(s["padded"], 16 * 2)

        @block.gpsimd
        def _(pool):
            for t in slab + [t for pair in up for t in pair]:
                nc.gpsimd.memset(t[:].bitcast(f32), 0.0).then_inc(s["cleared"], 1)

            def store_r(g, i):
                if known(g):
                    w(pool, "r_done", 2 * (g + 1))
                    pool.dma_start(r_d[bass.ds(g, 1)].rearrange("o p h c -> (o p) h c"), r[:]).then_inc(r_stored, 16)

            def store_offsets(g, i):
                if known(g):
                    w(pool, "oms_done", 2 * (g + 1))
                    pool.dma_start(om_d[bass.ds(2 * g, 2)].rearrange("y p x o -> p y (x o)"),
                                   oms[i % 2][:].rearrange("p (y x) o -> p y (x o)", y=2)).then_inc(om_stored[i % 2], 16)

            store_r(0, 0)
            store_r(1, 1)

            def batch(b):
                for n in range(SB):
                    g = b * SB + n
                    store_r(g + 2, n + 2)
                    store_offsets(g - 1, n - 1)
            loop(pool, batch)
            store_offsets(NS - 1, SB - 1)
            pool.wait_ge(r_stored, 16 * NS)
            for i in range(2):
                pool.wait_ge(om_stored[i], 16 * NS // 2)

        @block.vector
        def _(dve):
            def normalise(g, i, b):
                if known(g):
                    w(dve, "xs_done", 2 * (g + 1))
                    for h in range(CH):
                        last = nc.vector.tensor_scalar(xn[:, h, :], xs[:, h, :], scale[:, h, bass.ds(b, 1)],
                                                       shift[:, h, bass.ds(b, 1)], ALU.mult, ALU.add)
                    last.then_inc(s["xn_done"], 1)

            def upsample_columns(g, i):
                if known(g):
                    w(dve, "c_turned", g + 1)
                    w(dve, "ux_done", g)
                    nc.vector.tensor_copy(cT[:, :, :, 1:HC + 1],
                                          tb[0][:, 0:256].rearrange("p (h y x) -> p h y x", h=CH, y=4)
                                          ).then_inc(s["cT_done"], 1)
                    w(dve, "cT_done", g + 1)
                    rows = cT[:].rearrange("p h y x -> p (h y) x")
                    nc.vector.tensor_copy(rows[:, :, 0:1], rows[:, :, 1:2])
                    nc.vector.tensor_copy(rows[:, :, CP - 1:CP], rows[:, :, CP - 2:CP - 1]).then_inc(s["cT_edged"], 1)
                    uxv = ux[:].rearrange("p h y (x t) -> p (h y) t x", t=2)
                    w(dve, "up_done", g)
                    for t in range(2):
                        last = nc.vector.tensor_scalar(uxv[:, :, t, :], rows[:, :, 1:HC + 1], 0.75, None, ALU.mult)
                    last.then_inc(s["ux_near"], 1)
                    w(dve, "ux_near", g + 1)
                    w(dve, "cT_edged", g + 1)
                    for t in range(2):
                        last = nc.vector.scalar_tensor_tensor(out=uxv[:, :, t, :], in0=rows[:, :, 2 * t:2 * t + HC], scalar=0.25,
                                                              in1=uxv[:, :, t, :], op0=ALU.mult, op1=ALU.add)
                    last.then_inc(s["ux_done"], 1)
                    w(dve, "ux_done", g + 1)
                    w(dve, "z_done", 6 * (g - 1))
                    inner = lambda t: t[:].rearrange("p h y x -> p (h y) x")[:, :, 1:W + 1]
                    hi, lo = up[i % 2]
                    src = ux[:].rearrange("p h y x -> p (h y) x")
                    nc.vector.tensor_copy(inner(hi), src).then_inc(s["up_hi_done"], 1)
                    w(dve, "up_hi_done", g + 1)
                    nc.vector.tensor_tensor(inner(lo), src, inner(hi).bitcast(f32), ALU.subtract).then_inc(s["up_done"], 1)

            def add_x(g, i):
                if known(g):
                    w(dve, r_stored, 16 * g)
                    for fo in range(CH):
                        w(dve, "slab_done", 2 * g + fo + 1)
                        nc.vector.tensor_tensor(r[:, fo, :], cal[fo][:], xs[:, fo, :], ALU.add).then_inc(s["r_done"], 1)

            def halo(g, i):
                if known(g):
                    n = i % SB
                    own, before = slab[i % 2], slab[(i - 1) % 2]
                    if n == 0:
                        last = nc.vector.memset(own[:, :, 0, :], 0.0)
                    else:
                        nc.vector.tensor_copy(before[:, :, 9, :], own[:, :, 1, :])
                        last = nc.vector.tensor_copy(own[:, :, 0, :], before[:, :, 8, :])
                    if n == SB - 1:
                        last = nc.vector.memset(own[:, :, 9, :], 0.0)
                    last.then_inc(s["halo_done"], 1)

            def mix_rows(g, i):
                if known(g):
                    w(dve, "halo_done", upto(g + 2))
                    d = lambda k: slab[i % 2][:, :, k:k + 7:2, :]
                    operands = ((0, ALU.subtract, 2), (1, ALU.add, 2), (2, ALU.subtract, 1), (1, ALU.subtract, 3))

                    def second_part(j):
                        w(dve, "fine_hi", 4 * g + j + 1)
                        nc.vector.tensor_tensor(fine[i % 2][1][:, j], mix[j % 2][:], fine[i % 2][0][:, j].bitcast(f32),
                                                ALU.subtract).then_inc(s["fine_lo"], 1)
                    for j, (a, op, b2) in enumerate(operands):
                        w(dve, "fine_lo", 4 * g + j - 1)
                        nc.vector.tensor_tensor(mix[j % 2][:], d(a), d(b2), op).then_inc(s["mixed"], 1)
                        if j > 0:
                            second_part(j - 1)
                    second_part(3)

            def rows_before(n):
                p = 4 * n % NRING
                return ((0, p, 1), (1, p, 3)) if n == 0 else ((0, NRING - 1, 1), (1, 0, 3)) if p == 0 else ((0, p - 1, 4),)

            def rows_after(n):
                p = 4 * n % NRING
                return ((0, p + 1, 3), (3, p + 3, 1)) if n == SB - 1 else \
                    ((0, p + 1, 3), (3, 0, 1)) if p == NRING - 4 else ((0, p + 1, 4),)

            def upsample_rows(g, n):
                here, before, after = ((0, 4 * n % NRING, 4),), rows_before(n), rows_after(n)
                zr = lambda dy, at, k: z[:, dy, :, at:at + k, :].rearrange("p o y x -> p o (y x)")
                pr = lambda t, at, k: part[:, t, :, at:at + k, :].rearrange("p o y x -> p o (y x)")
                w(dve, "z_out", 6 * upto(g + 2))
                w(dve, "omT_done", 2 * g)
                terms = (((1, 3.0, here), (1, 3.0, here)),
                         ((2, 3.0, here), (0, 3.0, here)),
                         ((0, 3.0, before), (0, 1.0, before)),
                         ((1, 1.0, before), (1, 1.0, after)),
                         ((2, 1.0, after), (2, 3.0, after)))
                for k, pair in enumerate(terms):
                    w(dve, "part_term", TERMS * g + k)
                    for t, (dy, factor, rows) in enumerate(pair):
                        for at, place, m in rows:
                            add_to = pr(t, at, m) if k > 0 else zr((0, 2)[t], place, m)
                            last = nc.vector.scalar_tensor_tensor(out=pr(t, at, m), in0=zr(dy, place, m), scalar=factor,
                                                                  in1=add_to, op0=ALU.mult, op1=ALU.add)
                    last.then_inc(s["part_term"], 1)
                w(dve, "part_term", TERMS * (g + 1))
                if n in (0, SB - 1):
                    t, dy, at, place = (0, 0, 0, 0) if n == 0 else (1, 2, 3, NRING - 1)
                    nc.vector.scalar_tensor_tensor(out=pr(t, at, 1), in0=zr(dy, place, 1), scalar=-4.0, in1=pr(t, at, 1),
                                                   op0=ALU.mult, op1=ALU.add).then_inc(s["edged"], 1)

            def offsets_out(g, i):
                if known(g):
                    w(dve, om_stored[i % 2], 8 * (g - i % 2))
                    for hy in range(2):
                        w(dve, "o_turned", 2 * g + hy + 1)
                        nc.vector.tensor_copy(oms[i % 2][:, 2 * hy:2 * hy + 2, :],
                                              tb[hy][:, 0:2 * NOM].rearrange("p (x o) -> p x o", x=2)
                                              ).then_inc(s["oms_done"], 1)
                    w(dve, "oms_done", 2 * (g + 1))
                    for k, op in enumerate((ALU.max, ALU.min)):
                        nc.vector.tensor_reduce(ext[:, bass.ds(g + k * NS, 1)], oms[i % 2][:, :, 0:2 * GK], axis=AX.XY, op=op
                                                ).then_inc(s["ext_done"], 1)

            def add_products(b, n, o):
                g = b * SB + n
                even, odd = (part[:, t, o].rearrange("p y x -> p (y x)") for t in range(2))
                w(dve, "conv_done", 2 * g + o + 1)
                w(dve, "part_term", TERMS * (g + 1))
                if n in (0, SB - 1):
                    w(dve, "edged", 2 * b + (1 if n == 0 else 2))
                nc.vector.tensor_tensor(even, even, product(0), ALU.add)
                nc.vector.tensor_tensor(odd, odd, product(1), ALU.add).then_inc(s["conv_added"], 1)
                w(dve, "conv_added", 4 * g + 2 * o + 1)
                nc.vector.tensor_tensor(even, even, product(1), ALU.add)
                nc.vector.tensor_tensor(odd, odd, product(2), ALU.subtract).then_inc(s["conv_added"], 1)
                w(dve, "conv_added", 4 * g + 2 * o + 2)
                w(dve, "o_turned", 2 * (g - 1))
                for hy in range(2):
                    for t, j, op in ((0, 2, ALU.add), (1, 3, ALU.subtract)):
                        last = nc.vector.tensor_tensor(
                            omT[n % 2][:, o, hy, :].rearrange("p (j a t c) -> p t a j c", a=2, t=2, c=4)[:, t],
                            part[:, t, o, 2 * hy:2 * hy + 2, :].rearrange("p a (j c) -> p a j c", c=4),
                            product(j)[:, 128 * hy:128 * hy + 128].rearrange("p (a j c) -> p a j c", a=2, c=4), op)
                last.then_inc(s["omT_done"], 1)

            dve.wait_ge(s["cleared"], 6)
            for g in range(2):
                normalise(g, g, 0)
                upsample_columns(g, g)
                add_x(g, g)
                halo(g, g)
            normalise(2, 2, 0)
            mix_rows(0, 0)
            upsample_columns(2, 2)

            def batch(b):
                for n in range(SB):
                    g = b * SB + n
                    upsample_rows(g, n)
                    upsample_columns(g + 3, n + 3)
                    add_x(g + 2, n + 2)
                    halo(g + 2, n + 2)
                    add_products(b, n, 0)
                    mix_rows(g + 1, n + 1)
                    normalise(g + 3, n + 3, b + (n + 3) // SB)
                    offsets_out(g - 1, n - 1)
                    add_products(b, n, 1)
            loop(dve, batch)
            offsets_out(NS - 1, SB - 1)

            dve.wait_ge(s["ext_done"], 2 * NS)
            nc.vector.tensor_reduce(far[:, 0:1], ext[:, 0:NS], axis=AX.X, op=ALU.max).then_inc(s["flagged"], 1)
            nc.vector.tensor_reduce(far[:, 1:2], ext[:, NS:], axis=AX.X, op=ALU.min).then_inc(s["flagged"], 1)
            dve.wait_ge(s["flagged"], 2)
            nc.vector.tensor_scalar(far[:, 1:2], far[:, 1:2], -1.0, None, ALU.mult).then_inc(s["flagged"], 1)
            dve.wait_ge(s["flag_T"], 1)
            nc.vector.tensor_copy(row[:], tb[0][0:2, 0:128]).then_inc(s["flagged"], 1)
            dve.wait_ge(s["flagged"], 4)
            nc.vector.tensor_reduce(top[:], row[:], axis=AX.X, op=ALU.max).then_inc(s["flagged"], 1)
            dve.wait_ge(s["flag_T2"], 1)
            nc.vector.tensor_copy(topr[:], tb[1][0:1, 0:2]).then_inc(s["flagged"], 1)
            dve.wait_ge(s["flagged"], 6)
            nc.vector.tensor_reduce(worst[:], topr[:], axis=AX.X, op=ALU.max).then_inc(s["flagged"], 1)
            dve.wait_ge(s["flagged"], 7)
            nc.vector.tensor_scalar(flag[:], worst[:], LIMIT, None, ALU.is_gt).then_inc(s["flagged"], 1)


def sample_and_project(nc, cpad, om_d, r_d, dcn_w, dcn_b, ident_d, coords_d, flag, out):
    ctx = ExitStack()
    with ctx:
        sb = lambda name, shape, dt=f32: ctx.enter_context(nc.sbuf_tensor(name, shape, dt))
        sem = lambda name: ctx.enter_context(nc.semaphore(name))
        ident = sb("ident2", [128, 128])
        coords = sb("coords", [128, NCOORD])
        base_y = coords[:, 0:ST * NK].rearrange("p (s k) -> p s k", k=NK)
        o = ST * NK
        ctr_y = coords[:, o:o + ST * WIN].rearrange("p (s a) -> p s a", a=WIN)
        o += ST * WIN
        base_x = coords[:, o:o + 2 * NK].rearrange("p (x k) -> p x k", k=NK)
        o += 2 * NK
        ctr_x = coords[:, o:o + 2 * WIN].rearrange("p (x a) -> p x a", a=WIN)
        o += 2 * WIN
        ctr_all = coords[:, o:o + NWIN * WIN].rearrange("p (w a) -> p w a", a=WIN)
        wd = [sb(f"wd{q}", [128, CH, NK, C], f32r) for q in range(2)]
        bias = sb("bias", [128, CH])
        k34 = sb("k34", [128, 1])
        om = [sb(f"om{i}", [128, 2, NOM]) for i in range(2)]
        pos = [sb(f"pos{i}", [128, 2, 2, GK]) for i in range(2)]
        lo, hi = sb("lo", [128, 2, 2, GK]), sb("hi", [128, 2, 2, GK])
        mask = [sb(f"mask{i}", [128, 2, GK]) for i in range(2)]
        coef = [sb(f"coef{i}", [128, 2, GK]) for i in range(2)]
        tap = [sb(f"tap{i}", [128, 2, GK, WIN]) for i in range(2)]
        NWT, NSUM = GH * NK * WQ, CH * NK * 256
        wt_all = sb("wt_all", [128, NWT + NSUM])
        wt = [wt_all[:, i * NWT:(i + 1) * NWT].rearrange("p (k q) -> p k q", q=WQ) for i in range(2)]
        sums = wt_all[:, NWT:].rearrange("p (h k c) -> p h k c", h=CH, k=NK)
        wtT = [sb(f"wtT{i}", [WQ, GH * NK, 128]) for i in range(2)]
        win = [sb(f"win{i}", [WQ, BLK, C]) for i in range(2)]
        val = [sb(f"val{q}", [128, CH, NK, 256], f32r) for q in range(2)]
        res = [sb(f"res{i}", [128, CH, 256]) for i in range(2)]
        rt = [sb(f"rt{i}", [128, CH, 256]) for i in range(2)]
        ot = [sb(f"ot{i}", [128, 512]) for i in range(2)]
        bank = lambda name: ctx.enter_context(nc.psum_tensor(name, [128, 512], f32))
        tb = [bank(f"tb{i}") for i in range(3)]
        vb = [bank(f"vb{i}") for i in range(3)]
        eb = [bank(f"eb{i}") for i in range(2)]
        ob = [b[:, 256:512] for b in eb]

        raw = wt_all[:, NWT:].rearrange("p (h k c) -> p h k c", h=CH, k=NK)
        consts, const_set, wd_hi, wd_lo = sem("consts2"), sem("const_set"), sem("wd_hi"), sem("wd_lo")
        wd_loaded = [sem(f"wd_loaded{h}") for h in range(CH)]
        CONSTS = 16 * 3

        def load_constants(sp):
            sp.dma_start(coords[:], coords_d).then_inc(consts, 16)
            sp.dma_start(ident[:], ident_d).then_inc(consts, 16)
            with nc.allow_non_contiguous_dma(reason="256 bias values, once"):
                sp.dma_start(bias[:], dcn_b.rearrange("(h p) -> p h", p=128)).then_inc(consts, 16)

        def load_weights(act):
            for h in range(CH):
                act.dma_start(raw[:, h], dcn_w.rearrange("u v (h p) f -> h p (u v) f", p=128)[h]
                              ).then_inc(wd_loaded[h], 16)

        def first_parts(act):
            for h in range(CH):
                act.wait_ge(wd_loaded[h], 16)
                nc.scalar.copy(wd[0][:, h], raw[:, h]).then_inc(wd_hi, 1)

        def second_parts(dve):
            for h in range(CH):
                dve.wait_ge(wd_hi, h + 1)
                nc.vector.tensor_tensor(wd[1][:, h], raw[:, h], wd[0][:, h].bitcast(f32), ALU.subtract).then_inc(wd_lo, 1)
            dve.wait_ge(wd_lo, CH)

        def wait(e, sm, v):
            if not isinstance(v, int) or v > 0:
                e.wait_ge(sm, v)

        def load_windows(sp, buf, first, step, signal):
            for a in range(WIN):
                src = bass.AP(tensor=cpad.tensor, offset=first + a * PADC * C,
                              ap=[[C, WIN], [step * C, BLK], [1, C]])
                sp.dma_start(win[buf][WIN * a:WIN * a + WIN], src).then_inc(signal, 16)

        def positions(dve, s, p, chain, start):
            def step(n, f):
                if n:
                    dve.wait_ge(chain, start + n)
                f().then_inc(chain, 1)
            omv = om[p][:, :, 0:2 * GK].rearrange("p x (t g k) -> p t x g k", t=2, k=NK)
            posv = pos[p][:].rearrange("p t x (g k) -> p t x g k", k=NK)
            g = nc.vector
            by = base_y[:, bass.ds(s, 1)].rearrange("p s k -> p (s k)").unsqueeze(1).unsqueeze(1).broadcast_to([128, 2, NG, NK])
            bx = base_x.unsqueeze(2).broadcast_to([128, 2, NG, NK])
            step(0, lambda: g.tensor_tensor(posv[:, 0], omv[:, 0], by, ALU.add))
            step(0, lambda: g.tensor_tensor(posv[:, 1], omv[:, 1], bx, ALU.add))
            step(2, lambda: g.tensor_scalar(lo[:], pos[p][:], 1.0, 1.0, ALU.add, ALU.min))
            step(2, lambda: g.tensor_scalar(hi[:], pos[p][:], -float(H), -1.0, ALU.add, ALU.max))
            step(4, lambda: g.tensor_tensor(lo[:], lo[:], hi[:], ALU.mult))
            step(4, lambda: g.tensor_scalar(pos[p][:], pos[p][:], 0.0, float(H - 1), ALU.max, ALU.min))
            step(5, lambda: g.tensor_scalar(lo[:], lo[:], -1.0, 0.0, ALU.mult, ALU.max))
            step(7, lambda: g.tensor_tensor(lo[:, 0], lo[:, 0], lo[:, 1], ALU.mult))
        NPOS = 8

        def distances(engine, p, hx, q, t, centers):
            return engine.tensor_tensor(
                tap[q][:, t], pos[p][:, t, hx].unsqueeze(2).broadcast_to([128, GK, WIN]),
                centers.unsqueeze(1).broadcast_to([128, GK, WIN]), ALU.subtract)

        def tap_weights(act, q, chain, start):
            nc.scalar.activation(tap[q][:], tap[q][:], ACT.Abs).then_inc(chain, 1)
            act.wait_ge(chain, start + 1)
            nc.scalar.activation(tap[q][:], tap[q][:], ACT.Identity, bias=k34[:], scale=-0.5).then_inc(chain, 1)

        def cap_weights(dve, p, hx, q, chain, start):
            nc.vector.scalar_tensor_tensor(out=tap[q][:], in0=tap[q][:], scalar=0.5, in1=tap[q][:],
                                           op0=ALU.mult, op1=ALU.max).then_inc(chain, 1)
            dve.wait_ge(chain, start + 1)
            nc.vector.tensor_scalar(tap[q][:], tap[q][:], 0.25, 0.0, ALU.add, ALU.max).then_inc(chain, 1)
            dve.wait_ge(chain, start + 2)
            nc.vector.scalar_tensor_tensor(out=tap[q][:, 0], in0=tap[q][:, 0], scalar=0.75,
                                           in1=coef[p][:, hx].unsqueeze(2).broadcast_to([128, GK, WIN]),
                                           op0=ALU.min, op1=ALU.mult).then_inc(chain, 1)
            nc.vector.tensor_scalar(tap[q][:, 1], tap[q][:, 1], 0.75, None, ALU.min).then_inc(chain, 1)

        def window_weights(q, half, g, w):
            gk = (half * GH + g) * NK
            shape = [128, NK, WIN, WIN]
            return nc.vector.tensor_tensor(
                wt[w][:, g * NK:(g + 1) * NK].rearrange("p k (a b) -> p k a b", a=WIN),
                tap[q][:, 0, gk:gk + NK].unsqueeze(3).broadcast_to(shape),
                tap[q][:, 1, gk:gk + NK].unsqueeze(2).broadcast_to(shape), ALU.mult)

        def transpose_batch(w, i, b):
            for j in range(4):
                last = nc.tensor.transpose(tb[b][0:WQ, 128 * j:128 * j + 128], wt[w][:, 4 * i + j, :], ident[:])
            return last

        def copy_batch(e, w, i, b):
            dst, src = wtT[w][:, 4 * i:4 * i + 4, :], tb[b][0:WQ, :].rearrange("p (i c) -> p i c", i=4)
            return nc.scalar.copy(dst, src) if e == "act" else nc.vector.tensor_copy(dst, src)

        def sample_block(w, q, half, j, v):
            for g in range(GH):
                ch = (half * GH + g) * 32
                last = nc.tensor.matmul(vb[v][32 * g:32 * g + 32, 144 * (j % 3):144 * (j % 3) + 144],
                                        win[q][:, j, ch:ch + 32],
                                        wtT[w][:, g * NK:(g + 1) * NK, 16 * j:16 * j + 16],
                                        start=True, stop=True)
            return last

        def samples(of, hx, half, j0, v):
            n = min(3, BLK - j0)
            src = vb[v][:, 0:144 * n].rearrange("p (j k c) -> p k j c", j=n, k=NK)
            at = 128 * hx + 16 * j0
            dst = of[:, half, :, at:at + 16 * n].rearrange("p k (j c) -> p k j c", j=n)
            return dst, src

        def project(half, k):
            for fo in range(CH):
                for wp, vp in ((0, 0), (0, 1), (1, 0)):
                    last = nc.tensor.matmul(eb[fo][:, 0:256], wd[wp][:, half, k, 128 * fo:128 * fo + 128],
                                            val[vp][:, half, k, :], start=(half == 0 and k == 0 and wp + vp == 0),
                                            stop=(half == CH - 1 and k == NK - 1 and wp == 1))
            return last

        def finish(p, fo):
            return nc.scalar.activation(
                res[p][:, fo, :].rearrange("p (r j c) -> p j r c", r=4, c=4),
                eb[fo][:, 0:256].rearrange("p (j r c) -> p j r c", r=4, c=4), ACT.Relu, bias=bias[:, fo:fo + 1])

        def turn_result(p):
            for c2 in range(2):
                for fo in range(CH):
                    last = nc.tensor.transpose(ob[c2][:, 128 * fo:128 * fo + 128],
                                               res[p][:, fo, 128 * c2:128 * c2 + 128], ident[:])
            return last

        def copy_result(p):
            for c2 in range(2):
                last = nc.scalar.copy(ot[p][:, 256 * c2:256 * c2 + 256], ob[c2])
            return last

        def out_rows(s):
            return out.rearrange("b h w c -> (b h w) c").rearrange("(s t p) c -> s p t c", t=2, p=128
                                                                    )[bass.ds(s, 1)].rearrange("o p t c -> (o p) t c")

        def fast():
            names = ("om_ready0 om_ready1 r_ready0 r_ready1 out_stored0 out_stored1 win_ready0 win_ready1 masked "
                     "pchain coef_ready dist_ready achain capped products batched "
                     "tb_out0 tb_out1 tb_out2 sampled val_hi vb_out0 vb_out1 vb_out2 projected finished summed turned ob_out").split()
            sems = {n: sem("f_" + n) for n in names}

            def w(e, name, v):
                wait(e, sems[name], v)

            def loop(e, strips):
                strips(0)
                strips(1)
                with e.Fori(2, ST // 2 - 1) as it:
                    strips(it)
                strips(ST // 2 - 1)

            AFTER_THIRDS = (3, 6, 8)

            def known(v, least, end):
                return not isinstance(v, int) or least <= v < end

            def copy_samples(e, me, s, u, v):
                n1 = 4 * s + u - 1
                if not known(n1, 0, UNITS * ST):
                    return
                strip, unit = (s, u - 1) if u else (s - 1, 3)
                half = unit % 2
                dst, src = samples(val[0], unit // 2, half, 3 * v, v)
                if me == "act":
                    w(e, "sampled", 3 * n1 + v + 1)
                    w(e, "projected", 2 * (strip - 1) + half + 1)
                    nc.scalar.copy(dst, src).then_inc(sems["val_hi"], 1)
                else:
                    w(e, "val_hi", 3 * n1 + v + 1)
                    rest, _ = samples(val[1], unit // 2, half, 3 * v, v)
                    nc.vector.tensor_tensor(rest, src, dst.bitcast(f32), ALU.subtract).then_inc(sems[f"vb_out{v}"], 1)

            def sp_fast(sp):
                def strips(it):
                    at = ((it // 8) * (PADC - HC) + 4 * it) * PADC * C
                    if not isinstance(it, int):
                        at = sp.snap(at)
                    for p in range(2):
                        s = 2 * it + p
                        for hx in range(2):
                            w(sp, "sampled", 6 * (2 * s + hx - 1))
                            load_windows(sp, hx, at + 2 * p * PADC * C + 16 * hx * C, 2, sems[f"win_ready{hx}"])
                        w(sp, "summed", s - 1)
                        sp.dma_start(rt[p][:], r_d[bass.ds(it, 1), :, :, 256 * p:256 * p + 256].rearrange(
                            "o p h c -> (o p) h c")).then_inc(sems[f"r_ready{p}"], 16)
                loop(sp, strips)
                for p in range(2):
                    sp.wait_ge(sems[f"out_stored{p}"], 16 * ST // 2)

            def pool_fast(pool):
                def load_om(s, p):
                    pool.dma_start(om[p][:], om_d[bass.ds(s, 1)].rearrange("o p x c -> (o p) x c")
                                   ).then_inc(sems[f"om_ready{p}"], 16)

                def strips(it):
                    for p in range(2):
                        s = 2 * it + p
                        if known(s, 0, ST - 1):
                            w(pool, "masked", s)
                            w(pool, "coef_ready", s)
                            load_om(s + 1, 1 - p)
                        w(pool, "coef_ready", s + 1)
                        for hx in range(2):
                            w(pool, "products", 8 * (2 * s + hx - 1))
                            cy = ctr_y[:, bass.ds(s, 1)].rearrange("p s a -> p (s a)")
                            distances(nc.gpsimd, p, hx, hx, 1, ctr_x[:, hx]).then_inc(sems["dist_ready"], 1)
                            distances(nc.gpsimd, p, hx, hx, 0, cy).then_inc(sems["dist_ready"], 1)
                load_om(0, 0)
                pool.wait_ge(consts, CONSTS)
                loop(pool, strips)

            def act_fast(act):
                def taps(qg, q):
                    if known(qg, 0, 2 * ST):
                        w(act, "dist_ready", 2 * (qg + 1))
                        tap_weights(act, q, sems["achain"], 2 * qg)

                def sigmoid(s, p, n16):
                    if known(s, 0, ST):
                        w(act, f"om_ready{p}", n16)
                        w(act, "coef_ready", s - 1)
                        nc.scalar.activation(mask[p][:], om[p][:, :, 2 * GK:NOM], ACT.Sigmoid
                                             ).then_inc(sems["masked"], 1)

                def slot(s, p, u, half_s):
                    n = 4 * s + u
                    if u == 0:
                        sigmoid(s + 1, 1 - p, 16 * (half_s + 1 + p))
                    for i in range(NT):
                        if known(s, 0, ST):
                            w(act, "batched", 9 * n + i + 1)
                            w(act, "sampled", 3 * (n - 1))
                            copy_batch("act", u % 2, i, i % 3).then_inc(sems[f"tb_out{i % 3}"], 1)
                        if i in AFTER_THIRDS:
                            copy_samples(act, "act", s, u, AFTER_THIRDS.index(i))
                        if (u, i) == (2, 1) and known(s - 1, 0, ST):
                            w(act, "projected", 2 * s)
                            w(act, "turned", s - 2)
                            for fo in range(CH):
                                finish(1 - p, fo).then_inc(sems["finished"], 1)
                        if (u, i) in ((0, 3), (1, 6)):
                            taps(2 * s + 1 + u, 1 - u)
                        if (u, i) == (3, 2) and known(s - 2, 0, ST):
                            w(act, "turned", s - 1)
                            w(act, f"out_stored{p}", 16 * (half_s - 1))
                            copy_result(p).then_inc(sems["ob_out"], 1)
                            w(act, "ob_out", s - 1)
                            act.dma_start(out_rows(s - 2), ot[p][:].rearrange("p (t c) -> p t c", t=2)
                                          ).then_inc(sems[f"out_stored{p}"], 16)

                def strips(it):
                    for p in range(2):
                        for u in range(UNITS):
                            slot(2 * it + p, p, u, it)
                sigmoid(0, 0, 16)
                taps(0, 0)
                first_parts(act)
                loop(act, strips)
                strips(ST // 2)

            def dve_fast(dve):
                def cap(s, p, hx):
                    if known(s, 0, ST):
                        w(dve, "achain", 2 * (2 * s + hx + 1))
                        w(dve, "coef_ready", s + 1)
                        cap_weights(dve, p, hx, hx, sems["capped"], 4 * (2 * s + hx))
                        w(dve, "capped", 4 * (2 * s + hx + 1))

                def product(s, p, u, g):
                    if known(s, 0, ST):
                        n = 4 * s + u
                        w(dve, "batched", 9 * (n - 1))
                        window_weights(u // 2, u % 2, g, u % 2).then_inc(sems["products"], 1)

                def place(s, p, n16):
                    if known(s, 0, ST):
                        w(dve, f"om_ready{p}", n16)
                        w(dve, "dist_ready", 4 * (s - 1))
                        positions(dve, s, p, sems["pchain"], NPOS * s)
                        w(dve, "pchain", NPOS * (s + 1))
                        w(dve, "masked", s + 1)
                        nc.vector.tensor_tensor(coef[p][:], lo[:, 0], mask[p][:], ALU.mult).then_inc(sems["coef_ready"], 1)

                def slot(s, p, u, half_s):
                    n = 4 * s + u
                    after = (s, p, u + 1) if u < 3 else (s + 1, 1 - p, 0)
                    for i in range(NT):
                        if i in (0, 2, 4, 6):
                            product(*after, i // 2)
                        if i in AFTER_THIRDS:
                            copy_samples(dve, "dve", s, u, AFTER_THIRDS.index(i))
                        if i == 1 and u == 0:
                            place(s + 1, 1 - p, 16 * (half_s + 1 + p))
                        if i == 8 and u == 0:
                            cap(s, p, 1)
                        if i == 8 and u == 1:
                            cap(s + 1, 1 - p, 0)
                        if i == 4 and u == 1 and known(s - 2, 0, ST):
                            w(dve, "finished", 2 * (s - 1))
                            w(dve, f"r_ready{p}", 8 * (s - p))
                            nc.vector.tensor_tensor(res[p][:], res[p][:], rt[p][:], ALU.add).then_inc(sems["summed"], 1)

                def strips(it):
                    for p in range(2):
                        for u in range(UNITS):
                            slot(2 * it + p, p, u, it)
                place(0, 0, 16)
                cap(0, 0, 0)
                for g in range(GH):
                    product(0, 0, 0, g)
                second_parts(dve)
                loop(dve, strips)
                strips(ST // 2)

            def pe_fast(pe):
                LATE = 3

                def slot(s, p, u, half_s):
                    n = 4 * s + u
                    unit = (s, p, u - 1) if u else (s - 1, 1 - p, 3)
                    for i in range(NT):
                        if known(s, 0, ST):
                            w(pe, "products", 4 * n + (4 * i + 3) // NK + 1)
                            w(pe, f"tb_out{i % 3}", 3 * n + i // 3)
                            transpose_batch(u % 2, i, i % 3).then_inc(sems["batched"], 1)
                        if u < CH and i >= LATE and known(s - 1, 0, ST):
                            if i == LATE:
                                pe.wait_ge(wd_lo, CH)
                                for v in range(3):
                                    w(pe, f"vb_out{v}", 4 * (s - 1) + 3 + u)
                                w(pe, "finished", 2 * (s - 1))
                                w(pe, "ob_out", s - 2)
                            for k in range(NK * (i - LATE) // (NT - LATE), NK * (i - LATE + 1) // (NT - LATE)):
                                last = project(u, k)
                            if i == NT - 1:
                                last.then_inc(sems["projected"], 1)
                        if i >= 1 and known(4 * s + u - 1, 0, UNITS * ST):
                            v = (i - 1) // 3
                            if i % 3 == 1:
                                w(pe, f"vb_out{v}", n - 1)
                            if i == 1:
                                for b in range(3):
                                    w(pe, f"tb_out{b}", 3 * n)
                                w(pe, f"win_ready{unit[2] // 2}", 16 * WIN * (unit[0] + 1))
                            last = sample_block(unit[2] % 2, unit[2] // 2, unit[2] % 2, i - 1, v)
                            if i in AFTER_THIRDS:
                                last.then_inc(sems["sampled"], 1)
                        if i == 6 and u == 2 and known(s - 2, 0, ST):
                            w(pe, "summed", s - 1)
                            w(pe, "finished", 2 * (min(s, ST) if isinstance(s, int) else s))
                            w(pe, "ob_out", s - 2)
                            turn_result(p).then_inc(sems["turned"], 1)

                def strips(it):
                    for p in range(2):
                        for u in range(UNITS):
                            slot(2 * it + p, p, u, it)
                loop(pe, strips)
                strips(ST // 2)

            return sp_fast, pool_fast, act_fast, dve_fast, pe_fast

        def general():
            names = ("om_ready r_ready out_stored win_ready masked pchain coef_ready dist_ready achain capped products "
                     "batched copied sampled zeroed added val_hi split projected finished summed turned ob_out").split()
            sems = {n: sem("g_" + n) for n in names}
            WINDOWS = NWIN * NWIN

            def w(e, name, v):
                wait(e, sems[name], v)

            def sp_general(sp):
                pass

            def pool_general(pool):
                pass

            def act_general(act):
                first_parts(act)
                with act.Fori(0, ST) as s:
                    act.dma_start(om[0][:], om_d[bass.ds(s, 1)].rearrange("o p x c -> (o p) x c")
                                  ).then_inc(sems["om_ready"], 16)
                    r_at = (s // 2) * (128 * CH * 512) + (s % 2) * 256
                    act.dma_start(rt[0][:], bass.AP(tensor=r_d.tensor, offset=r_at, ap=[[CH * 512, 128], [512, CH], [1, 256]])
                                  ).then_inc(sems["r_ready"], 16)
                    w(act, "om_ready", 16 * (s + 1))
                    nc.scalar.activation(mask[0][:], om[0][:, :, 2 * GK:NOM], ACT.Sigmoid).then_inc(sems["masked"], 1)
                    with act.Fori(0, NWIN) as wy:
                        with act.Fori(0, NWIN) as wx:
                            at = act.snap((((s // 16) * PADC + PADLO - 1 + WIN * wy) * PADC + PADLO - 1 + WIN * wx) * C)
                            for hx in range(2):
                                t = ((s * NWIN + wy) * NWIN + wx) * 2 + hx
                                load_windows(act, 0, at, 0, sems["win_ready"])
                                w(act, "dist_ready", 2 * (t + 1))
                                tap_weights(act, 0, sems["achain"], 2 * t)
                                w(act, "sampled", 6 * (t + 1))
                    for fo in range(CH):
                        w(act, "projected", s + 1)
                        finish(0, fo).then_inc(sems["finished"], 1)
                    w(act, "turned", s + 1)
                    copy_result(0).then_inc(sems["ob_out"], 1)
                    w(act, "ob_out", s + 1)
                    act.dma_start(out_rows(s), ot[0][:].rearrange("p (t c) -> p t c", t=2)
                                  ).then_inc(sems["out_stored"], 16)
                    w(act, "out_stored", 16 * (s + 1))
                    w(act, "coef_ready", s + 1)

            def dve_general(dve):
                second_parts(dve)
                with dve.Fori(0, ST) as s:
                    w(dve, "om_ready", 16 * (s + 1))
                    positions(dve, s, 0, sems["pchain"], NPOS * s)
                    w(dve, "pchain", NPOS * (s + 1))
                    w(dve, "masked", s + 1)
                    nc.vector.tensor_tensor(coef[0][:], lo[:, 0], mask[0][:], ALU.mult).then_inc(sems["coef_ready"], 1)
                    w(dve, "coef_ready", s + 1)
                    nc.vector.memset(sums, 0.0).then_inc(sems["zeroed"], 1)
                    with dve.Fori(0, NWIN) as wy:
                        with dve.Fori(0, NWIN) as wx:
                            for hx in range(2):
                                t = ((s * NWIN + wy) * NWIN + wx) * 2 + hx
                                for d, win_no in enumerate((wy, wx)):
                                    centers = ctr_all[:, bass.ds(win_no, 1)].rearrange("p w a -> p (w a)")
                                    distances(nc.vector, 0, hx, 0, d, centers).then_inc(sems["dist_ready"], 1)
                                w(dve, "achain", 2 * (t + 1))
                                cap_weights(dve, 0, hx, 0, sems["capped"], 4 * t)
                                w(dve, "capped", 4 * (t + 1))
                                for half in range(2):
                                    n = 2 * t + half
                                    for g in range(GH):
                                        window_weights(0, half, g, 0).then_inc(sems["products"], 1)
                                    for i in range(NT):
                                        w(dve, "batched", 9 * n + i + 1)
                                        copy_batch("dve", 0, i, i % 3).then_inc(sems["copied"], 1)
                                    for v in range(3):
                                        w(dve, "sampled", 3 * n + v + 1)
                                        w(dve, "zeroed", s + 1)
                                        dst, src = samples(sums, hx, half, 3 * v, v)
                                        nc.vector.tensor_tensor(dst, src, dst, ALU.add).then_inc(sems["added"], 1)
                                    w(dve, "products", 4 * (n + 1))
                                    w(dve, "added", 3 * (n + 1))
                    nc.vector.tensor_copy(val[0][:], sums).then_inc(sems["val_hi"], 1)
                    w(dve, "val_hi", s + 1)
                    nc.vector.tensor_tensor(val[1][:], sums, val[0][:].bitcast(f32), ALU.subtract
                                            ).then_inc(sems["split"], 1)
                    w(dve, "split", s + 1)
                    w(dve, "finished", 2 * (s + 1))
                    w(dve, "r_ready", 16 * (s + 1))
                    nc.vector.tensor_tensor(res[0][:], res[0][:], rt[0][:], ALU.add).then_inc(sems["summed"], 1)

            def pe_general(pe):
                pe.wait_ge(wd_lo, CH)
                with pe.Fori(0, ST) as s:
                    with pe.Fori(0, WINDOWS) as i:
                        for hx in range(2):
                            t = s * (2 * WINDOWS) + 2 * i + hx
                            for half in range(2):
                                n = 2 * t + half
                                for i4 in range(NT):
                                    w(pe, "products", 4 * n + (4 * i4 + 3) // NK + 1)
                                    if i4 >= 3:
                                        w(pe, "copied", 9 * n + i4 - 2)
                                    transpose_batch(0, i4, i4 % 3).then_inc(sems["batched"], 1)
                                w(pe, "copied", 9 * (n + 1))
                                w(pe, "win_ready", 16 * WIN * (t + 1))
                                for v in range(3):
                                    for j in range(3 * v, min(3 * v + 3, BLK)):
                                        last = sample_block(0, 0, half, j, v)
                                    last.then_inc(sems["sampled"], 1)
                                w(pe, "added", 3 * (n + 1))
                    w(pe, "split", s + 1)
                    for half in range(CH):
                        for k in range(NK):
                            last = project(half, k)
                    last.then_inc(sems["projected"], 1)
                    w(pe, "summed", s + 1)
                    turn_result(0).then_inc(sems["turned"], 1)
                    w(pe, "ob_out", s + 1)

            return sp_general, pool_general, act_general, dve_general, pe_general

        fast_sp, fast_pool, fast_act, fast_dve, fast_pe = fast()
        gen_sp, gen_pool, gen_act, gen_dve, gen_pe = general()

        def choose(e, fast_path, general_path):
            beyond = e.value_load(flag[0:1, 0:1], min_val=0, max_val=1)
            with e.If(beyond == 0):
                fast_path(e)
            with e.Else():
                general_path(e)

        with nc.Block() as block:
            @block.sync
            def _(sp):
                load_constants(sp)
                choose(sp, fast_sp, gen_sp)

            @block.gpsimd
            def _(pool):
                choose(pool, fast_pool, gen_pool)

            @block.scalar
            def _(act):
                act.wait_ge(consts, CONSTS)
                load_weights(act)
                act.wait_ge(const_set, 1)
                choose(act, fast_act, gen_act)

            @block.vector
            def _(dve):
                nc.vector.memset(k34[:], 0.75).then_inc(const_set, 1)
                dve.wait_ge(consts, CONSTS)
                choose(dve, fast_dve, gen_dve)

            @block.tensor
            def _(pe):
                pe.wait_ge(consts, CONSTS)
                choose(pe, fast_pe, gen_pe)


def conv_preact(nc, x, coarse, attend_w, select_w, offset_w, om_w, om_b, dcn_w, dcn_b, ident, gmean, coords, out):
    cpad = nc.dram_tensor("cpad", [B, PADC, PADC, C], f32, kind="Internal").ap()
    om_d = nc.dram_tensor("om_d", [ST, 128, 2, NOM], f32, kind="Internal").ap()
    r_d = nc.dram_tensor("r_d", [B * SB, 128, CH, 512], f32, kind="Internal").ap()
    with nc.sbuf_tensor("flag", [1, 1], i32) as flag:
        with ExitStack() as ctx:
            wf, wc = ([ctx.enter_context(nc.sbuf_tensor(f"{name}{q}", [128, CH, rows, 3, NOM], f32r)) for q in range(2)]
                      for name, rows in (("wf", 4), ("wc", 3)))
            scale, shift = (ctx.enter_context(nc.sbuf_tensor(n, [128, CH, B], f32)) for n in ("scale", "shift"))
            statistics_and_weights(nc, x, attend_w, om_w, offset_w, ident, gmean, wf, wc, scale, shift)
            offsets_and_calibration(nc, x, coarse, select_w, om_b, ident, cpad, wf, wc, scale, shift, om_d, r_d, flag)
        sample_and_project(nc, cpad, om_d, r_d, dcn_w, dcn_b, ident, coords, flag, out)


_INS = ["x", "L0_conv_coarse", "L0_conv_attend_w", "L0_conv_select_w", "L0_conv_offset_w", "L0_conv_om_w",
        "L0_conv_om_b", "L0_conv_dcn_w", "L0_conv_dcn_b"]


def _constants():
    import numpy as np
    p = np.arange(128)
    j, r, c = p // 16, p // 4 % 4, p % 4
    block_row = np.arange(ST) % (H // 4)
    k, a, hx = np.arange(NK), np.arange(WIN), np.arange(2)
    base_y = 4 * block_row[None, :, None] + r[:, None, None] + k // 3 - 1
    base_x = 32 * hx[None, :, None] + (4 * j + c)[:, None, None] + k % 3 - 1
    centre = lambda n: 2 * n + 0.5
    ctr_y = np.broadcast_to(centre(2 * block_row[:, None] - PADLO + a), (128, ST, WIN))
    ctr_x = centre(2 * (BLK * hx[None, :, None] + j[:, None, None]) - PADLO + a)
    ctr_all = np.broadcast_to(centre(-1 + WIN * np.arange(NWIN)[:, None] + a), (128, NWIN, WIN))
    coords = np.concatenate([t.reshape(128, -1) for t in (base_y, ctr_y, base_x, ctr_x, ctr_all)], 1)
    return {"ident": np.eye(128, dtype=np.float32),
            "gmean": np.kron(np.eye(16), np.full((8, 8), 0.125)).astype(np.float32),
            "coords": coords.astype(np.float32)}


def kernel(**inputs):
    import numpy as np
    import concourse.bacc as bacc
    from concourse.bass_utils import run_bass_kernel_spmd

    nc = bacc.Bacc("TRN2", target_bir_lowering=False, num_devices=1)
    arrays, args = {}, []
    given = {name: np.ascontiguousarray(inputs[name]) for name in _INS} | _constants()
    for name, a in given.items():
        arrays[f"in_{name}"] = a
        args.append(nc.dram_tensor(f"in_{name}", a.shape, mybir.dt.from_np(a.dtype), kind="ExternalInput").ap())
    out = nc.dram_tensor("out_0", (B, H, W, C), f32, kind="ExternalOutput").ap()
    conv_preact(nc, *args, out)
    got = run_bass_kernel_spmd(nc, [arrays], core_ids=[0])
    return got.results[0]["out_0"]
```
